# Optimizing a Trainium2 kernel written in Bass

```python
import numpy as np
import jax
import jax.numpy as jnp

def _softmax(x, axis=-1):
    return jax.nn.softmax(x, axis=axis)

def _gelu(x):
    return jax.nn.gelu(x, approximate=True)

def _silu(x):
    return jax.nn.silu(x)

def _sigmoid(x):
    return jax.nn.sigmoid(x)

def _layernorm(x, axis=-1, eps=1e-05):
    m = jnp.mean(x, axis=axis, keepdims=True)
    v = jnp.var(x, axis=axis, keepdims=True)
    return (x - m) / jnp.sqrt(v + eps)

def _scatter_add(tgt, idx, src, axis=0):
    return tgt.at[idx].add(src)

def _segment_sum(src, seg, n):
    return jax.ops.segment_sum(src, seg, n)
kernel_name = 'mk_decoder_preln_d2_seqx_r8_49e7e7'

def setup_inputs(seed: int=0):
    np.random.seed(seed)
    _w = jnp.asarray

    def _rec_inputs():
        import jax
        import jax.numpy as jnp
        _rk = jax.random.key(seed)
        x = 7.22e-05 + 1 * jax.random.normal(jax.random.fold_in(_rk, 1), (16, 128, 128), jnp.float32)
        _lenS = 128 - jax.random.randint(jax.random.fold_in(_rk, 7), (16,), 0, max(1, 128 // 4) + 1, jnp.int32)
        _lenS2 = 120 - jax.random.randint(jax.random.fold_in(_rk, 8), (16,), 0, max(1, 120 // 4) + 1, jnp.int32)
        _ctx_1024P = jax.random.normal(jax.random.fold_in(_rk, 11), (16, 16, 128), jnp.float32)
        _ctx_1024c = jax.random.dirichlet(jax.random.fold_in(_rk, 511), 0.3 * jnp.ones((16,), jnp.float32), (16, 120))
        _ctx_1024t = jnp.einsum('bsk,bkd->bsd', _ctx_1024c, _ctx_1024P)
        _ctx_1024t = _ctx_1024t * jax.lax.rsqrt(jnp.mean(jnp.square(_ctx_1024t)) + 1e-12) * 0.953939
        ctx_1024 = 4.13588e-05 + 0.999923 * (_ctx_1024t + 0.3 * jax.random.normal(jax.random.fold_in(_rk, 611), (16, 120, 128), jnp.float32))
        _validS = jnp.arange(128)[None, :] < _lenS[:, None]
        _validS2 = jnp.arange(120)[None, :] < _lenS2[:, None]
        _causal = jnp.tril(jnp.ones((128, 128), dtype=bool))
        mask_Bx1xSxS2_bk1 = jnp.broadcast_to(_validS2[:, None, None, :], (16, 1, 128, 120))
        return (x, ctx_1024, mask_Bx1xSxS2_bk1)
    x, ctx_1024, mask_Bx1xSxS2_bk1 = _rec_inputs()

    def _L0_attn_setup():
        import jax, jax.numpy as jnp
        import numpy as np
        N_HEADS = 16
        HIDDEN = 128
        HEAD_DIM = 64
        BSZ = 4
        SEQ = 128
        SCALE = HEAD_DIM ** (-0.5)
        key = jax.random.key(seed)
        k_x, k_q, k_k, k_v, k_o = jax.random.split(key, 5)
        s = HIDDEN ** (-0.5)
        return {'x': jax.random.normal(k_x, (BSZ, SEQ, HIDDEN), dtype=jnp.float32), 'wq': jax.random.normal(k_q, (N_HEADS * HEAD_DIM, HIDDEN), dtype=jnp.float32) * s, 'wk': jax.random.normal(k_k, (N_HEADS * HEAD_DIM, HIDDEN), dtype=jnp.float32) * s, 'wv': jax.random.normal(k_v, (N_HEADS * HEAD_DIM, HIDDEN), dtype=jnp.float32) * s, 'wo': jax.random.normal(k_o, (HIDDEN, N_HEADS * HEAD_DIM), dtype=jnp.float32) * s}
    _L0_attn_all = _L0_attn_setup()
    _L0_attn_in = {k: v for k, v in _L0_attn_all.items() if k in ('wq', 'wk', 'wv', 'wo')}
    del _L0_attn_all

    def _L0_xattn_setup():
        import jax, jax.numpy as jnp
        import numpy as np
        B, S, D, H = (4, 256, 128, 16)
        HD = D // H
        key = jax.random.key(seed)
        ks = jax.random.split(key, 12)
        scale = 1.0 / np.sqrt(D)
        inp = {'queries': jax.random.normal(ks[0], (B, S, D), jnp.float32), 'keys': jax.random.normal(ks[1], (B, S, D), jnp.float32), 'values': jax.random.normal(ks[2], (B, S, D), jnp.float32), 'mask': jax.random.randint(ks[3], (B, 1, S, S), 0, 2).astype(bool), 'Wq': jax.random.normal(ks[4], (D, D), jnp.float32) * scale, 'bq': jnp.zeros((D,), jnp.float32), 'Wk': jax.random.normal(ks[5], (D, D), jnp.float32) * scale, 'bk': jnp.zeros((D,), jnp.float32), 'Wv': jax.random.normal(ks[6], (D, D), jnp.float32) * scale, 'bv': jnp.zeros((D,), jnp.float32), 'Wo': jax.random.normal(ks[7], (D, D), jnp.float32) * scale, 'bo': jnp.zeros((D,), jnp.float32)}
        return inp
    _L0_xattn_all = _L0_xattn_setup()
    _L0_xattn_in = {k: v for k, v in _L0_xattn_all.items() if k in ('Wq', 'bq', 'Wk', 'bk', 'Wv', 'bv', 'Wo', 'bo')}
    del _L0_xattn_all

    def _L0_ffn_setup():
        import jax, jax.numpy as jnp
        import numpy as np
        from math import ceil
        CAPACITY_FACTOR = 2.0
        MIN_CAPACITY = 4
        key = jax.random.key(seed)
        ks = jax.random.split(key, 4)
        B, S, D, Di, E = (4, 256, 128, 512, 8)
        x = jax.random.normal(ks[0], (B, S, D), dtype=jnp.float32)
        Wr = jax.random.normal(ks[1], (D, E), dtype=jnp.float32) * D ** (-0.5)
        W1 = jax.random.normal(ks[2], (E, D, Di), dtype=jnp.float32) * D ** (-0.5)
        b1 = jnp.zeros((E, Di), dtype=jnp.float32)
        W2 = jax.random.normal(ks[3], (E, Di, D), dtype=jnp.float32) * Di ** (-0.5)
        b2 = jnp.zeros((E, D), dtype=jnp.float32)
        return {'x': x, 'Wr': Wr, 'W1': W1, 'b1': b1, 'W2': W2, 'b2': b2}
    _L0_ffn_all = _L0_ffn_setup()
    _L0_ffn_in = {k: v for k, v in _L0_ffn_all.items() if k in ('Wr', 'W1', 'b1', 'W2', 'b2')}
    del _L0_ffn_all

    def _L1_attn_setup():
        import jax, jax.numpy as jnp
        import numpy as np
        B, P, D = (8, 128, 128)
        H, N = (16, 64)
        key = jax.random.key(seed)
        k1, k2, k3 = jax.random.split(key, 3)
        inputs = jax.random.normal(k1, (B, P, D), dtype=jnp.float32)
        w_qkv = jax.random.normal(k2, (H, 3, D, N), dtype=jnp.float32) * 0.05
        w_o = jax.random.normal(k3, (N * H, D), dtype=jnp.float32) * 0.05
        return {'inputs': inputs, 'w_qkv': w_qkv, 'w_o': w_o}
    _L1_attn_all = _L1_attn_setup()
    _L1_attn_in = {k: v for k, v in _L1_attn_all.items() if k in ('w_qkv', 'w_o')}
    del _L1_attn_all

    def _L1_xattn_setup():
        import jax, jax.numpy as jnp
        import numpy as np
        D_MODEL = 128
        B, S = (4, 256)
        key = jax.random.key(seed)
        ks = jax.random.split(key, 10)
        s = 1.0 / np.sqrt(D_MODEL)
        return {'k': jax.random.normal(ks[0], (B, S, D_MODEL), jnp.float32), 'v': jax.random.normal(ks[1], (B, S, D_MODEL), jnp.float32), 'q': jax.random.normal(ks[2], (B, S, D_MODEL), jnp.float32), 'Wk': jax.random.normal(ks[3], (D_MODEL, D_MODEL), jnp.float32) * s, 'Wv': jax.random.normal(ks[4], (D_MODEL, D_MODEL), jnp.float32) * s, 'bv': jnp.zeros((D_MODEL,), jnp.float32), 'Wq': jax.random.normal(ks[5], (D_MODEL, D_MODEL), jnp.float32) * s, 'bq': jnp.zeros((D_MODEL,), jnp.float32), 'Wo': jax.random.normal(ks[6], (D_MODEL, D_MODEL), jnp.float32) * s, 'bo': jnp.zeros((D_MODEL,), jnp.float32)}
    _L1_xattn_all = _L1_xattn_setup()
    _L1_xattn_in = {k: v for k, v in _L1_xattn_all.items() if k in ('Wk', 'Wv', 'bv', 'Wq', 'bq', 'Wo', 'bo')}
    del _L1_xattn_all

    def _L1_ffn_setup():
        import jax, jax.numpy as jnp
        import numpy as np
        B, S, H = (2, 128, 128)
        E, F = (16, 64)
        G, TOPK_G, TOPK = (4, 2, 4)
        N_SHARED = 2
        ROUTE_SCALE = 1.0
        FS = N_SHARED * F

        def _gate(x, w_gate):
            T = x.shape[0]
            scores = jax.nn.sigmoid(x @ w_gate.T)
            sv = scores.reshape(T, G, E // G)
            group_scores = jax.lax.top_k(sv, 2)[0].sum(-1)
            top_groups = jax.lax.top_k(group_scores, TOPK_G)[1]
            allowed = jnp.zeros((T, G), dtype=bool).at[jnp.arange(T)[:, None], top_groups].set(True)
            masked = jnp.where(allowed[:, :, None], sv, -jnp.inf).reshape(T, E)
            _, idx = jax.lax.top_k(masked, TOPK)
            w = jnp.take_along_axis(scores, idx, axis=1)
            w = w / (w.sum(-1, keepdims=True) + 1e-06) * ROUTE_SCALE
            return (w, idx)

        def _swiglu(x, w1, w3, w2):
            return jax.nn.silu(x @ w1.T) * (x @ w3.T) @ w2.T
        key = jax.random.key(seed)
        ks = jax.random.split(key, 8)
        scale = 0.02
        return {'hidden_states': jax.random.normal(ks[0], (B, S, H), dtype=jnp.float32), 'w_gate': jax.random.normal(ks[1], (E, H), dtype=jnp.float32) * scale, 'w1_e': jax.random.normal(ks[2], (E, F, H), dtype=jnp.float32) * scale, 'w3_e': jax.random.normal(ks[3], (E, F, H), dtype=jnp.float32) * scale, 'w2_e': jax.random.normal(ks[4], (E, H, F), dtype=jnp.float32) * scale, 'w1_s': jax.random.normal(ks[5], (FS, H), dtype=jnp.float32) * scale, 'w3_s': jax.random.normal(ks[6], (FS, H), dtype=jnp.float32) * scale, 'w2_s': jax.random.normal(ks[7], (H, FS), dtype=jnp.float32) * scale}
    _L1_ffn_all = _L1_ffn_setup()
    _L1_ffn_in = {k: v for k, v in _L1_ffn_all.items() if k in ('w_gate', 'w1_e', 'w3_e', 'w2_e', 'w1_s', 'w3_s', 'w2_s')}
    del _L1_ffn_all
    return {'x': x, 'ctx_1024': ctx_1024, 'mask_Bx1xSxS2_bk1': mask_Bx1xSxS2_bk1, 'L0_attn_wq': _L0_attn_in['wq'], 'L0_attn_wk': _L0_attn_in['wk'], 'L0_attn_wv': _L0_attn_in['wv'], 'L0_attn_wo': _L0_attn_in['wo'], 'L0_xattn_Wq': _L0_xattn_in['Wq'], 'L0_xattn_bq': _L0_xattn_in['bq'], 'L0_xattn_Wk': _L0_xattn_in['Wk'], 'L0_xattn_bk': _L0_xattn_in['bk'], 'L0_xattn_Wv': _L0_xattn_in['Wv'], 'L0_xattn_bv': _L0_xattn_in['bv'], 'L0_xattn_Wo': _L0_xattn_in['Wo'], 'L0_xattn_bo': _L0_xattn_in['bo'], 'L0_ffn_Wr': _L0_ffn_in['Wr'], 'L0_ffn_W1': _L0_ffn_in['W1'], 'L0_ffn_b1': _L0_ffn_in['b1'], 'L0_ffn_W2': _L0_ffn_in['W2'], 'L0_ffn_b2': _L0_ffn_in['b2'], 'L1_attn_w_qkv': _L1_attn_in['w_qkv'], 'L1_attn_w_o': _L1_attn_in['w_o'], 'L1_xattn_Wk': _L1_xattn_in['Wk'], 'L1_xattn_Wv': _L1_xattn_in['Wv'], 'L1_xattn_bv': _L1_xattn_in['bv'], 'L1_xattn_Wq': _L1_xattn_in['Wq'], 'L1_xattn_bq': _L1_xattn_in['bq'], 'L1_xattn_Wo': _L1_xattn_in['Wo'], 'L1_xattn_bo': _L1_xattn_in['bo'], 'L1_ffn_w_gate': _L1_ffn_in['w_gate'], 'L1_ffn_w1_e': _L1_ffn_in['w1_e'], 'L1_ffn_w3_e': _L1_ffn_in['w3_e'], 'L1_ffn_w2_e': _L1_ffn_in['w2_e'], 'L1_ffn_w1_s': _L1_ffn_in['w1_s'], 'L1_ffn_w3_s': _L1_ffn_in['w3_s'], 'L1_ffn_w2_s': _L1_ffn_in['w2_s']}

def reference(x, ctx_1024, mask_Bx1xSxS2_bk1, L0_attn_wq, L0_attn_wk, L0_attn_wv, L0_attn_wo, L0_xattn_Wq, L0_xattn_bq, L0_xattn_Wk, L0_xattn_bk, L0_xattn_Wv, L0_xattn_bv, L0_xattn_Wo, L0_xattn_bo, L0_ffn_Wr, L0_ffn_W1, L0_ffn_b1, L0_ffn_W2, L0_ffn_b2, L1_attn_w_qkv, L1_attn_w_o, L1_xattn_Wk, L1_xattn_Wv, L1_xattn_bv, L1_xattn_Wq, L1_xattn_bq, L1_xattn_Wo, L1_xattn_bo, L1_ffn_w_gate, L1_ffn_w1_e, L1_ffn_w3_e, L1_ffn_w2_e, L1_ffn_w1_s, L1_ffn_w3_s, L1_ffn_w2_s):
    import jax
    import jax.numpy as jnp

    def _L0_attn_ref(x, wq, wk, wv, wo):
        import jax, jax.numpy as jnp
        import numpy as np
        N_HEADS = 16
        HIDDEN = 128
        HEAD_DIM = 64
        BSZ = 4
        SEQ = 128
        SCALE = HEAD_DIM ** (-0.5)
        bsz, seqlen, _ = x.shape
        xq = jnp.einsum('bsh,oh->bso', x, wq)
        xk = jnp.einsum('bsh,oh->bso', x, wk)
        xv = jnp.einsum('bsh,oh->bso', x, wv)
        xq = xq.reshape(bsz, N_HEADS, seqlen, HEAD_DIM)
        xk = xk.reshape(bsz, N_HEADS, seqlen, HEAD_DIM)
        xv = xv.reshape(bsz, N_HEADS, seqlen, HEAD_DIM)
        scores = jnp.einsum('bhid,bhjd->bhij', xq, xk) * SCALE
        scores = jax.nn.softmax(scores, axis=-1)
        out = jnp.einsum('bhij,bhjd->bhid', scores, xv)
        out = out.reshape(bsz, seqlen, N_HEADS * HEAD_DIM)
        return jnp.einsum('bso,ho->bsh', out, wo)

    def _L0_xattn_ref(queries, keys, values, mask, Wq, bq, Wk, bk, Wv, bv, Wo, bo):
        import jax, jax.numpy as jnp
        import numpy as np
        B, S, D, H = (4, 256, 128, 16)
        HD = D // H
        b, sq, d = queries.shape

        def split_heads(x):
            return x.reshape(b, x.shape[1], H, HD).transpose(0, 2, 1, 3)
        q = split_heads(queries @ Wq + bq)
        k = split_heads(keys @ Wk + bk)
        v = split_heads(values @ Wv + bv)
        scores = jnp.einsum('bhqd,bhkd->bhqk', q, k) / jnp.sqrt(jnp.float32(HD))
        scores = jnp.where(mask, jnp.float32(-1000000000000000.0), scores)
        attn = jax.nn.softmax(scores, axis=-1)
        ctx = jnp.einsum('bhqk,bhkd->bhqd', attn, v)
        ctx = ctx.transpose(0, 2, 1, 3).reshape(b, sq, d)
        return ctx @ Wo + bo

    def _L0_ffn_ref(x, Wr, W1, b1, W2, b2):
        import jax, jax.numpy as jnp
        import numpy as np
        from math import ceil
        CAPACITY_FACTOR = 2.0
        MIN_CAPACITY = 4
        B, S, D = x.shape
        E = Wr.shape[1]
        N = B * S
        k = max(MIN_CAPACITY, ceil(N * CAPACITY_FACTOR / E))
        xt = x.reshape(N, D)
        scores = jax.nn.softmax(xt @ Wr, axis=-1)
        G, idx = jax.lax.top_k(scores.T, k)
        X_in = xt[idx]
        h = jax.nn.gelu(jnp.einsum('ekd,edh->ekh', X_in, W1) + b1[:, None, :], approximate=False)
        X_e = jnp.einsum('ekh,ehd->ekd', h, W2) + b2[:, None, :]
        contrib = (G[..., None] * X_e).reshape(E * k, D)
        out = jnp.zeros((N, D), dtype=x.dtype).at[idx.reshape(-1)].add(contrib)
        return out.reshape(B, S, D)

    def _L1_attn_ref(inputs, w_qkv, w_o):
        import jax, jax.numpy as jnp
        import numpy as np
        B, P, D = (8, 128, 128)
        H, N = (16, 64)
        proj = jnp.einsum('bpv,havn->bhapn', inputs, w_qkv)
        q = proj[:, :, 0]
        k = proj[:, :, 1]
        v = proj[:, :, 2]
        head_dim = q.shape[-1]
        scale = 1.0 / jnp.sqrt(jnp.asarray(head_dim, dtype=jnp.float32))
        scores = jnp.einsum('bhqn,bhkn->bhqk', q, k) * scale
        attn = jax.nn.softmax(scores, axis=-1)
        out = jnp.einsum('bhqk,bhkn->bhqn', attn, v)
        b, h, p, n = out.shape
        concat = out.transpose(0, 2, 1, 3).reshape(b, p, h * n)
        return jnp.einsum('bpi,ij->bpj', concat, w_o)

    def _L1_xattn_ref(k, v, q, Wk, Wv, bv, Wq, bq, Wo, bo):
        import jax, jax.numpy as jnp
        import numpy as np
        D_MODEL = 128
        B, S = (4, 256)
        kp = jnp.einsum('bsd,ed->bse', k, Wk)
        vp = jnp.einsum('bsd,ed->bse', v, Wv) + bv
        qp = jnp.einsum('bsd,ed->bse', q, Wq) + bq
        scale = 1.0 / jnp.sqrt(jnp.float32(kp.shape[-1]))
        scores = jnp.einsum('bqd,bkd->bqk', qp, kp) * scale
        probs = jax.nn.softmax(scores, axis=-1)
        ctx = jnp.einsum('bqk,bkd->bqd', probs, vp)
        return jnp.einsum('bqd,ed->bqe', ctx, Wo) + bo

    def _L1_ffn_ref(hidden_states, w_gate, w1_e, w3_e, w2_e, w1_s, w3_s, w2_s):
        import jax, jax.numpy as jnp
        import numpy as np
        B, S, H = (2, 128, 128)
        E, F = (16, 64)
        G, TOPK_G, TOPK = (4, 2, 4)
        N_SHARED = 2
        ROUTE_SCALE = 1.0
        FS = N_SHARED * F

        def _gate(x, w_gate):
            T = x.shape[0]
            scores = jax.nn.sigmoid(x @ w_gate.T)
            sv = scores.reshape(T, G, E // G)
            group_scores = jax.lax.top_k(sv, 2)[0].sum(-1)
            top_groups = jax.lax.top_k(group_scores, TOPK_G)[1]
            allowed = jnp.zeros((T, G), dtype=bool).at[jnp.arange(T)[:, None], top_groups].set(True)
            masked = jnp.where(allowed[:, :, None], sv, -jnp.inf).reshape(T, E)
            _, idx = jax.lax.top_k(masked, TOPK)
            w = jnp.take_along_axis(scores, idx, axis=1)
            w = w / (w.sum(-1, keepdims=True) + 1e-06) * ROUTE_SCALE
            return (w, idx)

        def _swiglu(x, w1, w3, w2):
            return jax.nn.silu(x @ w1.T) * (x @ w3.T) @ w2.T
        shape = hidden_states.shape
        x = hidden_states.reshape(-1, H)
        weights, idx = _gate(x, w_gate)
        combine = (jax.nn.one_hot(idx, E, dtype=x.dtype) * weights[..., None]).sum(1)
        g = jax.nn.silu(jnp.einsum('th,efh->tef', x, w1_e))
        u = jnp.einsum('th,efh->tef', x, w3_e)
        routed = jnp.einsum('tef,ehf,te->th', g * u, w2_e, combine)
        shared = _swiglu(x, w1_s, w3_s, w2_s)
        return (routed + shared).reshape(shape)
    x = x + _L0_attn_ref(_layernorm(x, axis=-1), L0_attn_wq, L0_attn_wk, L0_attn_wv, L0_attn_wo)
    x = x + _L0_xattn_ref(_layernorm(x, axis=-1), ctx_1024, ctx_1024, mask_Bx1xSxS2_bk1, L0_xattn_Wq, L0_xattn_bq, L0_xattn_Wk, L0_xattn_bk, L0_xattn_Wv, L0_xattn_bv, L0_xattn_Wo, L0_xattn_bo)
    x = x + _L0_ffn_ref(_layernorm(x, axis=-1), L0_ffn_Wr, L0_ffn_W1, L0_ffn_b1, L0_ffn_W2, L0_ffn_b2)
    x = x + _L1_attn_ref(_layernorm(x, axis=-1), L1_attn_w_qkv, L1_attn_w_o)
    x = x + _L1_xattn_ref(ctx_1024, ctx_1024, _layernorm(x, axis=-1), L1_xattn_Wk, L1_xattn_Wv, L1_xattn_bv, L1_xattn_Wq, L1_xattn_bq, L1_xattn_Wo, L1_xattn_bo)
    x = x + _L1_ffn_ref(_layernorm(x, axis=-1), L1_ffn_w_gate, L1_ffn_w1_e, L1_ffn_w3_e, L1_ffn_w2_e, L1_ffn_w1_s, L1_ffn_w3_s, L1_ffn_w2_s)
    return x

_drawn_inputs = setup_inputs


def setup_inputs(seed=0):
    import zlib

    import numpy as np

    out = dict(_drawn_inputs(seed))
    spreads = {'L0_xattn_bq': (0.0, 0.1),
     'L0_xattn_bk': (0.0, 0.8),
     'L0_xattn_bv': (0.0, 0.1),
     'L0_xattn_bo': (0.0, 0.1),
     'L0_ffn_b1': (0.0, 0.368),
     'L0_ffn_b2': (0.0, 0.1),
     'L1_xattn_bv': (0.0, 0.1),
     'L1_xattn_bq': (0.0, 0.466),
     'L1_xattn_bo': (0.0, 0.1)}
    factors = {'L1_ffn_w_gate': 8.0,
     'L1_ffn_w1_e': 8.0,
     'L1_ffn_w3_e': 8.0,
     'L1_ffn_w2_e': 8.0,
     'L1_ffn_w1_s': 8.0,
     'L1_ffn_w3_s': 8.0,
     'L1_ffn_w2_s': 8.0}
    for name, (base, spread) in spreads.items():
        noise = np.random.default_rng([zlib.crc32(name.encode()), seed]).standard_normal(out[name].shape)
        drawn = base * np.exp(spread * noise) if base else spread * noise
        out[name] = jnp.asarray(drawn.astype(out[name].dtype))
    for name, factor in factors.items():
        out[name] = (out[name] * factor).astype(out[name].dtype)
    return out
```

```python
from contextlib import ExitStack

import concourse.bass as bass
from concourse import mybir

F32 = mybir.dt.float32
BF16 = mybir.dt.bfloat16
U8 = mybir.dt.uint8
U32 = mybir.dt.uint32
ALU = mybir.AluOpType
ACT = mybir.ActivationFunctionType
AX = mybir.AxisListType

B = 16
T = 128
D = 128
KL = 120
N = B * T
H = 16
HD = 64
U = 4
HU = H // U
XHD = D // H
E0, F0, CAP = 8, 512, 512
C0 = F0 // 128
E1, F1 = 16, 64
G1, TOPG, TOPK = 4, 2, 4
FC = E1 * F1 // 128 + 1
EPS = 1e-5
GRP = 4
NG = B // GRP
GT = GRP * T
MASKED = -1.0e15


def need(eng, sem, value):
    if isinstance(value, int) and value <= 0:
        return
    eng.wait_ge(sem, value)


class Chain:

    def __init__(self, eng, sem, base=0):
        self.eng, self.sem, self.base, self.n = eng, sem, base, 0

    def step(self, ins):
        ins.then_inc(self.sem, 1)
        self.n += 1
        self.eng.wait_ge(self.sem, self.base + self.n)


def for_batches(eng, body):
    body(0, 0)
    body(1, 1)
    with eng.Fori(0, (B - 4) // 2) as i:
        body(2 * i + 2, 0)
        body(2 * i + 3, 1)
    body(B - 2, 0)
    body(B - 1, 1)


def for_groups(eng, body):
    body(0)
    with eng.Fori(1, NG - 1) as g:
        body(g)
    body(NG - 1)


class Namespace:
    pass


def known_first(b):
    return isinstance(b, int) and b == 0


def known_last(b):
    return isinstance(b, int) and b == B - 1




def loads_sync(sp, m, a):
    sp.dma_start(m.X[:, :], a["x"]).then_inc(m.ld["x"], 16)
    sp.dma_start(m.consts[:, :], a["consts"]).then_inc(m.ld["consts"], 16)
    sp.dma_start(m.att_w[0], a["wqT"]).then_inc(m.ld["wqkT"], 16)
    sp.dma_start(m.att_w[1], a["wkT"]).then_inc(m.ld["wqkT"], 16)
    sp.dma_start(m.att_w[2], a["wvT"]).then_inc(m.ld["wvT"], 16)
    sp.dma_start(m.w["w_o"][:, :], a["woT"]).then_inc(m.ld["woT"], 16)


def loads_pool(po, m, a):
    for tile, name in ((m.w["ctxT"], "ctxT"), (m.mask8, "mask")):
        po.dma_start(tile[:, :], a[name]).then_inc(m.ld["ctxT"], 16)
    for tile, name in ((m.w["x0Wk"], "x0Wk"), (m.w["x1WkT"], "x1WkT"), (m.w["WvBoth"], "WvBoth"), (m.w["x0bk"], "x0bk"),
                       (m.w["bvBoth"], "bvBoth")):
        po.dma_start(tile[:, :], a[name]).then_inc(m.ld["xkv"], 16)
    for tile, name in ((m.w["x0Wq"], "x0Wq"), (m.w["x0Wo"], "x0Wo"), (m.w["x0bq"], "x0bq"), (m.w["x0bo"], "x0bo")):
        po.dma_start(tile[:, :], a[name]).then_inc(m.ld["x0"], 16)
    for tile, name in ((m.w["Wr"], "Wr"), (m.w["W1"], "W1"), (m.w["W2"], "W2"), (m.w["b1T"], "b1T"), (m.w["b2rep"], "b2rep")):
        po.dma_start(tile[:, :], a[name]).then_inc(m.ld["ffn0"], 16)
    for tile, name in ((m.w["x1WqT"], "x1WqT"), (m.w["x1WoT"], "x1WoT"), (m.w["x1bq"], "x1bq"), (m.w["x1bo"], "x1bo")):
        po.dma_start(tile[:, :], a[name]).then_inc(m.ld["x1"], 16)
    for tile, name in ((m.w["gateT"], "gateT"), (m.w["w1T"], "w1T"), (m.w["w3T"], "w3T"), (m.w["w2T"], "w2T")):
        po.dma_start(tile[:, :], a[name]).then_inc(m.ld["ffn1"], 16)


def attention1_loads_pool(po, m, a):
    po.wait_ge(m.stream_ready, 2)
    for tile, name in ((m.w["wqkv"], "wqkv"), (m.w["w_o"], "w_o")):
        po.dma_start(tile[:, :], a[name]).then_inc(m.ld["attn1"], 16)


LOADED = {"x": 16, "consts": 16, "wqkT": 32, "wvT": 16, "woT": 16, "ctxT": 32, "xkv": 80, "x0": 64,
          "ffn0": 80, "attn1": 32, "x1": 64, "ffn1": 64}


def loaded(eng, m, name):
    eng.wait_ge(m.ld[name], LOADED[name])


def setup_vector(v, m):
    loaded(v, m, "consts")
    v.tensor_copy(m.identb[:, :], m.ident).then_inc(m.const_ready, 1)
    v.memset(m.ones[:, :], 1.0).then_inc(m.const_ready, 1)
    loaded(v, m, "x")
    for b in range(B):
        ins = v.bn_stats(m.stats[:, 6 * b:6 * b + 6], m.X[:, b * D:(b + 1) * D])
    ins.then_inc(m.stream_ready, 1)


def moments_vector(v, m, k):
    c = Chain(v, m.moment_chain, 6 * k)
    v.wait_ge(m.stream_ready, k + 1)
    st = m.stats[:, :].rearrange("p (b s) -> p s b", s=6)
    c.step(v.tensor_tensor(m.mean[:, :], st[:, 1], st[:, 4], ALU.add))
    c.step(v.tensor_tensor(m.st1[:, :], st[:, 1], st[:, 4], ALU.subtract))
    c.step(v.tensor_tensor(m.st2[:, :], st[:, 2], st[:, 5], ALU.add))
    c.step(v.tensor_scalar(m.mean[:, :], m.mean[:, :], 0.5, None, ALU.mult))
    c.step(v.tensor_tensor(m.st1[:, :], m.st1[:, :], m.st1[:, :], ALU.mult))
    c.step(v.tensor_scalar(m.st2[:, :], m.st2[:, :], 1.0 / D, EPS, ALU.mult, ALU.add))
    v.scalar_tensor_tensor(m.st2[:, :], m.st1[:, :], 0.25, m.st2[:, :], ALU.mult, ALU.add).then_inc(m.var_ready, 1)


def moments_pool(po, m, k):
    po.wait_ge(m.var_ready, k + 1)
    if k == 0:
        loaded(po, m, "consts")
    po.tensor_tensor(m.rstd[:, :], m.st2[:, :], m.minus_half, ALU.pow).then_inc(m.rstd_ready, 1)


def normalise(v, m, b, dst):
    return v.tensor_scalar(dst, m.X[:, bass.ds(b * D, D)], m.mean[:, bass.ds(b, 1)], m.rstd[:, bass.ds(b, 1)],
                           ALU.subtract, ALU.mult)


ATT_SEMS = ["xn_ready", "xT_in_psum", "xT_ready", "q_proj", "k_proj", "v_proj", "q_ready", "k_ready", "v_evac",
            "scores_ready", "max_done", "negmax_ready", "exp_done", "inverse_ready", "probs_ready", "probsT_in_psum",
            "probsT_ready", "av_done", "av_evac", "out_done", "res_done"]


def att_tiles(m):
    t = Namespace()
    ar = m.arena
    t.Q = [ar[:, 0:2048], ar[:, 2048:4096]]
    t.K = [ar[:, 4096:6144], ar[:, 6144:8192]]
    t.V = [ar[:, 8192:9216], ar[:, 9216:10240]]
    t.Vst = [ar[:, 10240:11264], ar[:, 11264:12288]]
    t.P = [ar[:, 12288 + 512 * i:12800 + 512 * i] for i in range(U)]
    t.PT = [ar[:, 14336 + 512 * i:14848 + 512 * i] for i in range(2)]
    t.OT = [ar[:, 15360 + 1024 * i:16384 + 1024 * i] for i in range(2)]
    t.negmax = [m.small[:, 4 * u:4 * u + 4] for u in range(U)]
    t.total = [m.small[:, 16 + 4 * u:20 + 4 * u] for u in range(U)]
    t.inverse = [m.small[:, 32 + 4 * u:36 + 4 * u] for u in range(U)]
    t.xn = [m.xn[:, 0:D], m.xn[:, D:2 * D]]
    t.xT = [m.XTs[:, 0:T], m.XTs[:, T:2 * T]]
    return t


PIECES = {0: [("q", 0), ("q", 1)], 1: [("k", 0)], 2: [("k", 1), ("v", 0)], 3: [("v", 1)]}


def att_tensor(pe, m, layer):
    s, t = m.att[layer], att_tiles(m)
    wq, wk, wv, wo = m.att_w

    def transpose_tokens(b, p):
        pe.wait_ge(s["xn_ready"], b + 1)
        need(pe, s["res_done"], b - 2)
        need(pe, s["xT_ready"], b)
        pe.transpose(m.MX[:, 0:T], t.xn[p], m.ident).then_inc(s["xT_in_psum"], 1)

    def project(b, p, kind, g):
        bank = m.PJ[g]
        if kind == "q":
            if g == 0:
                pe.wait_ge(s["xT_ready"], b + 1)
            need(pe, s["v_evac"], 2 * b - 1 + g)
        elif kind == "k":
            pe.wait_ge(s["q_ready"], 2 * b + 1 + g)
        else:
            pe.wait_ge(s["k_ready"], 2 * b + 1 + g)
        if kind == "v":
            pe.matmul(bank[:, :], t.xT[p], wv[:, 512 * g:512 * g + 512], start=True, stop=True).then_inc(s["v_proj"], 1)
            return
        w, done = (wq, s["q_proj"]) if kind == "q" else (wk, s["k_proj"])
        for c in range(4):
            chunk = 4 * g + c
            ins = pe.matmul(bank[:, c * T:(c + 1) * T], w[:, chunk * 128:(chunk + 1) * 128], t.xT[p],
                            start=True, stop=True)
        ins.then_inc(done, 1)

    def scores(b, p, u):
        n = U * b + u
        if u == 0:
            pe.wait_ge(s["q_ready"], 2 * (b + 1))
            pe.wait_ge(s["k_ready"], 2 * (b + 1))
        need(pe, s["exp_done"], n - 1)
        bank = m.S[u % 2]
        if layer == 0:
            for j in range(HU):
                h = HU * u + j
                ins = pe.matmul(bank[:, j * 128:(j + 1) * 128], t.Q[p][0:HD, h * 128:(h + 1) * 128],
                                t.K[p][0:HD, h * 128:(h + 1) * 128], start=True, stop=True)
        else:
            for j in range(2):
                pair = 2 * u + j
                ins = pe.matmul(bank[:, j * 256:(j + 1) * 256], t.Q[p][:, pair * 128:(pair + 1) * 128],
                                t.K[p][:, pair * 256:(pair + 1) * 256], start=True, stop=True)
        ins.then_inc(s["scores_ready"], 1)

    def transpose_probs(n, u):
        pe.wait_ge(s["probs_ready"], n + 1)
        need(pe, s["probsT_ready"], n - 1)
        for j in range(HU):
            ins = pe.transpose(m.TP[u % 2][:, j * 128:(j + 1) * 128], t.P[u][:, j * 128:(j + 1) * 128], m.ident)
        ins.then_inc(s["probsT_in_psum"], 1)

    def values(b, p, u):
        n = U * b + u
        pe.wait_ge(s["probsT_ready"], n + 1)
        need(pe, s["av_evac"], n)
        if u == 0:
            if layer == 0:
                pe.wait_ge(m.v_load[p], 8 * (b - p) + 16)
            else:
                pe.wait_ge(s["v_evac"], 2 * (b + 1))
        PT, V = t.PT[u % 2], t.V[p]
        for j in range(HU):
            h = HU * u + j
            if layer == 0:
                for par in range(2):
                    ins = pe.matmul(m.OV[par * 64:par * 64 + 64, j * 64:j * 64 + 64], V[:, h * HD:(h + 1) * HD],
                                    PT[:, j * 128 + par * 64:j * 128 + par * 64 + 64], start=True, stop=True)
            else:
                par = j % 2
                ins = pe.matmul(m.OV[par * 64:par * 64 + 64, (j // 2) * 128:(j // 2) * 128 + 128],
                                V[:, h * HD:(h + 1) * HD], PT[:, j * 128:(j + 1) * 128], start=True, stop=True)
        ins.then_inc(s["av_done"], 1)

    def output(b, p):
        pe.wait_ge(s["av_evac"], U * (b + 1))
        need(pe, s["xT_ready"], min(b + 3, B) if isinstance(b, int) else b + 3)
        need(pe, s["res_done"], b)
        for c in range(8):
            ins = pe.matmul(m.MX[:, 0:D], t.OT[p][:, c * T:(c + 1) * T], wo[:, c * D:(c + 1) * D],
                            start=(c == 0), stop=(c == 7))
        ins.then_inc(s["out_done"], 1)

    loaded(pe, m, "consts")
    transpose_tokens(0, 0)
    for name in (("wqkT", "wvT", "woT") if layer == 0 else ("attn1",)):
        loaded(pe, m, name)
    for u in range(U):
        for kind, g in PIECES[u]:
            project(0, 0, kind, g)
    transpose_tokens(1, 1)

    def slots(b, p):
        for u in range(U):
            scores(b, p, u)
            if not known_last(b):
                for kind, g in PIECES[u]:
                    project(b + 1, 1 - p, kind, g)
            n = U * b + u
            if not (known_first(b) and u < 1):
                transpose_probs(n - 1, (u - 1) % U)
            if not (known_first(b) and u < 2):
                values(b if u >= 2 else b - 1, p if u >= 2 else 1 - p, (u - 2) % U)
            if u == 2 and not known_first(b):
                output(b - 1, 1 - p)
            if u == 3 and not (isinstance(b, int) and b + 2 >= B):
                transpose_tokens(b + 2, p)

    for_batches(pe, slots)
    transpose_probs(U * B - 1, U - 1)
    values(B - 1, 1, U - 2)
    values(B - 1, 1, U - 1)
    output(B - 1, 1)


def att_scalar(act, m, layer):
    s, t = m.att[layer], att_tiles(m)
    scale = HD ** -0.5

    def exps(b, p, u):
        n = U * b + u
        act.wait_ge(s["negmax_ready"], n + 1)
        need(act, s["probsT_in_psum"], n - 3)
        for j in range(HU):
            ins = act.activation(t.P[u][:, j * 128:(j + 1) * 128], m.S[u % 2][:, j * 128:(j + 1) * 128], ACT.Exp,
                                 bias=t.negmax[u][:, j:j + 1], scale=scale, accum_out=t.total[u][:, j:j + 1])
        ins.then_inc(s["exp_done"], 1)

    def take_q(b, p, g):
        act.wait_ge(s["q_proj"], 2 * b + g + 1)
        if layer == 0:
            for par in range(2):
                src = m.PJ[g][par * 64:par * 64 + 64, :].rearrange("d (c h t) -> d c h t", c=4, t=8)
                dst = t.Q[p][0:HD, :].rearrange("d (h r c t) -> d r c h t", h=H, r=2, c=8)[:, par, 4 * g:4 * g + 4]
                ins = act.activation(dst, src, ACT.Copy)
        else:
            ins = act.activation(t.Q[p][:, 512 * g:512 * g + 512], m.PJ[g][:, :], ACT.Copy)
        ins.then_inc(s["q_ready"], 1)

    def take_v(b, p, g):
        act.wait_ge(s["v_proj"], 2 * b + g + 1)
        if layer == 0:
            if not (isinstance(b, int) and b < 2):
                act.wait_ge(m.v_save[p], 8 * (b - p))
            dst = t.Vst[p]
        else:
            dst = t.V[p]
        act.activation(dst[:, 512 * g:512 * g + 512], m.PJ[g][:, :], ACT.Copy).then_inc(s["v_evac"], 1)

    def take_probsT(n, u):
        act.wait_ge(s["probsT_in_psum"], n + 1)
        need(act, s["av_done"], n - 1)
        act.activation(t.PT[u % 2], m.TP[u % 2][:, :], ACT.Copy).then_inc(s["probsT_ready"], 1)

    def take_xT(b, p):
        act.wait_ge(s["xT_in_psum"], b + 1)
        act.activation(t.xT[p], m.MX[:, 0:T], ACT.Copy).then_inc(s["xT_ready"], 1)

    def piece(b, p, kind, g):
        if kind == "q":
            take_q(b, p, g)
        elif kind == "v":
            take_v(b, p, g)

    act.preload_act_table(ACT.Exp)
    take_xT(0, 0)
    for u in range(U):
        for kind, g in PIECES[u]:
            piece(0, 0, kind, g)
    take_xT(1, 1)

    def slots(b, p):
        for u in range(U):
            exps(b, p, u)
            if not known_last(b):
                for kind, g in PIECES[u]:
                    piece(b + 1, 1 - p, kind, g)
            if not (known_first(b) and u < 1):
                take_probsT(U * b + u - 1, (u - 1) % U)
            if u == 3 and not (isinstance(b, int) and b + 2 >= B):
                take_xT(b + 2, p)

    for_batches(act, slots)
    take_probsT(U * B - 1, U - 1)


def att_vector(v, m, layer):
    s, t = m.att[layer], att_tiles(m)
    scale = HD ** -0.5

    def take_k(b, p, g):
        v.wait_ge(s["k_proj"], 2 * b + g + 1)
        for par in range(2):
            if layer == 0:
                src = m.PJ[g][par * 64:par * 64 + 64, :].rearrange("d (c h t) -> d c h t", c=4, t=8)
                dst = t.K[p][0:HD, :].rearrange("d (h t c r) -> d r c h t", h=H, t=8, r=2)[:, par, 4 * g:4 * g + 4]
            else:
                src = m.PJ[g][par * 64:par * 64 + 64, :].rearrange("d (c j) -> d c j", c=4)
                dst = t.K[p][par * 64:par * 64 + 64, :].rearrange("d (c r j) -> d r c j", r=2, j=128)[
                    :, par, 4 * g:4 * g + 4]
            ins = v.tensor_copy(dst, src)
        ins.then_inc(s["k_ready"], 1)

    def maxima(b, p, u):
        n = U * b + u
        v.wait_ge(s["scores_ready"], n + 1)
        v.tensor_reduce(t.mx[u], m.S[u % 2][:, :].rearrange("p (j k) -> p j k", j=HU), AX.X, ALU.max)\
            .then_inc(s["max_done"], 1)
        v.wait_ge(s["max_done"], n + 1)
        v.tensor_scalar(t.negmax[u], t.mx[u], -scale, None, ALU.mult).then_inc(s["negmax_ready"], 1)

    def inverse(b, p, u):
        n = U * b + u
        v.wait_ge(s["exp_done"], n + 1)
        v.reciprocal(t.inverse[u], t.total[u]).then_inc(s["inverse_ready"], 1)

    def take_av(b, p, u):
        n = U * b + u
        v.wait_ge(s["av_done"], n + 1)
        if layer == 0:
            src = m.OV[:, 0:256].rearrange("p (h c t) -> p h c t", h=HU, c=8)
            dst = t.OT[p].rearrange("p (c h t) -> p h c t", c=8, t=8)[:, HU * u:HU * u + HU]
        else:
            src, dst = m.OV[:, 0:256], t.OT[p][:, 256 * u:256 * u + 256]
        v.tensor_copy(dst, src).then_inc(s["av_evac"], 1)

    def take_output(b, p):
        v.wait_ge(s["out_done"], b + 1)
        x = m.X[:, bass.ds(b * D, D)]
        v.tensor_tensor(x, x, m.MX[:, 0:D], ALU.add).then_inc(s["res_done"], 1)
        v.wait_ge(s["res_done"], b + 1)
        return v.bn_stats(m.stats[:, bass.ds(6 * b, 6)], x)

    def tokens(b, p):
        need(v, s["xT_in_psum"], b - 1)
        normalise(v, m, b, t.xn[p]).then_inc(s["xn_ready"], 1)

    t.mx = [m.small[:, 64 + 4 * u:68 + 4 * u] for u in range(U)]
    v.wait_ge(m.rstd_ready, m.att_k[layer] + 1)
    if layer == 1:
        for p in range(2):
            ins = v.memset(t.K[p].bitcast(U32), 0)
        ins.then_inc(m.zeroed, 1)
        v.wait_ge(m.zeroed, 1)
    tokens(0, 0)
    tokens(1, 1)
    take_k(0, 0, 0)
    take_k(0, 0, 1)

    def slots(b, p):
        for u in range(U):
            maxima(b, p, u)
            if not (known_first(b) and u < 3):
                take_av(b if u == 3 else b - 1, p if u == 3 else 1 - p, (u - 3) % U)
            if not known_last(b):
                for kind, g in PIECES[u]:
                    if kind == "k":
                        take_k(b + 1, 1 - p, g)
            if u == 3 and not known_first(b):
                take_output(b - 1, 1 - p)
            inverse(b, p, u)
            if u == 1 and not (isinstance(b, int) and b + 2 >= B):
                tokens(b + 2, p)

    for_batches(v, slots)
    for u in range(1, U):
        take_av(B - 1, 1, u)
    take_output(B - 1, 1).then_inc(m.stream_ready, 1)


def att_pool(po, m, layer):
    s, t = m.att[layer], att_tiles(m)

    def divide(b, p, u):
        n = U * b + u
        po.wait_ge(s["inverse_ready"], n + 1)
        P = t.P[u].rearrange("p (j k) -> p j k", j=HU)
        po.tensor_tensor(P, P, t.inverse[u].unsqueeze(2).to_broadcast([128, HU, 128]), ALU.mult)\
            .then_inc(s["probs_ready"], 1)

    def slots(b, p):
        for u in range(U):
            divide(b, p, u)

    for_batches(po, slots)


def att_sync(sp, m, scratch):
    s, t = m.att[0], att_tiles(m)

    def move(b, p):
        sp.wait_ge(s["v_evac"], 2 * (b + 1))
        sp.dma_start(scratch[p], t.Vst[p]).then_inc(m.v_save[p], 16)
        sp.wait_ge(m.v_save[p], 8 * (b - p) + 16)
        sp.dma_start(t.V[p].rearrange("p (h d) -> p h d", h=H),
                     scratch[p].rearrange("(h t) (c d) -> (t c) h d", h=H, d=HD)).then_inc(m.v_load[p], 16)

    for_batches(sp, move)


def context_tensor(pe, m):
    loaded(pe, m, "ctxT")
    loaded(pe, m, "xkv")
    pe.wait_ge(m.stream_ready, 2)
    for g in range(NG):
        cols = slice(GRP * KL * g, GRP * KL * (g + 1))
        for w, bank, made, taken in ((m.w["x0Wk"], m.PJ[0], m.k0_made, m.k0_taken), (m.w["x1WkT"], m.PJ[1], m.k1_made, m.k1_taken)):
            need(pe, taken, g)
            pe.matmul(bank[:, 0:GRP * KL], w[:, :], m.w["ctxT"][:, cols], start=True, stop=True).then_inc(made, 1)
    for b in range(B):
        if b % 2 == 0:
            need(pe, m.v01_taken, b // 2 - 1)
        ins = pe.matmul(m.S[b // 2 % 2][0:KL, 256 * (b % 2):256 * (b % 2) + 256], m.w["ctxT"][:, KL * b:KL * (b + 1)],
                        m.w["WvBoth"][:, :], start=True, stop=True)
        if b % 2 == 1:
            ins.then_inc(m.v01_made, 1)


def context_scalar(act, m):
    for g in range(NG):
        act.wait_ge(m.k1_made, g + 1)
        act.activation(m.KT1[:, GRP * KL * g:GRP * KL * (g + 1)], m.PJ[1][:, 0:GRP * KL], ACT.Copy)\
            .then_inc(m.k1_taken, 1)


def context_vector(v, m):
    loaded(v, m, "ctxT")
    loaded(v, m, "xkv")
    v.tensor_scalar(m.maskb[:, :], m.mask8[:, :], MASKED, None, ALU.mult).then_inc(m.mask_ready, 1)
    for g in range(NG):
        v.wait_ge(m.k0_made, g + 1)
        v.tensor_scalar(m.KT0[:, GRP * KL * g:GRP * KL * (g + 1)], m.PJ[0][:, 0:GRP * KL], m.w["x0bk"][:, 0:1], None,
                        ALU.add).then_inc(m.k0_taken, 1)
    for i in range(B // 2):
        v.wait_ge(m.v01_made, i + 1)
        bias = m.w["bvBoth"][0:KL, :].unsqueeze(1).to_broadcast([KL, 2, 2 * D])
        v.tensor_tensor(m.V01[:, 512 * i:512 * i + 512].rearrange("k (b d) -> k b d", b=2),
                        m.S[i % 2][0:KL, :].rearrange("k (b d) -> k b d", b=2), bias, ALU.add)\
            .then_inc(m.v01_taken, 1)


CR_SEMS = ["xn_ready", "xT_in_psum", "xT_ready", "q_proj", "q_ready", "kblk_ready", "scores_ready", "max_done",
           "negmax_ready", "exp_done", "probsT_in_psum", "probsT_ready", "av_done", "inv_done", "o_ready",
           "oT_in_psum", "oT_ready", "out_done", "res_done"]


def cr_tiles(m):
    t = Namespace()
    ar = m.arena
    t.Kblk = [ar[:, 0:1920], ar[:, 1920:3840]]
    t.P = [ar[:, 4096 + 512 * u:4096 + 512 * u + HU * KL] for u in range(U)]
    t.PT = [ar[:, 6144:6656], ar[:, 6656:7168]]
    t.qT = [ar[:, 7168:7296], ar[:, 7296:7424]]
    t.o = ar[:, 7424:7552]
    t.oT = ar[:, 7552:7680]
    t.total = [m.small[:, 0:16], m.small[:, 16:32]]
    t.inverse = m.small[:, 32:48]
    t.negmax = [m.small[:, 48 + 4 * u:52 + 4 * u] for u in range(U)]
    t.mx = [m.small[:, 64 + 4 * u:68 + 4 * u] for u in range(U)]
    t.xn = [m.xn[:, 0:D], m.xn[:, D:2 * D]]
    t.xT = m.XTs[:, 0:T]
    t.O = [m.OV, m.PJ[1]]
    return t


def cross0_tensor(pe, m):
    s, t = m.cr, cr_tiles(m)

    def transpose_tokens(b, p):
        pe.wait_ge(s["xn_ready"], b + 1)
        need(pe, s["res_done"], b - 2)
        need(pe, s["xT_ready"], b)
        pe.transpose(m.MX[:, 0:T], t.xn[p], m.ident).then_inc(s["xT_in_psum"], 1)

    def project(b):
        pe.wait_ge(s["xT_ready"], b + 1)
        need(pe, s["q_ready"], b)
        pe.matmul(m.PJ[0][:, 0:T], m.w["x0Wq"][:, :], t.xT, start=True, stop=True).then_inc(s["q_proj"], 1)

    def scores(b, p, u):
        n = U * b + u
        if u == 0:
            pe.wait_ge(s["q_ready"], b + 1)
            pe.wait_ge(s["kblk_ready"], b + 1)
        need(pe, s["exp_done"], n - 1)
        mask = m.maskb[:, bass.ds(b * KL, KL)].unsqueeze(1).to_broadcast([128, HU, KL])
        pe.matmul(m.S[u % 2][:, 0:HU * KL].rearrange("p (j k) -> p j k", j=HU), m.identb[:, :], mask,
                  start=True, stop=False)
        pe.matmul(m.S[u % 2][:, 0:HU * KL], t.qT[p], t.Kblk[p][:, HU * KL * u:HU * KL * (u + 1)],
                  start=False, stop=True).then_inc(s["scores_ready"], 1)

    def transpose_probs(n, u):
        pe.wait_ge(s["exp_done"], n + 1)
        need(pe, s["probsT_ready"], n - 1)
        for j in range(HU):
            ins = pe.transpose(m.TP[u % 2][0:KL, j * 128:(j + 1) * 128], t.P[u][:, j * KL:(j + 1) * KL], m.ident)
        ins.then_inc(s["probsT_in_psum"], 1)

    def values(b, p, u):
        n = U * b + u
        pe.wait_ge(s["probsT_ready"], n + 1)
        if u == 0:
            need(pe, s["o_ready"], b - 1)
        for j in range(HU):
            h = HU * u + j
            ins = pe.matmul(t.O[p][:, h * XHD:(h + 1) * XHD], t.PT[u % 2][0:KL, j * 128:(j + 1) * 128],
                            m.V01[0:KL, bass.ds(b * 2 * D + h * XHD, XHD)], start=True, stop=True)
        ins.then_inc(s["av_done"], 1)

    def transpose_o(b):
        pe.wait_ge(s["o_ready"], b + 1)
        need(pe, s["xT_ready"], min(b + 3, B) if isinstance(b, int) else b + 3)
        need(pe, s["res_done"], b)
        pe.transpose(m.MX[:, 0:T], t.o, m.ident).then_inc(s["oT_in_psum"], 1)

    def output(b):
        pe.wait_ge(s["oT_ready"], b + 1)
        pe.matmul(m.MX[:, 0:D], m.ones[0:1, :], m.w["x0bo"][0:1, :], start=True, stop=False)
        pe.matmul(m.MX[:, 0:D], t.oT, m.w["x0Wo"][:, :], start=False, stop=True).then_inc(s["out_done"], 1)

    loaded(pe, m, "x0")
    pe.wait_ge(m.mask_ready, 1)
    pe.wait_ge(m.const_ready, 2)
    pe.wait_ge(m.v01_taken, B // 2)
    pe.wait_ge(m.k0_taken, NG)
    pe.wait_ge(m.k1_taken, NG)
    transpose_tokens(0, 0)
    project(0)

    def slots(b, p):
        for u in range(U):
            n = U * b + u
            scores(b, p, u)
            if not (known_first(b) and u < 1):
                transpose_probs(n - 1, (u - 1) % U)
            if u == 2 and not known_first(b):
                transpose_o(b - 1)
            if not (known_first(b) and u < 2):
                values(b if u >= 2 else b - 1, p if u >= 2 else 1 - p, (u - 2) % U)
            if u == 0 and not known_last(b):
                transpose_tokens(b + 1, 1 - p)
            if u == 2 and not known_last(b):
                project(b + 1)
            if u == 3 and not known_first(b):
                output(b - 1)

    for_batches(pe, slots)
    transpose_probs(U * B - 1, U - 1)
    values(B - 1, 1, U - 2)
    values(B - 1, 1, U - 1)
    transpose_o(B - 1)
    output(B - 1)


def cross0_scalar(act, m):
    s, t = m.cr, cr_tiles(m)

    def exps(b, p, u):
        n = U * b + u
        act.wait_ge(s["negmax_ready"], n + 1)
        need(act, s["probsT_in_psum"], n - 3)
        for j in range(HU):
            ins = act.activation(t.P[u][:, j * KL:(j + 1) * KL], m.S[u % 2][:, j * KL:(j + 1) * KL], ACT.Exp,
                                 bias=t.negmax[u][:, j:j + 1], scale=XHD ** -0.5,
                                 accum_out=t.total[p][:, HU * u + j:HU * u + j + 1])
        ins.then_inc(s["exp_done"], 1)

    def take_xT(b):
        act.wait_ge(s["xT_in_psum"], b + 1)
        act.activation(t.xT, m.MX[:, 0:T], ACT.Copy).then_inc(s["xT_ready"], 1)

    def take_q(b, p):
        act.wait_ge(s["q_proj"], b + 1)
        act.activation(t.qT[p], m.PJ[0][:, 0:T], ACT.Identity, bias=m.w["x0bq"][:, 0:1]).then_inc(s["q_ready"], 1)

    def take_oT(b):
        act.wait_ge(s["oT_in_psum"], b + 1)
        act.activation(t.oT, m.MX[:, 0:T], ACT.Copy).then_inc(s["oT_ready"], 1)

    loaded(act, m, "x0")
    act.preload_act_table(ACT.Exp)
    take_xT(0)
    take_q(0, 0)

    def slots(b, p):
        for u in range(U):
            exps(b, p, u)
            if u == 0 and not known_last(b):
                take_xT(b + 1)
            if u == 2 and not known_first(b):
                take_oT(b - 1)
            if u == 2 and not known_last(b):
                take_q(b + 1, 1 - p)

    for_batches(act, slots)
    take_oT(B - 1)


def cross0_vector(v, m):
    s, t = m.cr, cr_tiles(m)

    def maxima(b, u):
        n = U * b + u
        v.wait_ge(s["scores_ready"], n + 1)
        v.tensor_reduce(t.mx[u], m.S[u % 2][:, 0:HU * KL].rearrange("p (j k) -> p j k", j=HU), AX.X, ALU.max)\
            .then_inc(s["max_done"], 1)
        v.wait_ge(s["max_done"], n + 1)
        v.tensor_scalar(t.negmax[u], t.mx[u], -XHD ** -0.5, None, ALU.mult).then_inc(s["negmax_ready"], 1)

    def take_probsT(n, u):
        v.wait_ge(s["probsT_in_psum"], n + 1)
        need(v, s["av_done"], n - 1)
        v.tensor_copy(t.PT[u % 2][0:KL, :], m.TP[u % 2][0:KL, :]).then_inc(s["probsT_ready"], 1)

    def tokens(b, p):
        need(v, s["xT_in_psum"], b - 1)
        normalise(v, m, b, t.xn[p]).then_inc(s["xn_ready"], 1)

    def divide(b, p):
        v.wait_ge(s["av_done"], U * (b + 1))
        v.wait_ge(s["exp_done"], U * (b + 1))
        v.reciprocal(t.inverse, t.total[p]).then_inc(s["inv_done"], 1)
        v.wait_ge(s["inv_done"], b + 1)
        need(v, s["oT_in_psum"], b)
        v.tensor_tensor(t.o.rearrange("p (h d) -> p h d", h=H), t.O[p][:, 0:D].rearrange("p (h d) -> p h d", h=H),
                        t.inverse.unsqueeze(2).to_broadcast([128, H, XHD]), ALU.mult).then_inc(s["o_ready"], 1)

    def take_output(b):
        v.wait_ge(s["out_done"], b + 1)
        x = m.X[:, bass.ds(b * D, D)]
        v.tensor_tensor(x, x, m.MX[:, 0:D], ALU.add).then_inc(s["res_done"], 1)
        v.wait_ge(s["res_done"], b + 1)
        return v.bn_stats(m.stats[:, bass.ds(6 * b, 6)], x)

    v.wait_ge(m.rstd_ready, 2)
    tokens(0, 0)
    tokens(1, 1)

    def slots(b, p):
        for u in range(U):
            n = U * b + u
            maxima(b, u)
            if u == 0 and not (isinstance(b, int) and b < 2):
                take_output(b - 2)
            if u == 2 and not known_first(b):
                divide(b - 1, 1 - p)
            if not (known_first(b) and u < 1):
                take_probsT(n - 1, (u - 1) % U)
            if u == 1 and not (isinstance(b, int) and b + 2 >= B):
                tokens(b + 2, p)

    for_batches(v, slots)
    take_probsT(U * B - 1, U - 1)
    take_output(B - 2)
    divide(B - 1, 1)
    take_output(B - 1).then_inc(m.stream_ready, 1)


def cross0_pool(po, m):
    s, t = m.cr, cr_tiles(m)
    po.wait_ge(m.stream_ready, 2)
    po.wait_ge(m.k0_taken, NG)

    def blocks(b, p):
        if not (isinstance(b, int) and b < 2):
            po.wait_ge(s["scores_ready"], U * (b - 1))
        po.tensor_tensor(t.Kblk[p].rearrange("p (h k) -> p h k", h=H),
                         m.KT0[:, bass.ds(b * KL, KL)].unsqueeze(1).to_broadcast([128, H, KL]),
                         m.headmask.unsqueeze(2).to_broadcast([128, H, KL]), ALU.mult).then_inc(s["kblk_ready"], 1)

    for_batches(po, blocks)


X1_SEMS = ["xn_ready", "xT_in_psum", "xT_ready", "q_proj", "q_ready", "scores_ready", "max_done", "negmax_ready",
           "exp_done", "probsT_in_psum", "probsT_ready", "av_done", "inv_done", "o_ready", "oT_in_psum", "oT_ready",
           "out_done", "res_done"]


def x1_tiles(m):
    t = Namespace()
    ar = m.arena
    t.xn, t.xT, t.qT = m.xn[:, 0:GT], m.XTs[:, 0:GT], ar[:, 0:512]
    t.P, t.PT, t.o, t.oT = ar[:, 512:512 + GRP * KL], ar[:, 1024:1536], ar[:, 1536:2048], ar[:, 2048:2560]
    t.mx, t.negmax, t.total, t.inverse = (m.small[:, 4 * i:4 * i + 4] for i in range(4))
    return t


def cross1_tensor(pe, m):
    s, t = m.x1, x1_tiles(m)
    loaded(pe, m, "x1")

    def group(g):
        pe.wait_ge(s["xn_ready"], g + 1)
        need(pe, s["res_done"], g)
        for i in range(GRP):
            ins = pe.transpose(m.MX[:, i * T:(i + 1) * T], t.xn[:, i * D:(i + 1) * D], m.ident)
        ins.then_inc(s["xT_in_psum"], 1)
        pe.wait_ge(s["xT_ready"], g + 1)
        pe.matmul(m.PJ[0][:, :], m.w["x1WqT"][:, :], t.xT, start=True, stop=True).then_inc(s["q_proj"], 1)
        pe.wait_ge(s["q_ready"], g + 1)
        for i in range(GRP):
            ins = pe.matmul(m.S[0][:, i * KL:(i + 1) * KL], t.qT[:, i * T:(i + 1) * T],
                            m.KT1[:, bass.ds((GRP * g + i) * KL, KL)], start=True, stop=True)
        ins.then_inc(s["scores_ready"], 1)
        pe.wait_ge(s["exp_done"], g + 1)
        for i in range(GRP):
            ins = pe.transpose(m.TP[0][0:KL, i * 128:(i + 1) * 128], t.P[:, i * KL:(i + 1) * KL], m.ident)
        ins.then_inc(s["probsT_in_psum"], 1)
        pe.wait_ge(s["probsT_ready"], g + 1)
        for i in range(GRP):
            ins = pe.matmul(m.OV[:, i * D:(i + 1) * D], t.PT[0:KL, i * 128:(i + 1) * 128],
                            m.V01[0:KL, bass.ds((GRP * g + i) * 2 * D + D, D)], start=True, stop=True)
        ins.then_inc(s["av_done"], 1)
        pe.wait_ge(s["o_ready"], g + 1)
        for i in range(GRP):
            ins = pe.transpose(m.PJ[1][:, i * T:(i + 1) * T], t.o[:, i * D:(i + 1) * D], m.ident)
        ins.then_inc(s["oT_in_psum"], 1)
        pe.wait_ge(s["oT_ready"], g + 1)
        for i in range(GRP):
            pe.matmul(m.MX[:, i * D:(i + 1) * D], m.ones[0:1, :], m.w["x1bo"][0:1, :], start=True, stop=False)
            ins = pe.matmul(m.MX[:, i * D:(i + 1) * D], t.oT[:, i * T:(i + 1) * T], m.w["x1WoT"][:, :],
                            start=False, stop=True)
        ins.then_inc(s["out_done"], 1)

    for_groups(pe, group)


def cross1_scalar(act, m):
    s, t = m.x1, x1_tiles(m)
    loaded(act, m, "x1")

    def group(g):
        act.wait_ge(s["xT_in_psum"], g + 1)
        act.activation(t.xT, m.MX[:, :], ACT.Copy).then_inc(s["xT_ready"], 1)
        act.wait_ge(s["q_proj"], g + 1)
        act.activation(t.qT, m.PJ[0][:, :], ACT.Identity, bias=m.w["x1bq"][:, 0:1]).then_inc(s["q_ready"], 1)
        act.wait_ge(s["negmax_ready"], g + 1)
        for i in range(GRP):
            ins = act.activation(t.P[:, i * KL:(i + 1) * KL], m.S[0][:, i * KL:(i + 1) * KL], ACT.Exp,
                                 bias=t.negmax[:, i:i + 1], scale=D ** -0.5, accum_out=t.total[:, i:i + 1])
        ins.then_inc(s["exp_done"], 1)
        act.wait_ge(s["probsT_in_psum"], g + 1)
        act.activation(t.PT[0:KL, :], m.TP[0][0:KL, :], ACT.Copy).then_inc(s["probsT_ready"], 1)
        act.wait_ge(s["oT_in_psum"], g + 1)
        act.activation(t.oT, m.PJ[1][:, :], ACT.Copy).then_inc(s["oT_ready"], 1)

    for_groups(act, group)


def cross1_vector(v, m):
    s, t = m.x1, x1_tiles(m)
    v.wait_ge(m.rstd_ready, 5)

    def tokens(g):
        need(v, s["xT_in_psum"], g)
        for i in range(GRP):
            ins = normalise(v, m, GRP * g + i, t.xn[:, i * D:(i + 1) * D])
        ins.then_inc(s["xn_ready"], 1)

    def group(g):
        v.wait_ge(s["scores_ready"], g + 1)
        v.tensor_reduce(t.mx, m.S[0][:, 0:GRP * KL].rearrange("p (i k) -> p i k", i=GRP), AX.X, ALU.max)\
            .then_inc(s["max_done"], 1)
        v.wait_ge(s["max_done"], g + 1)
        v.tensor_scalar(t.negmax, t.mx, -D ** -0.5, None, ALU.mult).then_inc(s["negmax_ready"], 1)
        if not (isinstance(g, int) and g == NG - 1):
            tokens(g + 1)
        v.wait_ge(s["exp_done"], g + 1)
        v.reciprocal(t.inverse, t.total).then_inc(s["inv_done"], 1)
        v.wait_ge(s["inv_done"], g + 1)
        v.wait_ge(s["av_done"], g + 1)
        v.tensor_tensor(t.o.rearrange("p (i d) -> p i d", i=GRP), m.OV[:, :].rearrange("p (i d) -> p i d", i=GRP),
                        t.inverse.unsqueeze(2).to_broadcast([128, GRP, D]), ALU.mult).then_inc(s["o_ready"], 1)
        v.wait_ge(s["out_done"], g + 1)
        x = m.X[:, bass.ds(g * GT, GT)]
        v.tensor_tensor(x, x, m.MX[:, :], ALU.add).then_inc(s["res_done"], 1)
        v.wait_ge(s["res_done"], g + 1)
        for i in range(GRP):
            ins = v.bn_stats(m.stats[:, bass.ds(6 * (GRP * g + i), 6)], m.X[:, bass.ds((GRP * g + i) * D, D)])
        return ins

    tokens(0)
    group(0)
    with v.Fori(1, NG - 1) as g:
        group(g)
    group(NG - 1).then_inc(m.stream_ready, 1)


RT_SEMS = ["xn_ready", "xT_in_psum", "xT_ready", "xT_kept", "logits_done", "logits_ready"]


def router_tensor(pe, m, layer):
    s = m.rt
    w, E = ((m.w["Wr"], E0), (m.w["gateT"], E1))[layer]
    loaded(pe, m, ("ffn0", "ffn1")[layer])

    def group(g):
        k = g + NG * layer
        pe.wait_ge(s["xn_ready"], k + 1)
        need(pe, s["xT_ready"], k)
        for i in range(GRP):
            ins = pe.transpose(m.MX[:, i * T:(i + 1) * T], m.xn[:, i * D:(i + 1) * D], m.ident)
        ins.then_inc(s["xT_in_psum"], 1)
        pe.wait_ge(s["xT_ready"], k + 1)
        need(pe, s["logits_ready"], k)
        for i in range(GRP):
            ins = pe.matmul(m.OV[:, i * E:(i + 1) * E], m.XTs[:, i * T:(i + 1) * T], w[:, :], start=True, stop=True)
        ins.then_inc(s["logits_done"], 1)

    for_groups(pe, group)


def router_scalar(act, m, layer):
    s = m.rt

    def group(g):
        k = g + NG * layer
        act.wait_ge(s["xT_in_psum"], k + 1)
        need(act, s["logits_done"], k)
        need(act, s["xT_kept"], k)
        act.activation(m.XTs[:, :], m.MX[:, :], ACT.Copy).then_inc(s["xT_ready"], 1)

    for_groups(act, group)


def router_vector(v, m, layer):
    s = m.rt
    E = (E0, E1)[layer]
    LG = m.arena[:, 6400:6400 + B * E]
    v.wait_ge(m.rstd_ready, (2, 5)[layer] + 1)

    def group(g):
        k = g + NG * layer
        need(v, s["xT_in_psum"], k)
        for i in range(GRP):
            ins = normalise(v, m, GRP * g + i, m.xn[:, i * D:(i + 1) * D])
        ins.then_inc(s["xn_ready"], 1)
        v.wait_ge(s["xT_ready"], k + 1)
        v.tensor_copy(m.XTall[:, bass.ds(g * GT, GT)], m.XTs[:, :]).then_inc(s["xT_kept"], 1)
        v.wait_ge(s["logits_done"], k + 1)
        v.tensor_copy(LG[:, bass.ds(g * GRP * E, GRP * E)], m.OV[:, 0:GRP * E]).then_inc(s["logits_ready"], 1)

    for_groups(v, group)


def r0_tiles(m):
    t = Namespace()
    ar = m.arena
    t.H = [ar[:, 0:2048], ar[:, 2048:4096]]
    t.gateT = ar[:, 4096:4224]
    t.gate = ar[:, 4224:4352]
    t.b2sel = ar[:, 4352:6400]
    t.score = ar[:, 6400:6528]
    t.scoreT = ar[:, 7168:7296]
    t.junk, t.above, t.equal, t.rank = (ar[:, 7296 + 128 * i:7424 + 128 * i] for i in range(4))
    t.threshold, t.candidate, t.bit, t.count, t.kept, t.room = (m.small[:, i:i + 1] for i in range(6))
    t.counts = m.small[:, 6:8]
    t.row = m.small[:, 16:32]
    return t


BITS = 30


def route0_vector(v, m):
    t, s = r0_tiles(m), m.r0
    score = t.score.rearrange("p (b e) -> p b e", e=E0)
    row = t.row.unsqueeze(2).to_broadcast([128, B, E0])
    c = Chain(v, s["chain"])
    v.wait_ge(m.rt["logits_ready"], NG)
    c.step(v.tensor_reduce(t.row, score, AX.X, ALU.max))
    v.tensor_tensor(score, score, row, ALU.subtract).then_inc(s["shifted"], 1)
    v.wait_ge(s["exp_done"], 1)
    c.step(v.tensor_reduce(t.row, score, AX.X, ALU.add))
    c.step(v.reciprocal(t.row, t.row))
    v.tensor_tensor(score, score, row, ALU.mult).then_inc(s["score_ready"], 1)
    c.step(v.memset(t.threshold.bitcast(U32), 0))
    c.step(v.memset(t.bit.bitcast(U32), 1 << (BITS - 1)))
    v.wait_ge(s["scoreT_in_psum"], 1)
    c.step(v.tensor_copy(t.scoreT, m.MX[:, 0:128]))
    with v.Fori(0, BITS) as i:
        d = Chain(v, s["bits"], 4 * i)
        d.step(v.tensor_tensor(t.candidate.bitcast(U32), t.threshold.bitcast(U32), t.bit.bitcast(U32), ALU.bitwise_or))
        v.tensor_scalar(t.junk, t.scoreT, t.candidate, 0.0, ALU.is_ge, ALU.add, accum_out=t.count)\
            .then_inc(s["counted"], 1)
        d.step(v.tensor_scalar(t.bit.bitcast(U32), t.bit.bitcast(U32), 1, None, ALU.logical_shift_right))
        v.wait_ge(s["summed"], i + 1)
        d.step(v.tensor_scalar(t.kept, m.MX[:, 0:1], float(CAP), t.candidate, ALU.is_ge, ALU.mult))
        d.step(v.tensor_tensor(t.threshold, t.threshold, t.kept, ALU.max))
    c.step(v.tensor_scalar(t.above, t.scoreT, t.threshold, 0.0, ALU.is_gt, ALU.add, accum_out=t.counts[:, 0:1]))
    v.tensor_scalar(t.equal, t.scoreT, t.threshold, 0.0, ALU.is_equal, ALU.add, accum_out=t.counts[:, 1:2])\
        .then_inc(s["ties_counted"], 1)
    v.wait_ge(s["ties_summed"], 1)
    c.step(v.tensor_scalar(t.room, m.MX[:, 0:1], -1.0, float(CAP), ALU.mult, ALU.add))
    c.step(v.tensor_copy(t.count, m.MX[:, 1:2]))
    c.step(v.memset(t.junk, 1.0))
    c.step(v.tensor_tensor_scan(t.rank, t.junk, t.equal, t.count, ALU.mult, ALU.add))
    c.step(v.tensor_scalar(t.rank, t.rank, t.room, None, ALU.is_le))
    c.step(v.tensor_tensor(t.rank, t.rank, t.equal, ALU.mult))
    c.step(v.tensor_tensor(t.rank, t.rank, t.above, ALU.add))
    v.tensor_tensor(t.gateT, t.rank, t.scoreT, ALU.mult).then_inc(s["gateT_ready"], 1)
    v.wait_ge(s["gate_in_psum"], 1)
    v.tensor_copy(t.gate, m.MX[:, 0:128]).then_inc(s["gate_ready"], 1)


def route0_scalar(act, m):
    t, s = r0_tiles(m), m.r0
    act.wait_ge(s["shifted"], 1)
    act.activation(t.score, t.score, ACT.Exp).then_inc(s["exp_done"], 1)


def route0_tensor(pe, m):
    t, s = r0_tiles(m), m.r0
    pe.wait_ge(s["score_ready"], 1)
    pe.transpose(m.MX[:, 0:128], t.score, m.ident).then_inc(s["scoreT_in_psum"], 1)
    with pe.Fori(0, BITS) as i:
        pe.wait_ge(s["counted"], i + 1)
        pe.matmul(m.MX[:, 0:1], m.same_expert, t.count, start=True, stop=True).then_inc(s["summed"], 1)
    pe.wait_ge(s["ties_counted"], 1)
    pe.matmul(m.MX[:, 0:1], m.same_expert, t.counts[:, 0:1], start=True, stop=True)
    pe.matmul(m.MX[:, 1:2], m.earlier_rows, t.counts[:, 1:2], start=True, stop=True).then_inc(s["ties_summed"], 1)
    pe.wait_ge(s["gateT_ready"], 1)
    pe.transpose(m.MX[:, 0:128], t.gateT, m.ident).then_inc(s["gate_in_psum"], 1)


def route0_pool(po, m):
    t = r0_tiles(m)
    po.wait_ge(m.stream_ready, 3)
    loaded(po, m, "ffn0")
    po.tensor_tensor(t.b2sel.rearrange("p (b d) -> p b d", b=B), m.w["b2rep"][:, :].unsqueeze(1).to_broadcast([128, B, D]),
                     m.headmask.unsqueeze(2).to_broadcast([128, B, D]), ALU.mult).then_inc(m.r0["b2_ready"], 1)


def experts0_tensor(pe, m):
    t, s = r0_tiles(m), m.e0
    hidden_banks = [m.S[0], m.S[1], m.TP[0], m.TP[1]]

    def up(g, e):
        n = E0 * g + e
        for c in range(C0):
            need(pe, s["gelu_done"], C0 * n - (C0 - 1) + c)
            pe.matmul(hidden_banks[c][:, :], m.w["W1"][:, (e * C0 + c) * 128:(e * C0 + c + 1) * 128],
                      m.XTall[:, bass.ds(g * GT, GT)], start=True, stop=True).then_inc(s["up_done"], 1)

    def down(g, e):
        n = E0 * g + e
        H = t.H[e % 2]
        pe.wait_ge(s["gelu_done"], C0 * (n + 1))
        need(pe, s["add_done"], n - 1 + g)
        for i in range(GRP):
            for c in range(C0):
                ins = pe.matmul(m.PJ[e % 2][:, i * D:(i + 1) * D], H[:, c * GT + i * T:c * GT + (i + 1) * T],
                                m.w["W2"][:, (e * C0 + c) * D:(e * C0 + c + 1) * D], start=(c == 0), stop=(c == C0 - 1))
        ins.then_inc(s["down_done"], 1)

    def biases(g):
        need(pe, s["add_done"], (E0 + 1) * g)
        for i in range(GRP):
            ins = pe.matmul(m.OV[:, i * D:(i + 1) * D], t.gateT, m.b2sel_of(t, GRP * g + i), start=True, stop=True)
        ins.then_inc(s["bias_done"], 1)

    pe.wait_ge(m.rt["xT_kept"], NG)
    up(0, 0)
    pe.wait_ge(m.r0["b2_ready"], 1)

    def group(g):
        for e in range(E0):
            if e < E0 - 1:
                up(g, e + 1)
            elif not (isinstance(g, int) and g == NG - 1):
                up(g + 1, 0)
            down(g, e)
        biases(g)

    for_groups(pe, group)


def experts0_scalar(act, m):
    t, s = r0_tiles(m), m.e0
    hidden_banks = [m.S[0], m.S[1], m.TP[0], m.TP[1]]
    act.preload_act_table(ACT.Gelu)

    def group(g):
        for e in range(E0):
            n = E0 * g + e
            for c in range(C0):
                act.wait_ge(s["up_done"], C0 * n + c + 1)
                if c == 0:
                    need(act, s["down_done"], n - 1)
                act.activation(t.H[e % 2][:, c * GT:(c + 1) * GT], hidden_banks[c][:, :], ACT.Gelu,
                               bias=m.w["b1T"][:, e * C0 + c:e * C0 + c + 1]).then_inc(s["gelu_done"], 1)

    for_groups(act, group)


def experts0_vector(v, m):
    t, s = r0_tiles(m), m.e0
    v.wait_ge(m.r0["gate_ready"], 1)

    def group(g):
        for e in range(E0):
            v.wait_ge(s["down_done"], E0 * g + e + 1)
            need(v, s["add_done"], (E0 + 1) * g + e)
            for i in range(GRP):
                x = m.X[:, bass.ds((GRP * g + i) * D, D)]
                ins = v.scalar_tensor_tensor(x, m.PJ[e % 2][:, i * D:(i + 1) * D],
                                             t.gate[:, bass.ds((GRP * g + i) * E0 + e, 1)], x, ALU.mult, ALU.add)
            ins.then_inc(s["add_done"], 1)
        v.wait_ge(s["bias_done"], g + 1)
        v.wait_ge(s["add_done"], (E0 + 1) * g + E0)
        x = m.X[:, bass.ds(g * GT, GT)]
        v.tensor_tensor(x, x, m.OV[:, :], ALU.add).then_inc(s["add_done"], 1)
        v.wait_ge(s["add_done"], (E0 + 1) * (g + 1))
        for i in range(GRP):
            ins = v.bn_stats(m.stats[:, bass.ds(6 * (GRP * g + i), 6)], m.X[:, bass.ds((GRP * g + i) * D, D)])
        return ins

    group(0)
    with v.Fori(1, NG - 1) as g:
        group(g)
    group(NG - 1).then_inc(m.stream_ready, 1)


def r1_tiles(m):
    t = Namespace()
    ar = m.arena
    t.score = ar[:, 6400:6656]
    t.a, t.b, t.c, t.d = (ar[:, 6656 + 64 * i:6720 + 64 * i] for i in range(4))
    t.pair, t.tie = ar[:, 6912:7168], ar[:, 7168:7424]
    t.padded = ar[:, 7424:7808]
    t.marked = ar[:, 7808:8192]
    t.top = ar[:, 8192:8320]
    t.combine = ar[:, 8320:8576]
    t.row = m.small[:, 0:16]
    t.G = [ar[:, 0:1152], ar[:, 1152:2304]]
    t.Hn = [ar[:, 2304:3456], ar[:, 3456:4608]]
    t.HT = [ar[:, 8704:9856], ar[:, 9856:11008]]
    t.xT = [m.XTs[:, 0:T], m.XTs[:, T:2 * T]]
    return t


def route1_vector(v, m):
    t, s = r1_tiles(m), m.r1
    c = Chain(v, s["chain"])
    v.wait_ge(s["score_ready"], 1)
    ex = t.score.rearrange("p (g e) -> p e g", e=4)
    c.step(v.tensor_tensor(t.a, ex[:, 0], ex[:, 1], ALU.max))
    c.step(v.tensor_tensor(t.b, ex[:, 0], ex[:, 1], ALU.min))
    c.step(v.tensor_tensor(t.c, ex[:, 2], ex[:, 3], ALU.max))
    c.step(v.tensor_tensor(t.d, ex[:, 2], ex[:, 3], ALU.min))
    c.step(v.tensor_tensor(t.b, t.b, t.d, ALU.max))
    c.step(v.tensor_tensor(t.d, t.a, t.c, ALU.min))
    c.step(v.tensor_tensor(t.b, t.b, t.d, ALU.max))
    c.step(v.tensor_tensor(t.a, t.a, t.c, ALU.max))
    c.step(v.tensor_tensor(t.a, t.a, t.b, ALU.add))
    other = t.a.rearrange("p (b o) -> p b o", o=G1).unsqueeze(2).to_broadcast([128, B, G1, G1])
    own = t.a.rearrange("p (b o) -> p b o", o=G1).unsqueeze(3).to_broadcast([128, B, G1, G1])
    pair = t.pair.rearrange("p (b g o) -> p b g o", g=G1, o=G1)
    tie = t.tie.rearrange("p (b g o) -> p b g o", g=G1, o=G1)
    c.step(v.tensor_tensor(pair, other, own, ALU.is_gt))
    c.step(v.tensor_tensor(tie, other, own, ALU.is_equal))
    c.step(v.tensor_tensor(t.tie, t.tie, m.earlier_group, ALU.mult))
    c.step(v.tensor_tensor(t.pair, t.pair, t.tie, ALU.add))
    c.step(v.tensor_reduce(t.b, t.pair.rearrange("p (g o) -> p g o", o=G1), AX.X, ALU.add))
    c.step(v.tensor_scalar(t.b, t.b, float(TOPG), 4.0, ALU.is_lt, ALU.mult))
    c.step(v.tensor_scalar(t.b, t.b, -4.0, None, ALU.add))
    padded = t.padded.rearrange("p (b e) -> p b e", e=24)
    marked = t.marked.rearrange("p (b e) -> p b e", e=24)
    score = t.score.rearrange("p (b e) -> p b e", e=E1)
    c.step(v.memset(t.padded, -9.0))
    c.step(v.tensor_copy(marked[:, :, 0:E1].rearrange("p b (g e) -> p b g e", e=4),
                         t.b.rearrange("p (b g) -> p b g", g=G1).unsqueeze(3).to_broadcast([128, B, G1, 4])))
    c.step(v.tensor_tensor(padded[:, :, 0:E1], score, marked[:, :, 0:E1], ALU.add))
    for b in range(B):
        ins = v.max(t.top[:, 8 * b:8 * b + 8], t.padded[:, 24 * b:24 * b + 24])
    c.step(ins)
    c.step(v.memset(t.top.rearrange("p (b e) -> p b e", e=8)[:, :, TOPK:8], -9.0))
    for b in range(B):
        ins = v.match_replace(t.marked[:, 24 * b:24 * b + 24], t.top[:, 8 * b:8 * b + 8],
                              t.padded[:, 24 * b:24 * b + 24], -16.0)
    c.step(ins)
    combine = t.combine.rearrange("p (b e) -> p b e", e=E1)
    row = t.row.unsqueeze(2).to_broadcast([128, B, E1])
    c.step(v.tensor_scalar(combine, marked[:, :, 0:E1], -16.0, None, ALU.is_equal))
    c.step(v.tensor_tensor(t.combine, t.combine, t.score, ALU.mult))
    c.step(v.tensor_reduce(t.row, combine, AX.X, ALU.add))
    c.step(v.tensor_scalar(t.row, t.row, 1e-6, None, ALU.add))
    c.step(v.reciprocal(t.row, t.row))
    v.tensor_tensor(combine, combine, row, ALU.mult).then_inc(s["combine_ready"], 1)


def route1_scalar(act, m):
    t = r1_tiles(m)
    act.wait_ge(m.rt["logits_ready"], 2 * NG)
    act.activation(t.score, t.score, ACT.Sigmoid).then_inc(m.r1["score_ready"], 1)


def experts1_tensor(pe, m):
    t, s = r1_tiles(m), m.e1
    gate_banks, up_banks = [m.S[0], m.S[1], m.MX[:, 0:128]], [m.TP[0], m.TP[1], m.MX[:, 128:256]]

    def up(b, p):
        pe.wait_ge(s["xT_ready"], b + 1)
        for i in range(3):
            width = 512 if i < 2 else 128
            for banks, w, read, done in ((gate_banks, m.w["w1T"], s["silu_done"], s["gate_done"]), (up_banks, m.w["w3T"], s["mul_done"], s["up_done"])):
                need(pe, read, 3 * (b - 1) + i + 1)
                if i == 2:
                    need(pe, s["mul_done"], 3 * b)
                pe.matmul(banks[i][:, 0:width], t.xT[p], w[:, 512 * i:512 * i + width], start=True, stop=True)\
                    .then_inc(done, 1)

    def transpose_hidden(b, p, part):
        pe.wait_ge(s["gated"], b + 1)
        bank = m.PJ[part % 2]
        if part == 0:
            need(pe, s["hT_act"], 2 * b)
        elif part == 1:
            need(pe, s["hT_dve"], b)
        else:
            pe.wait_ge(s["hT_act"], 2 * b + 1)
        chunks = range(4 * part, min(4 * part + 4, FC))
        for i, c in enumerate(chunks):
            ins = pe.transpose(bank[:, i * T:(i + 1) * T], t.Hn[p][:, c * 128:(c + 1) * 128], m.ident)
        ins.then_inc(s["hT_in_psum"], 1)

    def down(b, p):
        pe.wait_ge(s["hT_act"], 2 * (b + 1))
        pe.wait_ge(s["hT_dve"], b + 1)
        need(pe, s["res_done"], b)
        for c in range(FC):
            ins = pe.matmul(m.OV[:, 0:D], t.HT[p][:, c * T:(c + 1) * T], m.w["w2T"][:, c * D:(c + 1) * D],
                            start=(c == 0), stop=(c == FC - 1))
        ins.then_inc(s["down_done"], 1)

    def slots(b, p):
        up(b, p)
        if not known_first(b):
            transpose_hidden(b - 1, 1 - p, 0)
            transpose_hidden(b - 1, 1 - p, 1)
        if not (isinstance(b, int) and b < 2):
            down(b - 2, p)
        if not known_first(b):
            transpose_hidden(b - 1, 1 - p, 2)

    for_batches(pe, slots)
    transpose_hidden(B - 1, 1, 0)
    transpose_hidden(B - 1, 1, 1)
    down(B - 2, 0)
    transpose_hidden(B - 1, 1, 2)
    down(B - 1, 1)


def experts1_scalar(act, m):
    t, s = r1_tiles(m), m.e1
    gate_banks = [m.S[0], m.S[1], m.MX[:, 0:128]]
    act.preload_act_table(ACT.Silu)
    act.wait_ge(m.rt["xT_kept"], 2 * NG)

    def take_x(b, p):
        need(act, s["up_done"], 3 * (b - 1))
        act.activation(t.xT[p], m.XTall[:, bass.ds(b * T, T)], ACT.Copy).then_inc(s["xT_ready"], 1)

    def take_hT(b, p, part):
        act.wait_ge(s["hT_in_psum"], 3 * b + part + 1)
        need(act, s["down_done"], b - 1)
        n = 4 if part == 0 else 1
        act.activation(t.HT[p][:, 4 * part * T:(4 * part + n) * T], m.PJ[0][:, 0:n * T], ACT.Copy)\
            .then_inc(s["hT_act"], 1)

    take_x(0, 0)

    def slots(b, p):
        if not known_last(b):
            take_x(b + 1, 1 - p)
        for i in range(3):
            width = 512 if i < 2 else 128
            act.wait_ge(s["gate_done"], 3 * b + i + 1)
            if i == 2:
                act.wait_ge(s["up_done"], 3 * (b + 1))
            if i == 0:
                need(act, s["mul_done"], 3 * (b - 1))
            act.activation(t.G[p][:, 512 * i:512 * i + width], gate_banks[i][:, 0:width], ACT.Silu)\
                .then_inc(s["silu_done"], 1)
        if not known_first(b):
            take_hT(b - 1, 1 - p, 0)
            take_hT(b - 1, 1 - p, 2)

    for_batches(act, slots)
    take_hT(B - 1, 1, 0)
    take_hT(B - 1, 1, 2)


def experts1_vector(v, m):
    t, s = r1_tiles(m), m.e1
    up_banks = [m.TP[0], m.TP[1], m.MX[:, 128:256]]

    def take_hT(b, p):
        v.wait_ge(s["hT_in_psum"], 3 * b + 2)
        need(v, s["down_done"], b - 1)
        v.tensor_copy(t.HT[p][:, 4 * T:8 * T], m.PJ[1][:, :]).then_inc(s["hT_dve"], 1)

    def take_output(b):
        v.wait_ge(s["down_done"], b + 1)
        x = m.X[:, bass.ds(b * D, D)]
        v.tensor_tensor(x, x, m.OV[:, 0:D], ALU.add).then_inc(s["res_done"], 1)

    def slots(b, p):
        for i in range(3):
            width = 512 if i < 2 else 128
            v.wait_ge(s["up_done"], 3 * b + i + 1)
            v.wait_ge(s["silu_done"], 3 * b + i + 1)
            if i == 0:
                need(v, s["hT_in_psum"], 3 * (b - 1))
            cols = slice(512 * i, 512 * i + width)
            v.tensor_tensor(t.Hn[p][:, cols], t.G[p][:, cols], up_banks[i][:, 0:width], ALU.mult)\
                .then_inc(s["mul_done"], 1)
        if not known_first(b):
            take_hT(b - 1, 1 - p)
        if not (isinstance(b, int) and b < 2):
            take_output(b - 2)

    for_batches(v, slots)
    take_hT(B - 1, 1)
    take_output(B - 2)
    take_output(B - 1)


def experts1_pool(po, m):
    t, s = r1_tiles(m), m.e1
    po.wait_ge(m.r1["combine_ready"], 1)

    def gate(b, p):
        po.wait_ge(s["mul_done"], 3 * (b + 1))
        h = t.Hn[p][:, 0:E1 * F1].rearrange("p (e f) -> p e f", e=E1)
        w = t.combine[:, bass.ds(b * E1, E1)].unsqueeze(2).to_broadcast([128, E1, F1])
        po.tensor_tensor(h, h, w, ALU.mult).then_inc(s["gated"], 1)

    for_batches(po, gate)


def program(nc, a, out, scratch, layers=6):
    with ExitStack() as ctx:
        def sb(name, shape, dt=F32):
            return ctx.enter_context(nc.sbuf_tensor(name, shape, dt))

        def ps(name):
            return ctx.enter_context(nc.psum_tensor(name, [128, 512], F32))

        def sem(name):
            return ctx.enter_context(nc.semaphore(name))

        def sems(prefix, names):
            return {n: sem(f"{prefix}_{n}") for n in names}

        m = Namespace()
        m.w = {name: sb(name, shape) for name, shape in WEIGHTS.items()}
        m.X = sb("X", [128, N])
        m.stats = sb("stats", [128, B * 6])
        m.mean, m.rstd, m.st1, m.st2 = (sb(n, [128, B]) for n in ("mean", "rstd", "st1", "st2"))
        m.xn = sb("xn", [128, 512])
        m.XTs = sb("XTs", [128, 512])
        m.small = sb("small", [128, 96])
        m.arena = sb("arena", [128, 17408])
        m.XTall = m.arena[:, 11264:11264 + N]
        m.consts = sb("consts", [128, 3 * 128 + 2 * 16 + 256])
        m.ident, m.same_expert, m.earlier_rows = (m.consts[:, 128 * i:128 * i + 128] for i in range(3))
        m.headmask, m.minus_half = m.consts[:, 384:400], m.consts[:, 400:416]
        m.earlier_group = m.consts[:, 416:672]
        m.identb = sb("identb", [128, 128], BF16)
        m.ones = sb("ones", [1, 128])
        m.mask8 = sb("mask8", [128, B * KL], U8)
        m.maskb = sb("maskb", [128, B * KL], BF16)
        m.KT0, m.KT1 = sb("KT0", [128, B * KL]), sb("KT1", [128, B * KL])
        m.V01 = sb("V01", [KL, B * 2 * D])

        m.S, m.TP, m.PJ = ([ps(f"{n}{i}") for i in range(2)] for n in ("S", "TP", "PJ"))
        m.OV, m.MX = ps("OV"), ps("MX")

        m.ld = {n: sem(f"ld_{n}") for n in LOADED}
        m.const_ready, m.stream_ready, m.var_ready, m.rstd_ready = (
            sem(n) for n in ("const_ready", "stream_ready", "var_ready", "rstd_ready"))
        m.moment_chain = sem("moment_chain")
        m.att = [sems(f"att{i}", ATT_SEMS) for i in range(2)]
        m.att_w = [m.w["wqkv"][:, H * HD * i:H * HD * (i + 1)] for i in range(3)] + [m.w["w_o"]]
        m.att_k = [0, 3]
        m.v_save, m.v_load = ([sem(f"v_{n}{p}") for p in range(2)] for n in ("save", "load"))
        m.k0_made, m.k0_taken, m.k1_made, m.k1_taken, m.v01_made, m.v01_taken, m.mask_ready, m.zeroed = (
            sem(n) for n in ("k0_made", "k0_taken", "k1_made", "k1_taken", "v01_made", "v01_taken", "mask_ready",
                             "zeroed"))
        m.cr = sems("cr", CR_SEMS)
        m.x1 = sems("x1", X1_SEMS)
        m.rt = sems("rt", RT_SEMS)
        m.r0 = sems("r0", ["chain", "bits", "shifted", "exp_done", "score_ready", "scoreT_in_psum", "counted", "summed",
                           "ties_counted", "ties_summed", "gateT_ready", "gate_in_psum", "gate_ready", "b2_ready"])
        m.e0 = sems("e0", ["up_done", "gelu_done", "down_done", "add_done", "bias_done"])
        m.r1 = sems("r1", ["chain", "score_ready", "combine_ready"])
        m.e1 = sems("e1", ["xT_ready", "gate_done", "up_done", "silu_done", "mul_done", "gated", "hT_in_psum",
                           "hT_act", "hT_dve", "down_done", "res_done"])
        m.b2sel_of = lambda t, b: t.b2sel[:, bass.ds(b * D, D)]
        out_saved = sem("out_saved")

        block = ctx.enter_context(nc.Block())

        @block.sync
        def _(sp):
            loads_sync(sp, m, a)
            att_sync(sp, m, scratch)
            if layers < 6:
                sp.wait_ge(m.stream_ready, layers + 1)
            for g in range(NG):
                if layers == 6:
                    sp.wait_ge(m.e1["res_done"], GRP * (g + 1))
                sp.dma_start(out[:, g * GT:(g + 1) * GT], m.X[:, g * GT:(g + 1) * GT]).then_inc(out_saved, 16)
            sp.wait_ge(out_saved, 16 * NG)

        @block.gpsimd
        def _(po):
            loads_pool(po, m, a)
            moments_pool(po, m, 0)
            att_pool(po, m, 0)
            if layers >= 2:
                attention1_loads_pool(po, m, a)
                moments_pool(po, m, 1)
                cross0_pool(po, m)
            if layers >= 3:
                moments_pool(po, m, 2)
                route0_pool(po, m)
            if layers >= 4:
                moments_pool(po, m, 3)
                att_pool(po, m, 1)
            if layers >= 5:
                moments_pool(po, m, 4)
            if layers >= 6:
                moments_pool(po, m, 5)
                experts1_pool(po, m)

        @block.scalar
        def _(act):
            att_scalar(act, m, 0)
            if layers >= 2:
                context_scalar(act, m)
                cross0_scalar(act, m)
            if layers >= 3:
                router_scalar(act, m, 0)
                route0_scalar(act, m)
                experts0_scalar(act, m)
            if layers >= 4:
                att_scalar(act, m, 1)
            if layers >= 5:
                cross1_scalar(act, m)
            if layers >= 6:
                router_scalar(act, m, 1)
                route1_scalar(act, m)
                experts1_scalar(act, m)

        @block.vector
        def _(v):
            setup_vector(v, m)
            moments_vector(v, m, 0)
            att_vector(v, m, 0)
            if layers >= 2:
                moments_vector(v, m, 1)
                context_vector(v, m)
                cross0_vector(v, m)
            if layers >= 3:
                moments_vector(v, m, 2)
                router_vector(v, m, 0)
                route0_vector(v, m)
                experts0_vector(v, m)
            if layers >= 4:
                moments_vector(v, m, 3)
                att_vector(v, m, 1)
            if layers >= 5:
                moments_vector(v, m, 4)
                cross1_vector(v, m)
            if layers >= 6:
                moments_vector(v, m, 5)
                router_vector(v, m, 1)
                route1_vector(v, m)
                experts1_vector(v, m)

        @block.tensor
        def _(pe):
            att_tensor(pe, m, 0)
            if layers >= 2:
                context_tensor(pe, m)
                cross0_tensor(pe, m)
            if layers >= 3:
                router_tensor(pe, m, 0)
                route0_tensor(pe, m)
                experts0_tensor(pe, m)
            if layers >= 4:
                att_tensor(pe, m, 1)
            if layers >= 5:
                cross1_tensor(pe, m)
            if layers >= 6:
                router_tensor(pe, m, 1)
                experts1_tensor(pe, m)


WEIGHTS = {
    "wqkv": [128, 3 * H * HD], "w_o": [128, H * HD],
    "ctxT": [128, B * KL], "x0Wk": [128, D], "x1WkT": [128, D], "WvBoth": [128, 2 * D], "x0bk": [128, 1],
    "bvBoth": [128, 2 * D], "x0Wq": [128, D], "x0Wo": [128, D], "x0bq": [128, 1], "x0bo": [1, D],
    "Wr": [128, E0], "W1": [128, E0 * F0], "W2": [128, E0 * F0], "b1T": [128, E0 * C0], "b2rep": [128, D],
    "x1WqT": [128, D], "x1WoT": [128, D], "x1bq": [128, 1], "x1bo": [1, D],
    "gateT": [128, E1], "w1T": [128, FC * 128], "w3T": [128, FC * 128], "w2T": [128, FC * 128],
}


def kernel(**inputs):
    import numpy as np
    import concourse.bacc as bacc
    from concourse.bass_utils import run_bass_kernel_spmd

    i = {k: np.asarray(x) for k, x in inputs.items()}

    def tall(w):
        return w.reshape(-1, 128, w.shape[-1]).transpose(1, 0, 2).reshape(128, -1)

    w1 = np.concatenate([i["L1_ffn_w1_e"].reshape(E1 * F1, D), i["L1_ffn_w1_s"]])
    w3 = np.concatenate([i["L1_ffn_w3_e"].reshape(E1 * F1, D), i["L1_ffn_w3_s"]])
    w2 = np.concatenate([i["L1_ffn_w2_e"].transpose(0, 2, 1).reshape(E1 * F1, D), i["L1_ffn_w2_s"].T])
    r, c = np.arange(128)[:, None], np.arange(128)[None, :]
    same = (r % E0 == c % E0).astype(np.float32)
    earlier = ((r % E0 == c % E0) & (r // E0 < c // E0)).astype(np.float32)
    heads = (r // XHD == np.arange(H)[None, :]).astype(np.float32)
    groups = np.tile((np.arange(G1)[:, None] > np.arange(G1)[None, :]).astype(np.float32).reshape(1, -1), (128, B))
    consts = np.concatenate([np.eye(128, dtype=np.float32), same, earlier, heads,
                             np.full((128, 16), -0.5, np.float32), groups], axis=1)
    a = {
        "x": i["x"].transpose(1, 0, 2).reshape(T, N), "consts": consts,
        "wqT": i["L0_attn_wq"].T, "wkT": i["L0_attn_wk"].T, "wvT": i["L0_attn_wv"].T, "woT": tall(i["L0_attn_wo"].T),
        "ctxT": i["ctx_1024"].transpose(2, 0, 1).reshape(D, B * KL),
        "mask": i["mask_Bx1xSxS2_bk1"][:, 0].transpose(1, 0, 2).reshape(T, B * KL),
        "x0Wk": i["L0_xattn_Wk"], "x1WkT": i["L1_xattn_Wk"].T,
        "WvBoth": np.concatenate([i["L0_xattn_Wv"], i["L1_xattn_Wv"].T], axis=1),
        "x0bk": i["L0_xattn_bk"][:, None],
        "bvBoth": np.tile(np.concatenate([i["L0_xattn_bv"], i["L1_xattn_bv"]])[None, :], (128, 1)),
        "x0Wq": i["L0_xattn_Wq"], "x0Wo": i["L0_xattn_Wo"], "x0bq": i["L0_xattn_bq"][:, None],
        "x0bo": i["L0_xattn_bo"][None, :],
        "Wr": i["L0_ffn_Wr"], "W1": i["L0_ffn_W1"].transpose(1, 0, 2).reshape(D, E0 * F0),
        "W2": tall(i["L0_ffn_W2"].reshape(E0 * F0, D)), "b1T": i["L0_ffn_b1"].reshape(E0 * C0, 128).T,
        "b2rep": np.tile(i["L0_ffn_b2"], (B, 1)),
        "wqkv": i["L1_attn_w_qkv"].transpose(2, 1, 0, 3).reshape(D, 3 * H * HD), "w_o": tall(i["L1_attn_w_o"]),
        "x1WqT": i["L1_xattn_Wq"].T, "x1WoT": i["L1_xattn_Wo"].T, "x1bq": i["L1_xattn_bq"][:, None],
        "x1bo": i["L1_xattn_bo"][None, :],
        "gateT": i["L1_ffn_w_gate"].T, "w1T": w1.T, "w3T": w3.T, "w2T": tall(w2),
    }
    nc = bacc.Bacc("TRN2", target_bir_lowering=False, num_devices=1)
    arrays, aps = {}, {}
    for name, x in a.items():
        x = np.ascontiguousarray(x)
        arrays[f"in_{name}"] = x
        aps[name] = nc.dram_tensor(f"in_{name}", x.shape, mybir.dt.from_np(x.dtype), kind="ExternalInput").ap()
    out = nc.dram_tensor("out", (T, N), F32, kind="ExternalOutput").ap()
    scratch = [nc.dram_tensor(f"v_scratch{p}", (T, H * HD), F32, kind="Internal").ap() for p in range(2)]
    program(nc, aps, out, scratch)
    result = run_bass_kernel_spmd(nc, [arrays], core_ids=[0]).results[0]["out"]
    return np.ascontiguousarray(result.reshape(T, B, D).transpose(1, 0, 2))
```

```python
from contextlib import ExitStack

import concourse.bass as bass
from concourse import mybir

F32 = mybir.dt.float32
F32R = mybir.dt.float32r
BF16 = mybir.dt.bfloat16
U8 = mybir.dt.uint8
U32 = mybir.dt.uint32
ALU = mybir.AluOpType
ACT = mybir.ActivationFunctionType
AX = mybir.AxisListType

B = 16
T = 128
D = 128
KL = 120
N = B * T
H = 16
HD = 64
U = 4
HU = H // U
XHD = D // H
E0, F0, CAP = 8, 512, 512
C0 = F0 // 128
E1, F1 = 16, 64
G1, TOPG, TOPK = 4, 2, 4
FC = E1 * F1 // 128 + 1
EPS = 1e-5
GRP = 4
NG = B // GRP
GT = GRP * T
MASKED = -1.0e15


def need(eng, sem, value):
    if isinstance(value, int) and value <= 0:
        return
    eng.wait_ge(sem, value)


class Chain:

    def __init__(self, eng, sem, base=0):
        self.eng, self.sem, self.base, self.n = eng, sem, base, 0

    def step(self, ins):
        ins.then_inc(self.sem, 1)
        self.n += 1
        self.eng.wait_ge(self.sem, self.base + self.n)


def for_batches(eng, body):
    body(0, 0)
    body(1, 1)
    with eng.Fori(0, (B - 4) // 2) as i:
        body(2 * i + 2, 0)
        body(2 * i + 3, 1)
    body(B - 2, 0)
    body(B - 1, 1)


def for_groups(eng, body):
    body(0)
    with eng.Fori(1, NG - 1) as g:
        body(g)
    body(NG - 1)


def split_product(pe, out, lhsT, rhs, start=True, stop=True):
    pe.matmul(out, lhsT[1], rhs[0], start=start, stop=False)
    pe.matmul(out, lhsT[0], rhs[1], start=False, stop=False)
    return pe.matmul(out, lhsT[0], rhs[0], start=False, stop=stop)


class Namespace:
    pass


def known_first(b):
    return isinstance(b, int) and b == 0


def known_last(b):
    return isinstance(b, int) and b == B - 1




def loads_sync(sp, m, a):
    sp.dma_start(m.X[:, :], a["x"]).then_inc(m.ld["x"], 16)
    sp.dma_start(m.consts[:, :], a["consts"]).then_inc(m.ld["consts"], 16)
    sp.dma_start(m.att_w[0], a["wqT"]).then_inc(m.ld["wqkT"], 16)
    sp.dma_start(m.att_w[1], a["wkT"]).then_inc(m.ld["wqkT"], 16)
    sp.dma_start(m.wv, a["wvT"]).then_inc(m.ld["wvT"], 16)
    sp.dma_start(m.w["w_o"][:, :], a["woT"]).then_inc(m.ld["woT"], 16)


def loads_pool(po, m, a):
    for tile, name in ((m.w["ctxT"], "ctxT"), (m.mask8, "mask")):
        po.dma_start(tile[:, :], a[name]).then_inc(m.ld["ctxT"], 16)
    for tile, name in ((m.w["x0Wk"], "x0Wk"), (m.w["x1WkT"], "x1WkT"), (m.w["WvBoth"], "WvBoth"), (m.w["x0bk"], "x0bk"),
                       (m.w["bvBoth"], "bvBoth")):
        po.dma_start(tile[:, :], a[name]).then_inc(m.ld["xkv"], 16)
    for tile, name in ((m.w["x0Wq"], "x0Wq"), (m.w["x0Wo"], "x0Wo"), (m.w["x0bq"], "x0bq"), (m.w["x0bo"], "x0bo")):
        po.dma_start(tile[:, :], a[name]).then_inc(m.ld["x0"], 16)
    for tile, name in ((m.w["Wr"], "Wr"), (m.w["W1"], "W1"), (m.w["W2"], "W2"), (m.w["b1T"], "b1T"), (m.w["b2rep"], "b2rep")):
        po.dma_start(tile[:, :], a[name]).then_inc(m.ld["ffn0"], 16)
    for tile, name in ((m.w["x1WqT"], "x1WqT"), (m.w["x1WoT"], "x1WoT"), (m.w["x1bq"], "x1bq"), (m.w["x1bo"], "x1bo")):
        po.dma_start(tile[:, :], a[name]).then_inc(m.ld["x1"], 16)
    po.dma_start(m.w["gateT"][:, :], a["gateT"]).then_inc(m.ld["ffn1"], 16)


def attention1_loads_pool(po, m, a):
    po.wait_ge(m.stream_ready, 2)
    for tile, name in ((m.w["wqkv"], "wqkv"), (m.w["w_o"], "w_o")):
        po.dma_start(tile[:, :], a[name]).then_inc(m.ld["attn1"], 16)


def experts1_loads_pool(po, m, a):
    po.wait_ge(m.stream_ready, 4)
    for tile, name in ((m.w1T, "w1T"), (m.w3T, "w3T"), (m.w2T, "w2T")):
        po.dma_start(tile, a[name]).then_inc(m.ld["ffn1"], 16)


ATT_PIECES, W1_PIECES, FFN1_PIECES = 2, B, 6
ATT_SPLIT = [0, ATT_PIECES + W1_PIECES]
W1_SPLIT, FFN1_SPLIT = ATT_PIECES, 2 * ATT_PIECES + W1_PIECES


def split_attention1_pool(po, m):
    loaded(po, m, "attn1")
    for i in range(ATT_PIECES):
        cols = slice(512 * i, 512 * i + 512)
        split_high(po, m, m.wv[:, cols], m.wv_hi[:, cols])
        po.wait_ge(m.split_hi, ATT_SPLIT[1] + i + 1)
        split_low(po, m, m.wv[:, cols], m.wv_hi[:, cols], m.wv_lo[:, cols])


def split_high(po, m, w, high):
    po.tensor_copy(high, w).then_inc(m.split_hi, 1)


def split_low(po, m, w, high, low):
    po.tensor_tensor(low, w, high, ALU.subtract).then_inc(m.split_lo, 1)


def split_experts1_pool(po, m):
    loaded(po, m, "ffn1")
    width = 2 * FC * 128 // FFN1_PIECES
    for i in range(FFN1_PIECES):
        cols = slice(width * i, width * (i + 1))
        split_high(po, m, m.w["W1"][:, cols], m.w13hi[:, cols])
        po.wait_ge(m.split_hi, FFN1_SPLIT + i + 1)
        split_low(po, m, m.w["W1"][:, cols], m.w13hi[:, cols], m.W1lo[:, cols])


LOADED = {"x": 16, "consts": 16, "wqkT": 32, "wvT": 16, "woT": 16, "ctxT": 32, "xkv": 80, "x0": 64,
          "ffn0": 80, "attn1": 32, "x1": 64, "ffn1": 64}


def loaded(eng, m, name):
    eng.wait_ge(m.ld[name], LOADED[name])


def setup_vector(v, m):
    loaded(v, m, "consts")
    v.tensor_copy(m.identb[:, :], m.ident).then_inc(m.const_ready, 1)
    v.memset(m.ones[:, :], 1.0).then_inc(m.const_ready, 1)
    loaded(v, m, "x")
    for b in range(B):
        ins = v.bn_stats(m.stats[:, 6 * b:6 * b + 6], m.X[:, b * D:(b + 1) * D])
    ins.then_inc(m.stream_ready, 1)


def moments_vector(v, m, k):
    c = Chain(v, m.moment_chain, 6 * k)
    v.wait_ge(m.stream_ready, k + 1)
    st = m.stats[:, :].rearrange("p (b s) -> p s b", s=6)
    c.step(v.tensor_tensor(m.mean[:, :], st[:, 1], st[:, 4], ALU.add))
    c.step(v.tensor_tensor(m.st1[:, :], st[:, 1], st[:, 4], ALU.subtract))
    c.step(v.tensor_tensor(m.st2[:, :], st[:, 2], st[:, 5], ALU.add))
    c.step(v.tensor_scalar(m.mean[:, :], m.mean[:, :], 0.5, None, ALU.mult))
    c.step(v.tensor_tensor(m.st1[:, :], m.st1[:, :], m.st1[:, :], ALU.mult))
    c.step(v.tensor_scalar(m.st2[:, :], m.st2[:, :], 1.0 / D, EPS, ALU.mult, ALU.add))
    v.scalar_tensor_tensor(m.st2[:, :], m.st1[:, :], 0.25, m.st2[:, :], ALU.mult, ALU.add).then_inc(m.var_ready, 1)


def moments_pool(po, m, k):
    po.wait_ge(m.var_ready, k + 1)
    if k == 0:
        loaded(po, m, "consts")
    po.tensor_tensor(m.rstd[:, :], m.st2[:, :], m.minus_half, ALU.pow).then_inc(m.rstd_ready, 1)


def normalise(v, m, b, dst):
    return v.tensor_scalar(dst, m.X[:, bass.ds(b * D, D)], m.mean[:, bass.ds(b, 1)], m.rstd[:, bass.ds(b, 1)],
                           ALU.subtract, ALU.mult)


ATT_SEMS = ["xn_ready", "xT_in_psum", "xT_ready", "xTv_ready", "q_proj", "k_proj", "v_proj", "q_ready", "k_ready", "v_evac",
            "scores_ready", "negmax_ready", "exp_done", "inverse_ready", "probs_ready", "probsT_in_psum",
            "probsT_ready", "av_done", "av_evac", "out_done", "res_done"]


def att_tiles(m):
    t = Namespace()
    ar = m.arena
    t.Q = [ar[:, 0:2048], ar[:, 2048:4096]]
    t.K = [ar[:, 4096:6144], ar[:, 6144:8192]]
    t.V = [ar[:, 8192:9216], ar[:, 9216:10240]]
    t.Vst = [ar[:, 10240:11264], ar[:, 11264:12288]]
    t.P = [ar[:, 12288 + 512 * i:12800 + 512 * i] for i in range(U)]
    t.PT = [ar[:, 14336 + 512 * i:14848 + 512 * i] for i in range(2)]
    t.OT = [ar[:, 15360 + 1024 * i:16384 + 1024 * i] for i in range(2)]
    t.negmax = [m.small[:, 4 * u:4 * u + 4] for u in range(U)]
    t.total = [m.small[:, 16 + 4 * u:20 + 4 * u] for u in range(U)]
    t.inverse = [m.small[:, 32 + 4 * u:36 + 4 * u] for u in range(U)]
    t.xn = [m.xn[:, 0:D], m.xn[:, D:2 * D]]
    t.xT = [m.XTs[:, 0:T], m.XTs[:, T:2 * T]]
    t.xTv = [(m.XTv[:, i * T:(i + 1) * T], m.XTv[:, (2 + i) * T:(3 + i) * T]) for i in range(2)]
    return t


PIECES = {0: [("q", 0), ("q", 1)], 1: [("k", 0)], 2: [("k", 1), ("v", 0)], 3: [("v", 1)]}


def att_tensor(pe, m, layer):
    s, t = m.att[layer], att_tiles(m)
    wq, wk = m.att_w

    def transpose_tokens(b, p):
        pe.wait_ge(s["xn_ready"], b + 1)
        need(pe, s["res_done"], b - 3)
        need(pe, s["xTv_ready"], b)
        pe.transpose(m.MX[:, 0:T], t.xn[p], m.ident).then_inc(s["xT_in_psum"], 1)

    def project(b, p, kind, g):
        bank = m.PJ[g]
        if kind == "q":
            if g == 0:
                pe.wait_ge(s["xT_ready"], b + 1)
            need(pe, s["v_evac"], 2 * b - 1 + g)
        elif kind == "k":
            pe.wait_ge(s["q_ready"], 2 * b + 1 + g)
        else:
            pe.wait_ge(s["k_ready"], 2 * b + 1 + g)
        if kind == "v":
            if known_first(b):
                pe.wait_ge(m.split_lo, ATT_SPLIT[layer] + 1 + g)
            pe.wait_ge(s["xTv_ready"], b + 1)
            cols = slice(512 * g, 512 * g + 512)
            split_product(pe, bank[:, :], t.xTv[p], (m.wv_hi[:, cols], m.wv_lo[:, cols])).then_inc(s["v_proj"], 1)
            return
        w, done = (wq, s["q_proj"]) if kind == "q" else (wk, s["k_proj"])
        for c in range(4):
            chunk = 4 * g + c
            ins = pe.matmul(bank[:, c * T:(c + 1) * T], w[:, chunk * 128:(chunk + 1) * 128], t.xT[p],
                            start=True, stop=True)
        ins.then_inc(done, 1)

    def scores(b, p, u):
        n = U * b + u
        if u == 0:
            pe.wait_ge(s["q_ready"], 2 * (b + 1))
            pe.wait_ge(s["k_ready"], 2 * (b + 1))
        need(pe, s["exp_done"], n - 1)
        bank = m.S[u % 2]
        if layer == 0:
            for j in range(HU):
                h = HU * u + j
                ins = pe.matmul(bank[:, j * 128:(j + 1) * 128], t.Q[p][0:HD, h * 128:(h + 1) * 128],
                                t.K[p][0:HD, h * 128:(h + 1) * 128], start=True, stop=True)
        else:
            for j in range(2):
                pair = 2 * u + j
                ins = pe.matmul(bank[:, j * 256:(j + 1) * 256], t.Q[p][:, pair * 128:(pair + 1) * 128],
                                t.K[p][:, pair * 256:(pair + 1) * 256], start=True, stop=True)
        ins.then_inc(s["scores_ready"], 1)

    def transpose_probs(n, u):
        pe.wait_ge(s["probs_ready"], n + 1)
        need(pe, s["probsT_ready"], n - 1)
        for j in range(HU):
            ins = pe.transpose(m.TP[u % 2][:, j * 128:(j + 1) * 128], t.P[u][:, j * 128:(j + 1) * 128], m.ident)
        ins.then_inc(s["probsT_in_psum"], 1)

    def values(b, p, u):
        n = U * b + u
        pe.wait_ge(s["probsT_ready"], n + 1)
        need(pe, s["av_evac"], n)
        if u == 0:
            if layer == 0:
                pe.wait_ge(m.v_load[p], 8 * (b - p) + 16)
            else:
                pe.wait_ge(s["v_evac"], 2 * (b + 1))
        PT, V = t.PT[u % 2], t.V[p]
        for j in range(HU):
            h = HU * u + j
            if layer == 0:
                for par in range(2):
                    ins = pe.matmul(m.OV[par * 64:par * 64 + 64, j * 64:j * 64 + 64], V[:, h * HD:(h + 1) * HD],
                                    PT[:, j * 128 + par * 64:j * 128 + par * 64 + 64], start=True, stop=True)
            else:
                par = j % 2
                ins = pe.matmul(m.OV[par * 64:par * 64 + 64, (j // 2) * 128:(j // 2) * 128 + 128],
                                V[:, h * HD:(h + 1) * HD], PT[:, j * 128:(j + 1) * 128], start=True, stop=True)
        ins.then_inc(s["av_done"], 1)

    def output(b, p):
        pe.wait_ge(s["av_evac"], U * (b + 1))
        need(pe, s["xTv_ready"], min(b + 4, B) if isinstance(b, int) else b + 4)
        need(pe, s["res_done"], b)
        for c in range(8):
            ins = pe.matmul(m.MX[:, 0:D], t.OT[p][:, c * T:(c + 1) * T], m.w["w_o"][:, c * D:(c + 1) * D],
                            start=(c == 0), stop=(c == 7))
        ins.then_inc(s["out_done"], 1)

    loaded(pe, m, "consts")
    transpose_tokens(0, 0)
    for name in (("wqkT", "woT") if layer == 0 else ("attn1",)):
        loaded(pe, m, name)
    for u in range(U):
        for kind, g in PIECES[u]:
            project(0, 0, kind, g)
    transpose_tokens(1, 1)

    def slots(b, p):
        for u in range(U):
            scores(b, p, u)
            if not known_last(b):
                for kind, g in PIECES[u]:
                    project(b + 1, 1 - p, kind, g)
            n = U * b + u
            if not (known_first(b) and u < 1):
                transpose_probs(n - 1, (u - 1) % U)
            if not (known_first(b) and u < 2):
                values(b if u >= 2 else b - 1, p if u >= 2 else 1 - p, (u - 2) % U)
            if u == 1 and not (isinstance(b, int) and b + 2 >= B):
                transpose_tokens(b + 2, p)
            if u == 2 and not known_first(b):
                output(b - 1, 1 - p)

    for_batches(pe, slots)
    transpose_probs(U * B - 1, U - 1)
    values(B - 1, 1, U - 2)
    values(B - 1, 1, U - 1)
    output(B - 1, 1)


def att_scalar(act, m, layer):
    s, t = m.att[layer], att_tiles(m)
    scale = HD ** -0.5

    def exps(b, p, u):
        n = U * b + u
        act.wait_ge(s["negmax_ready"], n + 1)
        need(act, s["probsT_in_psum"], n - 3)
        for j in range(HU):
            ins = act.activation(t.P[u][:, j * 128:(j + 1) * 128], m.S[u % 2][:, j * 128:(j + 1) * 128], ACT.Exp,
                                 bias=t.negmax[u][:, j:j + 1], accum_out=t.total[u][:, j:j + 1])
        ins.then_inc(s["exp_done"], 1)

    def take_q(b, p, g):
        act.wait_ge(s["q_proj"], 2 * b + g + 1)
        if layer == 0:
            for par in range(2):
                src = m.PJ[g][par * 64:par * 64 + 64, :].rearrange("d (c h t) -> d c h t", c=4, t=8)
                dst = t.Q[p][0:HD, :].rearrange("d (h r c t) -> d r c h t", h=H, r=2, c=8)[:, par, 4 * g:4 * g + 4]
                ins = act.activation(dst, src, ACT.Copy, scale=scale)
        else:
            ins = act.activation(t.Q[p][:, 512 * g:512 * g + 512], m.PJ[g][:, :], ACT.Copy, scale=scale)
        ins.then_inc(s["q_ready"], 1)

    def take_v(b, p, g):
        act.wait_ge(s["v_proj"], 2 * b + g + 1)
        if layer == 0:
            if not (isinstance(b, int) and b < 2):
                act.wait_ge(m.v_save[p], 8 * (b - p))
            dst = t.Vst[p]
        else:
            dst = t.V[p]
        act.activation(dst[:, 512 * g:512 * g + 512], m.PJ[g][:, :], ACT.Copy).then_inc(s["v_evac"], 1)

    def take_probsT(n, u):
        act.wait_ge(s["probsT_in_psum"], n + 1)
        need(act, s["av_done"], n - 1)
        act.activation(t.PT[u % 2], m.TP[u % 2][:, :], ACT.Copy).then_inc(s["probsT_ready"], 1)

    def take_xT(b, p):
        act.wait_ge(s["xT_in_psum"], b + 1)
        act.activation(t.xT[p], m.MX[:, 0:T], ACT.Copy)
        act.activation(t.xTv[p][0], m.MX[:, 0:T], ACT.Copy).then_inc(s["xT_ready"], 1)

    def piece(b, p, kind, g):
        if kind == "q":
            take_q(b, p, g)
        elif kind == "v":
            take_v(b, p, g)

    act.preload_act_table(ACT.Exp)
    take_xT(0, 0)
    if layer == 0:
        loaded(act, m, "wvT")
        for i in range(ATT_PIECES):
            cols = slice(512 * i, 512 * i + 512)
            act.activation(m.wv_hi[:, cols], m.wv[:, cols], ACT.Copy).then_inc(m.split_hi, 1)
    for u in range(U):
        for kind, g in PIECES[u]:
            piece(0, 0, kind, g)
    take_xT(1, 1)

    def slots(b, p):
        for u in range(U):
            exps(b, p, u)
            if not known_last(b):
                for kind, g in PIECES[u]:
                    piece(b + 1, 1 - p, kind, g)
            if not (known_first(b) and u < 1):
                take_probsT(U * b + u - 1, (u - 1) % U)
            if u == 1 and not (isinstance(b, int) and b + 2 >= B):
                take_xT(b + 2, p)

    for_batches(act, slots)
    take_probsT(U * B - 1, U - 1)


def att_vector(v, m, layer):
    s, t = m.att[layer], att_tiles(m)

    def take_k(b, p, g):
        v.wait_ge(s["k_proj"], 2 * b + g + 1)
        if layer == 1 and isinstance(b, int) and b < 2:
            v.wait_ge(m.zeroed, 2 + b)
        for par in range(2):
            if layer == 0:
                src = m.PJ[g][par * 64:par * 64 + 64, :].rearrange("d (c h t) -> d c h t", c=4, t=8)
                dst = t.K[p][0:HD, :].rearrange("d (h t c r) -> d r c h t", h=H, t=8, r=2)[:, par, 4 * g:4 * g + 4]
            else:
                src = m.PJ[g][par * 64:par * 64 + 64, :].rearrange("d (c j) -> d c j", c=4)
                dst = t.K[p][par * 64:par * 64 + 64, :].rearrange("d (c r j) -> d r c j", r=2, j=128)[
                    :, par, 4 * g:4 * g + 4]
            ins = v.tensor_copy(dst, src)
        ins.then_inc(s["k_ready"], 1)

    def maxima(b, p, u):
        n = U * b + u
        v.wait_ge(s["scores_ready"], n + 1)
        v.tensor_reduce(t.negmax[u], m.S[u % 2][:, :].rearrange("p (j k) -> p j k", j=HU), AX.X, ALU.max,
                        negate=True).then_inc(s["negmax_ready"], 1)

    def inverse(b, p, u):
        n = U * b + u
        v.wait_ge(s["exp_done"], n + 1)
        v.reciprocal(t.inverse[u], t.total[u]).then_inc(s["inverse_ready"], 1)

    def take_av(b, p, u):
        n = U * b + u
        v.wait_ge(s["av_done"], n + 1)
        if layer == 0:
            src = m.OV[:, 0:256].rearrange("p (h c t) -> p h c t", h=HU, c=8)
            dst = t.OT[p].rearrange("p (c h t) -> p h c t", c=8, t=8)[:, HU * u:HU * u + HU]
        else:
            src, dst = m.OV[:, 0:256], t.OT[p][:, 256 * u:256 * u + 256]
        v.tensor_copy(dst, src).then_inc(s["av_evac"], 1)

    def take_output(b, p):
        v.wait_ge(s["out_done"], b + 1)
        x = m.X[:, bass.ds(b * D, D)]
        v.tensor_tensor(x, x, m.MX[:, 0:D], ALU.add).then_inc(s["res_done"], 1)
        v.wait_ge(s["res_done"], b + 1)
        return v.bn_stats(m.stats[:, bass.ds(6 * b, 6)], x)

    def tokens(b, p):
        need(v, s["xT_in_psum"], b - 1)
        normalise(v, m, b, t.xn[p]).then_inc(s["xn_ready"], 1)

    def low_tokens(b, p):
        v.wait_ge(s["xT_ready"], b + 1)
        v.tensor_tensor(t.xTv[p][1], m.MX[:, 0:T], t.xTv[p][0], ALU.subtract).then_inc(s["xTv_ready"], 1)

    v.wait_ge(m.rstd_ready, m.att_k[layer] + 1)
    tokens(0, 0)
    tokens(1, 1)
    low_tokens(0, 0)
    if layer == 0:
        for i in range(ATT_PIECES):
            cols = slice(512 * i, 512 * i + 512)
            v.wait_ge(m.split_hi, i + 1)
            v.tensor_tensor(m.wv_lo[:, cols], m.wv[:, cols], m.wv_hi[:, cols], ALU.subtract).then_inc(m.split_lo, 1)
    take_k(0, 0, 0)
    take_k(0, 0, 1)
    low_tokens(1, 1)

    def slots(b, p):
        for u in range(U):
            if u == 2 and not (isinstance(b, int) and b + 2 >= B):
                low_tokens(b + 2, p)
            maxima(b, p, u)
            if not (known_first(b) and u < 3):
                take_av(b if u == 3 else b - 1, p if u == 3 else 1 - p, (u - 3) % U)
            if not known_last(b):
                for kind, g in PIECES[u]:
                    if kind == "k":
                        take_k(b + 1, 1 - p, g)
            if u == 3 and not known_first(b):
                take_output(b - 1, 1 - p)
            inverse(b, p, u)
            if u == 0 and not (isinstance(b, int) and b + 2 >= B):
                tokens(b + 2, p)

    for_batches(v, slots)
    for u in range(1, U):
        take_av(B - 1, 1, u)
    take_output(B - 1, 1).then_inc(m.stream_ready, 1)


def clear_keys_pool(po, m, p):
    po.wait_ge(m.stream_ready, 4)
    po.memset(att_tiles(m).K[p], 0.0).then_inc(m.zeroed, 1)


def att_pool(po, m, layer):
    s, t = m.att[layer], att_tiles(m)

    def divide(b, p, u):
        n = U * b + u
        po.wait_ge(s["inverse_ready"], n + 1)
        P = t.P[u].rearrange("p (j k) -> p j k", j=HU)
        po.tensor_tensor(P, P, t.inverse[u].unsqueeze(2).to_broadcast([128, HU, 128]), ALU.mult)\
            .then_inc(s["probs_ready"], 1)

    def slots(b, p):
        for u in range(U):
            divide(b, p, u)

    for_batches(po, slots)


def att_sync(sp, m, scratch):
    s, t = m.att[0], att_tiles(m)

    def move(b, p):
        sp.wait_ge(s["v_evac"], 2 * (b + 1))
        sp.dma_start(scratch[p], t.Vst[p]).then_inc(m.v_save[p], 16)
        sp.wait_ge(m.v_save[p], 8 * (b - p) + 16)
        sp.dma_start(t.V[p].rearrange("p (h d) -> p h d", h=H),
                     scratch[p].rearrange("(h t) (c d) -> (t c) h d", h=H, d=HD)).then_inc(m.v_load[p], 16)

    for_batches(sp, move)


def context_tensor(pe, m):
    loaded(pe, m, "ctxT")
    loaded(pe, m, "xkv")
    pe.wait_ge(m.stream_ready, 2)
    for g in range(NG):
        cols = slice(GRP * KL * g, GRP * KL * (g + 1))
        for w, bank, made, taken in ((m.w["x0Wk"], m.PJ[0], m.k0_made, m.k0_taken), (m.w["x1WkT"], m.PJ[1], m.k1_made, m.k1_taken)):
            need(pe, taken, g)
            pe.matmul(bank[:, 0:GRP * KL], w[:, :], m.w["ctxT"][:, cols], start=True, stop=True).then_inc(made, 1)
    for b in range(B):
        if b % 2 == 0:
            need(pe, m.v01_taken, b // 2 - 1)
        ins = pe.matmul(m.S[b // 2 % 2][0:KL, 256 * (b % 2):256 * (b % 2) + 256], m.w["ctxT"][:, KL * b:KL * (b + 1)],
                        m.w["WvBoth"][:, :], start=True, stop=True)
        if b % 2 == 1:
            ins.then_inc(m.v01_made, 1)


def context_scalar(act, m):
    for g in range(NG):
        act.wait_ge(m.k1_made, g + 1)
        act.activation(m.KT1[:, GRP * KL * g:GRP * KL * (g + 1)], m.PJ[1][:, 0:GRP * KL], ACT.Copy)\
            .then_inc(m.k1_taken, 1)


def context_vector(v, m):
    loaded(v, m, "ctxT")
    loaded(v, m, "xkv")
    v.tensor_scalar(m.maskb[:, :], m.mask8[:, :], MASKED, None, ALU.mult).then_inc(m.mask_ready, 1)
    for g in range(NG):
        v.wait_ge(m.k0_made, g + 1)
        cols = slice(GRP * KL * g, GRP * KL * (g + 1))
        v.tensor_scalar(m.KT0hi[:, cols], m.PJ[0][:, 0:GRP * KL], m.w["x0bk"][:, 0:1], None, ALU.add)\
            .then_inc(m.k0_high, 1)
        v.wait_ge(m.k0_high, g + 1)
        v.scalar_tensor_tensor(m.KT0lo[:, cols], m.PJ[0][:, 0:GRP * KL], m.w["x0bk"][:, 0:1], m.KT0hi[:, cols],
                               ALU.add, ALU.subtract).then_inc(m.k0_taken, 1)
    for i in range(B // 2):
        v.wait_ge(m.v01_made, i + 1)
        bias = m.w["bvBoth"][0:KL, :].unsqueeze(1).to_broadcast([KL, 2, 2 * D])
        v.tensor_tensor(m.V01[:, 512 * i:512 * i + 512].rearrange("k (b d) -> k b d", b=2),
                        m.S[i % 2][0:KL, :].rearrange("k (b d) -> k b d", b=2), bias, ALU.add)\
            .then_inc(m.v01_taken, 1)


CR_SEMS = ["xn_ready", "xT_in_psum", "xT_ready", "q_proj", "q_high", "q_ready", "kblk_ready", "vblk_ready",
           "scores_ready", "max_done", "negmax_ready", "exp_done", "probsT_in_psum", "probsT_ready", "av_done",
           "inv_done", "inv_ready", "invT_in_psum", "invT_ready", "oT_ready", "out_done", "res_done"]


def cr_tiles(m):
    t = Namespace()
    ar = m.arena
    t.Kblk = [(m.Kblk_parts[:, H * KL * p:H * KL * (p + 1)], m.Kblk_parts[:, H * KL * (2 + p):H * KL * (3 + p)])
              for p in range(2)]
    t.P = [ar[:, 7680 + 512 * u:7680 + 512 * u + HU * KL] for u in range(U)]
    t.PT = [ar[:, 9728:10240], ar[:, 10240:10752]]
    t.qT = [(m.q_parts[:, i * T:(i + 1) * T], m.q_parts[:, (2 + i) * T:(3 + i) * T]) for i in range(2)]
    t.invT, t.oT = ar[:, 11264:11392], ar[:, 11392:11520]
    t.Vblk = [ar[0:KL, 11520 + 512 * p:12032 + 512 * p] for p in range(2)]
    t.total = [m.small[:, 0:16], m.small[:, 16:32]]
    t.inverse = m.small[:, 32:48]
    t.spread = ar[:, 14464:14592]
    t.negmax = [m.small[:, 48 + 4 * u:52 + 4 * u] for u in range(U)]
    t.mx = [m.small[:, 64 + 4 * u:68 + 4 * u] for u in range(U)]
    t.xn = [m.xn[:, 0:D], m.xn[:, D:2 * D]]
    t.xT = m.XTs[:, 0:T]
    t.O = [m.OV, m.PJ[1]]
    return t


def cross0_tensor(pe, m):
    s, t = m.cr, cr_tiles(m)

    def transpose_tokens(b, p):
        pe.wait_ge(s["xn_ready"], b + 1)
        need(pe, s["q_ready"], b)
        pe.transpose(m.PJ[0][:, 0:T], t.xn[p], m.ident).then_inc(s["xT_in_psum"], 1)

    def project(b):
        pe.wait_ge(s["xT_ready"], b + 1)
        pe.matmul(m.PJ[0][:, 0:T], m.w["x0Wq"][:, :], t.xT, start=True, stop=True).then_inc(s["q_proj"], 1)

    def scores(b, p, u):
        n = U * b + u
        if u == 0:
            pe.wait_ge(s["q_ready"], b + 1)
            pe.wait_ge(s["kblk_ready"], b + 1)
        need(pe, s["exp_done"], n - 1)
        mask = m.maskb[:, bass.ds(b * KL, KL)].unsqueeze(1).to_broadcast([128, HU, KL])
        pe.matmul(m.S[u % 2][:, 0:HU * KL].rearrange("p (j k) -> p j k", j=HU), m.identb[:, :], mask,
                  start=True, stop=False)
        cols = slice(HU * KL * u, HU * KL * (u + 1))
        split_product(pe, m.S[u % 2][:, 0:HU * KL], t.qT[p], (t.Kblk[p][0][:, cols], t.Kblk[p][1][:, cols]),
                      start=False).then_inc(s["scores_ready"], 1)

    def transpose_probs(n, u):
        pe.wait_ge(s["exp_done"], n + 1)
        need(pe, s["probsT_ready"], n - 1)
        for j in range(HU):
            ins = pe.transpose(m.TP[u % 2][0:KL, j * 128:(j + 1) * 128], t.P[u][:, j * KL:(j + 1) * KL], m.ident)
        ins.then_inc(s["probsT_in_psum"], 1)

    def values(b, p, u):
        n = U * b + u
        pe.wait_ge(s["probsT_ready"], n + 1)
        if u == 0:
            pe.wait_ge(s["vblk_ready"], b + 1)
            need(pe, s["oT_ready"], b - 1)
        for j in range(HU):
            ins = pe.matmul(t.O[p][32 * u:32 * u + 32, 0:T], t.Vblk[p][:, 32 * (HU * u + j):32 * (HU * u + j) + 32],
                            t.PT[u % 2][0:KL, j * 128:(j + 1) * 128], start=(j == 0), stop=(j == HU - 1))
        ins.then_inc(s["av_done"], 1)

    def transpose_inverse(b):
        pe.wait_ge(s["inv_ready"], b + 1)
        need(pe, s["res_done"], b)
        pe.transpose(m.MX[:, 0:T], t.spread, m.ident)\
            .then_inc(s["invT_in_psum"], 1)

    def output(b):
        pe.wait_ge(s["oT_ready"], b + 1)
        pe.matmul(m.MX[:, 0:D], m.ones[0:1, :], m.w["x0bo"][0:1, :], start=True, stop=False)
        pe.matmul(m.MX[:, 0:D], t.oT, m.w["x0Wo"][:, :], start=False, stop=True).then_inc(s["out_done"], 1)

    loaded(pe, m, "x0")
    pe.wait_ge(m.mask_ready, 1)
    pe.wait_ge(m.const_ready, 2)
    pe.wait_ge(m.v01_taken, B // 2)
    pe.wait_ge(m.k0_taken, NG)
    pe.wait_ge(m.k1_taken, NG)
    transpose_tokens(0, 0)
    project(0)

    def slots(b, p):
        for u in range(U):
            n = U * b + u
            scores(b, p, u)
            if not (known_first(b) and u < 1):
                transpose_probs(n - 1, (u - 1) % U)
            if not (known_first(b) and u < 2):
                values(b if u >= 2 else b - 1, p if u >= 2 else 1 - p, (u - 2) % U)
            if u == 1 and not known_last(b):
                transpose_tokens(b + 1, 1 - p)
            if u == 1 and not known_first(b):
                transpose_inverse(b - 1)
            if u == 2 and not known_last(b):
                project(b + 1)
            if u == 3 and not known_first(b):
                output(b - 1)

    for_batches(pe, slots)
    transpose_inverse(B - 1)
    transpose_probs(U * B - 1, U - 1)
    values(B - 1, 1, U - 2)
    values(B - 1, 1, U - 1)
    output(B - 1)


def cross0_scalar(act, m):
    s, t = m.cr, cr_tiles(m)

    def exps(b, p, u):
        n = U * b + u
        act.wait_ge(s["negmax_ready"], n + 1)
        need(act, s["probsT_in_psum"], n - 3)
        if u == 0:
            need(act, s["inv_done"], b - 1)
        for j in range(HU):
            ins = act.activation(t.P[u][:, j * KL:(j + 1) * KL], m.S[u % 2][:, j * KL:(j + 1) * KL], ACT.Exp,
                                 bias=t.negmax[u][:, j:j + 1], scale=XHD ** -0.5,
                                 accum_out=t.total[p][:, HU * u + j:HU * u + j + 1])
        ins.then_inc(s["exp_done"], 1)

    def take_xT(b):
        act.wait_ge(s["xT_in_psum"], b + 1)
        act.activation(t.xT, m.PJ[0][:, 0:T], ACT.Copy).then_inc(s["xT_ready"], 1)

    def take_q(b, p):
        act.wait_ge(s["q_proj"], b + 1)
        act.activation(t.qT[p][0], m.PJ[0][:, 0:T], ACT.Identity, bias=m.w["x0bq"][:, 0:1]).then_inc(s["q_high"], 1)

    def spread_inverse(b):
        act.wait_ge(s["inv_done"], b + 1)
        need(act, s["invT_in_psum"], b)
        act.activation(t.spread.rearrange("p (h d) -> p h d", h=H), t.inverse.unsqueeze(2).to_broadcast([128, H, XHD]),
                       ACT.Copy).then_inc(s["inv_ready"], 1)

    def take_inverse(b):
        act.wait_ge(s["invT_in_psum"], b + 1)
        need(act, s["oT_ready"], b)
        act.activation(t.invT, m.MX[:, 0:T], ACT.Copy).then_inc(s["invT_ready"], 1)

    def place_values(b, p):
        need(act, s["av_done"], U * (b - 1))
        for j in range(HU):
            own = t.Vblk[p].rearrange("k (u c) -> k u c", u=U)[:, :, (32 + XHD) * j:(32 + XHD) * j + XHD]
            head = m.V01[0:KL, bass.ds(b * 2 * D, D)].rearrange("k (u c) -> k u c", u=U)[:, :, XHD * j:XHD * (j + 1)]
            ins = act.activation(own, head, ACT.Copy)
        ins.then_inc(s["vblk_ready"], 1)

    loaded(act, m, "x0")
    act.preload_act_table(ACT.Exp)
    act.wait_ge(m.v01_taken, B // 2)
    act.wait_ge(m.zeroed, 1)
    place_values(0, 0)
    take_xT(0)
    take_q(0, 0)

    def slots(b, p):
        for u in range(U):
            exps(b, p, u)
            if u == 0 and not known_first(b):
                spread_inverse(b - 1)
            if u == 1 and not known_last(b):
                take_xT(b + 1)
            if u == 1 and not known_first(b):
                take_inverse(b - 1)
            if u == 2 and not known_last(b):
                take_q(b + 1, 1 - p)
            if u == 3 and not known_last(b):
                place_values(b + 1, 1 - p)

    for_batches(act, slots)
    spread_inverse(B - 1)
    take_inverse(B - 1)


def cross0_vector(v, m):
    s, t = m.cr, cr_tiles(m)

    def maxima(b, u):
        n = U * b + u
        v.wait_ge(s["scores_ready"], n + 1)
        v.tensor_reduce(t.mx[u], m.S[u % 2][:, 0:HU * KL].rearrange("p (j k) -> p j k", j=HU), AX.X, ALU.max)\
            .then_inc(s["max_done"], 1)
        v.wait_ge(s["max_done"], n + 1)
        v.tensor_scalar(t.negmax[u], t.mx[u], -XHD ** -0.5, None, ALU.mult).then_inc(s["negmax_ready"], 1)

    def take_probsT(n, u):
        v.wait_ge(s["probsT_in_psum"], n + 1)
        need(v, s["av_done"], n - 1)
        v.tensor_copy(t.PT[u % 2][0:KL, :], m.TP[u % 2][0:KL, :]).then_inc(s["probsT_ready"], 1)

    def tokens(b, p):
        need(v, s["xT_in_psum"], b - 1)
        normalise(v, m, b, t.xn[p]).then_inc(s["xn_ready"], 1)

    def low_q(b, p):
        v.wait_ge(s["q_high"], b + 1)
        v.scalar_tensor_tensor(t.qT[p][1], m.PJ[0][:, 0:T], m.w["x0bq"][:, 0:1], t.qT[p][0], ALU.add, ALU.subtract)\
            .then_inc(s["q_ready"], 1)

    def inverses(b, p):
        v.wait_ge(s["exp_done"], U * (b + 1))
        need(v, s["inv_ready"], b)
        v.reciprocal(t.inverse, t.total[p]).then_inc(s["inv_done"], 1)

    def divide(b, p):
        v.wait_ge(s["av_done"], U * (b + 1))
        v.wait_ge(s["invT_ready"], b + 1)
        need(v, s["out_done"], b)
        v.tensor_tensor(t.oT, t.O[p][:, 0:T], t.invT, ALU.mult).then_inc(s["oT_ready"], 1)

    def take_output(b):
        v.wait_ge(s["out_done"], b + 1)
        x = m.X[:, bass.ds(b * D, D)]
        v.tensor_tensor(x, x, m.MX[:, 0:D], ALU.add).then_inc(s["res_done"], 1)
        v.wait_ge(s["res_done"], b + 1)
        return v.bn_stats(m.stats[:, bass.ds(6 * b, 6)], x)

    loaded(v, m, "x0")
    v.wait_ge(m.rstd_ready, 2)
    tokens(0, 0)
    tokens(1, 1)
    low_q(0, 0)

    def slots(b, p):
        for u in range(U):
            n = U * b + u
            maxima(b, u)
            if u == 2 and not known_first(b):
                divide(b - 1, 1 - p)
            if not (known_first(b) and u < 1):
                take_probsT(n - 1, (u - 1) % U)
            if u == 0 and not known_first(b):
                inverses(b - 1, 1 - p)
            if u == 1 and not (isinstance(b, int) and b + 2 >= B):
                tokens(b + 2, p)
            if u == 3 and not known_last(b):
                low_q(b + 1, 1 - p)
            if u == 3 and not known_first(b):
                take_output(b - 1)

    for_batches(v, slots)
    inverses(B - 1, 1)
    take_probsT(U * B - 1, U - 1)
    divide(B - 1, 1)
    take_output(B - 1).then_inc(m.stream_ready, 1)


def cross0_pool(po, m):
    s, t = m.cr, cr_tiles(m)
    po.wait_ge(m.stream_ready, 2)
    po.memset(m.arena[:, 11520:12544], 0.0).then_inc(m.zeroed, 1)
    po.wait_ge(m.k0_taken, NG)

    def blocks(b, p):
        if not (isinstance(b, int) and b < 2):
            po.wait_ge(s["scores_ready"], U * (b - 1))
        if not known_first(b):
            po.wait_ge(m.split_hi, W1_SPLIT + b)
        for part, keys in zip(t.Kblk[p], (m.KT0hi, m.KT0lo)):
            ins = po.tensor_tensor(part.rearrange("p (h k) -> p h k", h=H),
                                   keys[:, bass.ds(b * KL, KL)].unsqueeze(1).to_broadcast([128, H, KL]),
                                   m.headmask.unsqueeze(2).to_broadcast([128, H, KL]), ALU.mult)
        ins.then_inc(s["kblk_ready"], 1)
        if not known_first(b):
            w1_low(b - 1)
        split_high(po, m, m.w["W1"][:, piece(b)], m.W1hi[:, piece(b)])

    def piece(b):
        return bass.ds(b * (E0 * F0 // B), E0 * F0 // B)

    def w1_low(b):
        split_low(po, m, m.w["W1"][:, piece(b)], m.W1hi[:, piece(b)], m.W1lo[:, piece(b)])

    loaded(po, m, "ffn0")
    for_batches(po, blocks)
    po.wait_ge(m.split_hi, W1_SPLIT + B)
    w1_low(B - 1)


X1_SEMS = ["xn_ready", "xT_in_psum", "xT_ready", "q_proj", "q_ready", "scores_ready", "max_done", "negmax_ready",
           "exp_done", "probsT_in_psum", "probsT_ready", "av_done", "inv_done", "o_ready", "oT_in_psum", "oT_ready",
           "out_done", "res_done"]
STAGES = 8


def x1_tiles(m):
    t = Namespace()
    ar = m.arena
    t.xn, t.xT, t.qT, t.P, t.PT, t.o, t.oT = ([ar[:, 256 * i + 128 * p:256 * i + 128 * p + 128] for p in range(2)]
                                              for i in range(7))
    t.mx, t.negmax, t.total, t.inverse = ([m.small[:, 2 * i + p:2 * i + p + 1] for p in range(2)] for i in range(4))
    t.X, t.Q, t.S, t.PTp, t.AV, t.OTp, t.Y = (bank[:, 0:128] for bank in (m.MX, m.PJ[0], m.S[0], m.TP[0], m.OV,
                                                                          m.PJ[1], m.TP[1]))
    return t


def for_steps(eng, stages):
    def step(b, parity):
        for k in reversed(range(STAGES)):
            if stages[k] is not None and not (isinstance(b, int) and not 0 <= b + STAGES - 1 - k < B):
                stages[k](b + STAGES - 1 - k, (parity + STAGES - 1 - k) % 2)

    for b in range(1 - STAGES, 2):
        step(b, b % 2)
    with eng.Fori(0, (B - STAGES) // 2 - 1) as i:
        step(2 * i + 2, 0)
        step(2 * i + 3, 1)
    for b in range(B - STAGES, B):
        step(b, b % 2)


def cross1_tensor(pe, m):
    s, t = m.x1, x1_tiles(m)
    loaded(pe, m, "x1")

    def transpose_tokens(b, p):
        pe.wait_ge(s["xn_ready"], b + 1)
        need(pe, s["xT_ready"], b)
        pe.transpose(t.X, t.xn[p], m.ident).then_inc(s["xT_in_psum"], 1)

    def project(b, p):
        pe.wait_ge(s["xT_ready"], b + 1)
        need(pe, s["q_ready"], b)
        pe.matmul(t.Q, m.w["x1WqT"][:, :], t.xT[p], start=True, stop=True).then_inc(s["q_proj"], 1)

    def scores(b, p):
        pe.wait_ge(s["q_ready"], b + 1)
        need(pe, s["exp_done"], b)
        pe.matmul(t.S[:, 0:KL], t.qT[p], m.KT1[:, bass.ds(b * KL, KL)], start=True, stop=True)\
            .then_inc(s["scores_ready"], 1)

    def transpose_probs(b, p):
        pe.wait_ge(s["exp_done"], b + 1)
        need(pe, s["probsT_ready"], b)
        pe.transpose(t.PTp[0:KL, :], t.P[p][:, 0:KL], m.ident).then_inc(s["probsT_in_psum"], 1)

    def values(b, p):
        pe.wait_ge(s["probsT_ready"], b + 1)
        need(pe, s["o_ready"], b)
        pe.matmul(t.AV, t.PT[p][0:KL, :], m.V01[0:KL, bass.ds(b * 2 * D + D, D)], start=True, stop=True)\
            .then_inc(s["av_done"], 1)

    def transpose_o(b, p):
        pe.wait_ge(s["o_ready"], b + 1)
        need(pe, s["oT_ready"], b)
        pe.transpose(t.OTp, t.o[p], m.ident).then_inc(s["oT_in_psum"], 1)

    def output(b, p):
        pe.wait_ge(s["oT_ready"], b + 1)
        need(pe, s["res_done"], b)
        pe.matmul(t.Y, m.ones[0:1, :], m.w["x1bo"][0:1, :], start=True, stop=False)
        pe.matmul(t.Y, t.oT[p], m.w["x1WoT"][:, :], start=False, stop=True).then_inc(s["out_done"], 1)

    for_steps(pe, [None, transpose_tokens, project, scores, transpose_probs, values, transpose_o, output])


def cross1_scalar(act, m):
    s, t = m.x1, x1_tiles(m)
    loaded(act, m, "x1")

    def take_xT(b, p):
        act.wait_ge(s["xT_in_psum"], b + 1)
        need(act, s["q_proj"], b - 1)
        act.activation(t.xT[p], t.X, ACT.Copy).then_inc(s["xT_ready"], 1)

    def take_q(b, p):
        act.wait_ge(s["q_proj"], b + 1)
        need(act, s["scores_ready"], b - 1)
        act.activation(t.qT[p], t.Q, ACT.Identity, bias=m.w["x1bq"][:, 0:1]).then_inc(s["q_ready"], 1)

    def exps(b, p):
        act.wait_ge(s["negmax_ready"], b + 1)
        need(act, s["probsT_in_psum"], b - 1)
        act.activation(t.P[p][:, 0:KL], t.S[:, 0:KL], ACT.Exp, bias=t.negmax[p], scale=D ** -0.5,
                       accum_out=t.total[p]).then_inc(s["exp_done"], 1)

    def take_oT(b, p):
        act.wait_ge(s["oT_in_psum"], b + 1)
        need(act, s["out_done"], b - 1)
        act.activation(t.oT[p], t.OTp, ACT.Copy).then_inc(s["oT_ready"], 1)

    for_steps(act, [None, take_xT, take_q, exps, None, None, take_oT, None])


def cross1_vector(v, m):
    s, t = m.x1, x1_tiles(m)
    v.wait_ge(m.rstd_ready, 5)

    def tokens(b, p):
        need(v, s["xT_in_psum"], b - 1)
        normalise(v, m, b, t.xn[p]).then_inc(s["xn_ready"], 1)

    def maxima(b, p):
        v.wait_ge(s["scores_ready"], b + 1)
        v.tensor_reduce(t.mx[p], t.S[:, 0:KL], AX.X, ALU.max).then_inc(s["max_done"], 1)
        v.wait_ge(s["max_done"], b + 1)
        v.tensor_scalar(t.negmax[p], t.mx[p], -D ** -0.5, None, ALU.mult).then_inc(s["negmax_ready"], 1)

    def take_probsT(b, p):
        v.wait_ge(s["probsT_in_psum"], b + 1)
        need(v, s["av_done"], b - 1)
        v.tensor_copy(t.PT[p][0:KL, :], t.PTp[0:KL, :]).then_inc(s["probsT_ready"], 1)
        v.wait_ge(s["exp_done"], b + 1)
        v.reciprocal(t.inverse[p], t.total[p]).then_inc(s["inv_done"], 1)

    def take_values(b, p):
        v.wait_ge(s["av_done"], b + 1)
        v.wait_ge(s["inv_done"], b + 1)
        need(v, s["oT_in_psum"], b - 1)
        v.tensor_scalar(t.o[p], t.AV, t.inverse[p], None, ALU.mult).then_inc(s["o_ready"], 1)

    def take_output(b, p):
        v.wait_ge(s["out_done"], b + 1)
        x = m.X[:, bass.ds(b * D, D)]
        v.tensor_tensor(x, x, t.Y, ALU.add).then_inc(s["res_done"], 1)
        v.wait_ge(s["res_done"], b + 1)
        ins = v.bn_stats(m.stats[:, bass.ds(6 * b, 6)], x)
        if known_last(b):
            ins.then_inc(m.stream_ready, 1)

    for_steps(v, [tokens, None, None, maxima, take_probsT, take_values, None, take_output])


RT_SEMS = ["xn_ready", "xT_in_psum", "xT_ready", "xT_kept", "logits_done", "logits_ready"]


def rt_tiles(m):
    t = Namespace()
    t.xn = [m.xn[:, 0:D], m.xn[:, D:2 * D]]
    t.xT = [m.XTs[:, 0:T], m.XTs[:, T:2 * T]]
    t.X = [m.MX[:, 0:T], m.PJ[0][:, 0:T]]
    t.L = [m.OV, m.PJ[1]]
    return t


def router_tensor(pe, m, layer):
    s, t = m.rt, rt_tiles(m)
    w, E = ((m.w["Wr"], E0), (m.w["gateT"], E1))[layer]
    loaded(pe, m, ("ffn0", "ffn1")[layer])

    def transpose_tokens(b, p):
        k = b + B * layer
        pe.wait_ge(s["xn_ready"], k + 1)
        need(pe, s["xT_kept"], k - 1)
        pe.transpose(t.X[p], t.xn[p], m.ident).then_inc(s["xT_in_psum"], 1)

    def slots(b, p):
        k = b + B * layer
        if not known_last(b):
            transpose_tokens(b + 1, 1 - p)
        pe.wait_ge(s["xT_ready"], k + 1)
        need(pe, s["logits_ready"], k - 1)
        pe.matmul(t.L[p][:, 0:E], t.xT[p], w[:, :], start=True, stop=True).then_inc(s["logits_done"], 1)

    transpose_tokens(0, 0)
    for_batches(pe, slots)


def router_scalar(act, m, layer):
    s, t = m.rt, rt_tiles(m)

    def slots(b, p):
        k = b + B * layer
        act.wait_ge(s["xT_in_psum"], k + 1)
        need(act, s["logits_done"], k - 1)
        act.activation(m.XThi[:, bass.ds(b * T, T)], t.X[p], ACT.Copy)
        act.activation(t.xT[p], t.X[p], ACT.Copy).then_inc(s["xT_ready"], 1)

    for_batches(act, slots)


def router_vector(v, m, layer):
    s, t = m.rt, rt_tiles(m)
    E = (E0, E1)[layer]
    LG = m.arena[:, 6400:6400 + B * E]
    v.wait_ge(m.rstd_ready, (2, 5)[layer] + 1)

    def tokens(b, p):
        k = b + B * layer
        need(v, s["xT_in_psum"], k - 1)
        normalise(v, m, b, t.xn[p]).then_inc(s["xn_ready"], 1)

    def slots(b, p):
        k = b + B * layer
        v.wait_ge(s["xT_ready"], k + 1)
        cols = bass.ds(b * T, T)
        v.tensor_tensor(m.XTlo[:, cols], t.X[p], m.XThi[:, cols], ALU.subtract).then_inc(s["xT_kept"], 1)
        if not (isinstance(b, int) and b + 2 >= B):
            tokens(b + 2, p)
        v.wait_ge(s["logits_done"], k + 1)
        v.tensor_copy(LG[:, bass.ds(b * E, E)], t.L[p][:, 0:E]).then_inc(s["logits_ready"], 1)

    tokens(0, 0)
    tokens(1, 1)
    for_batches(v, slots)


def r0_tiles(m):
    t = Namespace()
    ar = m.arena
    t.H = [ar[:, 0:2048], ar[:, 2048:4096]]
    t.Y = [ar[:, i:i + 512] for i in (8192, 8704, 9216, 9728, 10240, 10752, 15360, 15872)]
    t.gateT = ar[:, 4096:4224]
    t.gate = ar[:, 4224:4352]
    t.b2sel = ar[:, 4352:6400]
    t.score = ar[:, 6400:6528]
    t.scoreT = ar[:, 7168:7296]
    t.junk, t.above, t.equal, t.rank = (ar[:, 7296 + 128 * i:7424 + 128 * i] for i in range(4))
    t.threshold, t.candidate, t.bit, t.count, t.kept, t.room = (m.small[:, i:i + 1] for i in range(6))
    t.counts = m.small[:, 6:8]
    t.row = m.small[:, 16:32]
    return t


BITS = 30


def route0_vector(v, m):
    t, s = r0_tiles(m), m.r0
    score = t.score.rearrange("p (b e) -> p b e", e=E0)
    row = t.row.unsqueeze(2).to_broadcast([128, B, E0])
    c = Chain(v, s["chain"])
    v.wait_ge(m.rt["logits_ready"], B)
    c.step(v.tensor_reduce(t.row, score, AX.X, ALU.max))
    v.tensor_tensor(score, score, row, ALU.subtract).then_inc(s["shifted"], 1)
    v.wait_ge(s["exp_done"], 1)
    c.step(v.tensor_reduce(t.row, score, AX.X, ALU.add))
    c.step(v.reciprocal(t.row, t.row))
    v.tensor_tensor(score, score, row, ALU.mult).then_inc(s["score_ready"], 1)
    c.step(v.memset(t.threshold.bitcast(U32), 0))
    c.step(v.memset(t.bit.bitcast(U32), 1 << (BITS - 1)))
    v.wait_ge(s["scoreT_in_psum"], 1)
    c.step(v.tensor_copy(t.scoreT, m.MX[:, 0:128]))
    with v.Fori(0, BITS) as i:
        d = Chain(v, s["bits"], 4 * i)
        d.step(v.tensor_tensor(t.candidate.bitcast(U32), t.threshold.bitcast(U32), t.bit.bitcast(U32), ALU.bitwise_or))
        v.tensor_scalar(t.junk, t.scoreT, t.candidate, 0.0, ALU.is_ge, ALU.add, accum_out=t.count)\
            .then_inc(s["counted"], 1)
        d.step(v.tensor_scalar(t.bit.bitcast(U32), t.bit.bitcast(U32), 1, None, ALU.logical_shift_right))
        v.wait_ge(s["summed"], i + 1)
        d.step(v.tensor_scalar(t.kept, m.MX[:, 0:1], float(CAP), t.candidate, ALU.is_ge, ALU.mult))
        d.step(v.tensor_tensor(t.threshold, t.threshold, t.kept, ALU.max))
    c.step(v.tensor_scalar(t.above, t.scoreT, t.threshold, 0.0, ALU.is_gt, ALU.add, accum_out=t.counts[:, 0:1]))
    v.tensor_scalar(t.equal, t.scoreT, t.threshold, 0.0, ALU.is_equal, ALU.add, accum_out=t.counts[:, 1:2])\
        .then_inc(s["ties_counted"], 1)
    v.wait_ge(s["ties_summed"], 1)
    c.step(v.tensor_scalar(t.room, m.MX[:, 0:1], -1.0, float(CAP), ALU.mult, ALU.add))
    c.step(v.tensor_copy(t.count, m.MX[:, 1:2]))
    c.step(v.memset(t.junk, 1.0))
    c.step(v.tensor_tensor_scan(t.rank, t.junk, t.equal, t.count, ALU.mult, ALU.add))
    c.step(v.tensor_scalar(t.rank, t.rank, t.room, None, ALU.is_le))
    c.step(v.tensor_tensor(t.rank, t.rank, t.equal, ALU.mult))
    c.step(v.tensor_tensor(t.rank, t.rank, t.above, ALU.add))
    v.tensor_tensor(t.gateT, t.rank, t.scoreT, ALU.mult).then_inc(s["gateT_ready"], 1)
    v.wait_ge(s["gate_in_psum"], 1)
    v.tensor_copy(t.gate, m.MX[:, 0:128]).then_inc(s["gate_ready"], 1)


def route0_scalar(act, m):
    t, s = r0_tiles(m), m.r0
    act.wait_ge(s["shifted"], 1)
    act.activation(t.score, t.score, ACT.Exp).then_inc(s["exp_done"], 1)


def route0_pool(po, m):
    t = r0_tiles(m)
    po.wait_ge(m.stream_ready, 3)
    loaded(po, m, "ffn0")
    po.tensor_tensor(t.b2sel.rearrange("p (b d) -> p b d", b=B), m.w["b2rep"][:, :].unsqueeze(1).to_broadcast([128, B, D]),
                     m.headmask.unsqueeze(2).to_broadcast([128, B, D]), ALU.mult).then_inc(m.r0["b2_ready"], 1)


def experts0_tensor(pe, m):
    t, s, r = r0_tiles(m), m.e0, m.r0
    hidden_banks = [m.S[0], m.S[1], m.TP[0], m.TP[1]]

    def up(g, e, c):
        n = E0 * g + e
        need(pe, s["gelu_done"], C0 * n - (C0 - 1) + c)
        w, x = slice((e * C0 + c) * 128, (e * C0 + c + 1) * 128), bass.ds(g * GT, GT)
        split_product(pe, hidden_banks[c][:, :], (m.W1hi[:, w], m.W1lo[:, w]), (m.XThi[:, x], m.XTlo[:, x]))\
            .then_inc(s["up_done"], 1)

    def down(g, e, i):
        n = E0 * g + e
        H = t.H[e % 2]
        if i == 0:
            pe.wait_ge(s["gelu_done"], C0 * (n + 1))
            if isinstance(g, int) and g == 0:
                need(pe, s["y_saved"], e - 1)
            else:
                need(pe, s["add_done"], n - 1 + g)
        for c in range(C0):
            ins = pe.matmul(m.PJ[e % 2][:, i * D:(i + 1) * D], H[:, c * GT + i * T:c * GT + (i + 1) * T],
                            m.w["W2"][:, (e * C0 + c) * D:(e * C0 + c + 1) * D], start=(c == 0), stop=(c == C0 - 1))
        if i == GRP - 1:
            ins.then_inc(s["down_done"], 1)

    def biases(g):
        need(pe, s["add_done"], (E0 + 1) * g)
        for i in range(GRP):
            ins = pe.matmul(m.OV[:, i * D:(i + 1) * D], t.gateT, m.b2sel_of(t, GRP * g + i), start=True, stop=True)
        ins.then_inc(s["bias_done"], 1)

    def threshold_step(k):
        if k < BITS:
            pe.wait_ge(r["counted"], k + 1)
            pe.matmul(m.MX[:, 0:1], m.same_expert, t.count, start=True, stop=True).then_inc(r["summed"], 1)
        elif k == BITS:
            pe.wait_ge(r["ties_counted"], 1)
            pe.matmul(m.MX[:, 0:1], m.same_expert, t.counts[:, 0:1], start=True, stop=True)
            pe.matmul(m.MX[:, 1:2], m.earlier_rows, t.counts[:, 1:2], start=True, stop=True)\
                .then_inc(r["ties_summed"], 1)

    pe.wait_ge(m.rt["xT_kept"], B)
    pe.wait_ge(m.rt["logits_ready"], B)
    pe.wait_ge(m.split_lo, W1_SPLIT + W1_PIECES)
    for c in range(C0):
        up(0, 0, c)
    pe.wait_ge(r["score_ready"], 1)
    pe.transpose(m.MX[:, 0:128], t.score, m.ident).then_inc(r["scoreT_in_psum"], 1)
    for e in range(E0):
        for c in range(C0):
            threshold_step(C0 * e + c)
            up(0 if e < E0 - 1 else 1, (e + 1) % E0, c)
            down(0, e, c)
    pe.wait_ge(r["gateT_ready"], 1)
    pe.transpose(m.MX[:, 0:128], t.gateT, m.ident).then_inc(r["gate_in_psum"], 1)
    pe.wait_ge(r["b2_ready"], 1)
    biases(0)

    def group(g):
        for e in range(E0):
            if e < E0 - 1 or not (isinstance(g, int) and g == NG - 1):
                for c in range(C0):
                    up(g if e < E0 - 1 else g + 1, (e + 1) % E0, c)
            for i in range(GRP):
                down(g, e, i)
        biases(g)

    with pe.Fori(1, NG - 1) as g:
        group(g)
    group(NG - 1)


def experts0_scalar(act, m):
    t, s = r0_tiles(m), m.e0
    hidden_banks = [m.S[0], m.S[1], m.TP[0], m.TP[1]]
    act.preload_act_table(ACT.Gelu)

    def gelus(g, e):
        n = E0 * g + e
        for c in range(C0):
            act.wait_ge(s["up_done"], C0 * n + c + 1)
            if c == 0:
                need(act, s["down_done"], n - 1)
            act.activation(t.H[e % 2][:, c * GT:(c + 1) * GT], hidden_banks[c][:, :], ACT.Gelu,
                           bias=m.w["b1T"][:, e * C0 + c:e * C0 + c + 1]).then_inc(s["gelu_done"], 1)

    gelus(0, 0)
    for e in range(E0):
        if e < E0 - 1:
            gelus(0, e + 1)
        act.wait_ge(s["down_done"], e + 1)
        act.activation(t.Y[e], m.PJ[e % 2][:, :], ACT.Copy).then_inc(s["y_saved"], 1)

    def group(g):
        for e in range(E0):
            gelus(g, e)

    with act.Fori(1, NG - 1) as g:
        group(g)
    group(NG - 1)


def experts0_vector(v, m):
    t, s = r0_tiles(m), m.e0

    def group(g):
        first = isinstance(g, int) and g == 0
        for e in range(E0):
            v.wait_ge(s["y_saved"] if first else s["down_done"], E0 * g + e + 1)
            need(v, s["add_done"], (E0 + 1) * g + e)
            for i in range(GRP):
                x = m.X[:, bass.ds((GRP * g + i) * D, D)]
                y = (t.Y[e] if first else m.PJ[e % 2])[:, i * D:(i + 1) * D]
                ins = v.scalar_tensor_tensor(x, y, t.gate[:, bass.ds((GRP * g + i) * E0 + e, 1)], x, ALU.mult, ALU.add)
            ins.then_inc(s["add_done"], 1)
        v.wait_ge(s["bias_done"], g + 1)
        v.wait_ge(s["add_done"], (E0 + 1) * g + E0)
        x = m.X[:, bass.ds(g * GT, GT)]
        v.tensor_tensor(x, x, m.OV[:, :], ALU.add).then_inc(s["add_done"], 1)
        v.wait_ge(s["add_done"], (E0 + 1) * (g + 1))
        for i in range(GRP):
            ins = v.bn_stats(m.stats[:, bass.ds(6 * (GRP * g + i), 6)], m.X[:, bass.ds((GRP * g + i) * D, D)])
        return ins

    v.wait_ge(m.r0["gate_ready"], 1)
    group(0)
    with v.Fori(1, NG - 1) as g:
        group(g)
    group(NG - 1).then_inc(m.stream_ready, 1)


def r1_tiles(m):
    t = Namespace()
    ar = m.arena
    t.score = ar[:, 6400:6656]
    t.a, t.b, t.c, t.d = (ar[:, 6656 + 64 * i:6720 + 64 * i] for i in range(4))
    t.pair, t.tie = ar[:, 6912:7168], ar[:, 7168:7424]
    t.padded = ar[:, 7424:7808]
    t.marked = ar[:, 7808:8192]
    t.top = ar[:, 8192:8320]
    t.combine = ar[:, 8320:8576]
    t.row = m.small[:, 0:16]
    t.G = [ar[:, 0:1152], ar[:, 1152:2304]]
    t.Hn = [ar[:, 2304:3456], ar[:, 3456:4608]]
    t.HT = [ar[:, 8704:9856], ar[:, 9856:11008]]
    t.xT = [(m.XTparts[:, i * T:(i + 1) * T], m.XTparts[:, (2 + i) * T:(3 + i) * T]) for i in range(2)]
    return t


def route1_vector(v, m):
    t, s = r1_tiles(m), m.r1
    c = Chain(v, s["chain"])
    v.wait_ge(s["score_ready"], 1)
    ex = t.score.rearrange("p (g e) -> p e g", e=4)
    c.step(v.tensor_tensor(t.a, ex[:, 0], ex[:, 1], ALU.max))
    c.step(v.tensor_tensor(t.b, ex[:, 0], ex[:, 1], ALU.min))
    c.step(v.tensor_tensor(t.c, ex[:, 2], ex[:, 3], ALU.max))
    c.step(v.tensor_tensor(t.d, ex[:, 2], ex[:, 3], ALU.min))
    c.step(v.tensor_tensor(t.b, t.b, t.d, ALU.max))
    c.step(v.tensor_tensor(t.d, t.a, t.c, ALU.min))
    c.step(v.tensor_tensor(t.b, t.b, t.d, ALU.max))
    c.step(v.tensor_tensor(t.a, t.a, t.c, ALU.max))
    c.step(v.tensor_tensor(t.a, t.a, t.b, ALU.add))
    other = t.a.rearrange("p (b o) -> p b o", o=G1).unsqueeze(2).to_broadcast([128, B, G1, G1])
    own = t.a.rearrange("p (b o) -> p b o", o=G1).unsqueeze(3).to_broadcast([128, B, G1, G1])
    pair = t.pair.rearrange("p (b g o) -> p b g o", g=G1, o=G1)
    tie = t.tie.rearrange("p (b g o) -> p b g o", g=G1, o=G1)
    c.step(v.tensor_tensor(pair, other, own, ALU.is_gt))
    c.step(v.tensor_tensor(tie, other, own, ALU.is_equal))
    c.step(v.tensor_tensor(t.tie, t.tie, m.earlier_group, ALU.mult))
    c.step(v.tensor_tensor(t.pair, t.pair, t.tie, ALU.add))
    c.step(v.tensor_reduce(t.b, t.pair.rearrange("p (g o) -> p g o", o=G1), AX.X, ALU.add))
    c.step(v.tensor_scalar(t.b, t.b, float(TOPG), 4.0, ALU.is_lt, ALU.mult))
    c.step(v.tensor_scalar(t.b, t.b, -4.0, None, ALU.add))
    padded = t.padded.rearrange("p (b e) -> p b e", e=24)
    marked = t.marked.rearrange("p (b e) -> p b e", e=24)
    score = t.score.rearrange("p (b e) -> p b e", e=E1)
    c.step(v.memset(t.padded, -9.0))
    c.step(v.tensor_copy(marked[:, :, 0:E1].rearrange("p b (g e) -> p b g e", e=4),
                         t.b.rearrange("p (b g) -> p b g", g=G1).unsqueeze(3).to_broadcast([128, B, G1, 4])))
    c.step(v.tensor_tensor(padded[:, :, 0:E1], score, marked[:, :, 0:E1], ALU.add))
    for b in range(B):
        ins = v.max(t.top[:, 8 * b:8 * b + 8], t.padded[:, 24 * b:24 * b + 24])
    c.step(ins)
    c.step(v.memset(t.top.rearrange("p (b e) -> p b e", e=8)[:, :, TOPK:8], -9.0))
    for b in range(B):
        ins = v.match_replace(t.marked[:, 24 * b:24 * b + 24], t.top[:, 8 * b:8 * b + 8],
                              t.padded[:, 24 * b:24 * b + 24], -16.0)
    c.step(ins)
    combine = t.combine.rearrange("p (b e) -> p b e", e=E1)
    row = t.row.unsqueeze(2).to_broadcast([128, B, E1])
    c.step(v.tensor_scalar(combine, marked[:, :, 0:E1], -16.0, None, ALU.is_equal))
    c.step(v.tensor_tensor(t.combine, t.combine, t.score, ALU.mult))
    c.step(v.tensor_reduce(t.row, combine, AX.X, ALU.add))
    c.step(v.tensor_scalar(t.row, t.row, 1e-6, None, ALU.add))
    c.step(v.reciprocal(t.row, t.row))
    v.tensor_tensor(combine, combine, row, ALU.mult).then_inc(s["combine_ready"], 1)


def route1_scalar(act, m):
    t = r1_tiles(m)
    act.wait_ge(m.rt["logits_ready"], 2 * B)
    act.activation(t.score, t.score, ACT.Sigmoid).then_inc(m.r1["score_ready"], 1)


def experts1_tensor(pe, m):
    t, s = r1_tiles(m), m.e1
    gate_banks, up_banks = [m.S[0], m.S[1], m.MX[:, 0:128]], [m.TP[0], m.TP[1], m.MX[:, 128:256]]

    def up(b, p):
        pe.wait_ge(s["xT_ready"], b + 1)
        for i in range(3):
            width = 512 if i < 2 else 128
            for banks, w, read, done in ((gate_banks, (m.w1hi, m.w1lo), s["silu_done"], s["gate_done"]),
                                         (up_banks, (m.w3hi, m.w3lo), s["mul_done"], s["up_done"])):
                need(pe, read, 3 * (b - 1) + i + 1)
                if i == 2:
                    need(pe, s["mul_done"], 3 * b)
                cols = slice(512 * i, 512 * i + width)
                split_product(pe, banks[i][:, 0:width], t.xT[p], (w[0][:, cols], w[1][:, cols])).then_inc(done, 1)

    def transpose_hidden(b, p, part):
        pe.wait_ge(s["gated"], b + 1)
        bank = m.PJ[part % 2]
        if part == 0:
            need(pe, s["hT_act"], 2 * b)
        elif part == 1:
            need(pe, s["hT_dve"], b)
        else:
            pe.wait_ge(s["hT_act"], 2 * b + 1)
        chunks = range(4 * part, min(4 * part + 4, FC))
        for i, c in enumerate(chunks):
            ins = pe.transpose(bank[:, i * T:(i + 1) * T], t.Hn[p][:, c * 128:(c + 1) * 128], m.ident)
        ins.then_inc(s["hT_in_psum"], 1)

    def down(b, p):
        pe.wait_ge(s["hT_act"], 2 * (b + 1))
        pe.wait_ge(s["hT_dve"], b + 1)
        need(pe, s["res_done"], b)
        for c in range(FC):
            ins = pe.matmul(m.OV[:, 0:D], t.HT[p][:, c * T:(c + 1) * T], m.w2T[:, c * D:(c + 1) * D],
                            start=(c == 0), stop=(c == FC - 1))
        ins.then_inc(s["down_done"], 1)

    def slots(b, p):
        up(b, p)
        if not known_first(b):
            transpose_hidden(b - 1, 1 - p, 0)
            transpose_hidden(b - 1, 1 - p, 1)
        if not (isinstance(b, int) and b < 2):
            down(b - 2, p)
        if not known_first(b):
            transpose_hidden(b - 1, 1 - p, 2)

    pe.wait_ge(m.split_lo, FFN1_SPLIT + FFN1_PIECES)
    for_batches(pe, slots)
    transpose_hidden(B - 1, 1, 0)
    transpose_hidden(B - 1, 1, 1)
    down(B - 2, 0)
    transpose_hidden(B - 1, 1, 2)
    down(B - 1, 1)


def experts1_scalar(act, m):
    t, s = r1_tiles(m), m.e1
    gate_banks = [m.S[0], m.S[1], m.MX[:, 0:128]]
    act.preload_act_table(ACT.Silu)
    act.wait_ge(m.rt["xT_kept"], 2 * B)

    def take_x(b, p):
        need(act, s["up_done"], 3 * (b - 1))
        act.activation(t.xT[p][0], m.XThi[:, bass.ds(b * T, T)], ACT.Copy)
        act.activation(t.xT[p][1], m.XTlo[:, bass.ds(b * T, T)], ACT.Copy).then_inc(s["xT_ready"], 1)

    def take_hT(b, p, part):
        act.wait_ge(s["hT_in_psum"], 3 * b + part + 1)
        need(act, s["down_done"], b - 1)
        n = 4 if part == 0 else 1
        act.activation(t.HT[p][:, 4 * part * T:(4 * part + n) * T], m.PJ[0][:, 0:n * T], ACT.Copy)\
            .then_inc(s["hT_act"], 1)

    take_x(0, 0)

    def slots(b, p):
        if not known_last(b):
            take_x(b + 1, 1 - p)
        for i in range(3):
            width = 512 if i < 2 else 128
            act.wait_ge(s["gate_done"], 3 * b + i + 1)
            if i == 2:
                act.wait_ge(s["up_done"], 3 * (b + 1))
            if i == 0:
                need(act, s["mul_done"], 3 * (b - 1))
            act.activation(t.G[p][:, 512 * i:512 * i + width], gate_banks[i][:, 0:width], ACT.Silu)\
                .then_inc(s["silu_done"], 1)
        if not known_first(b):
            take_hT(b - 1, 1 - p, 0)
            take_hT(b - 1, 1 - p, 2)

    for_batches(act, slots)
    take_hT(B - 1, 1, 0)
    take_hT(B - 1, 1, 2)


def experts1_vector(v, m):
    t, s = r1_tiles(m), m.e1
    up_banks = [m.TP[0], m.TP[1], m.MX[:, 128:256]]

    def take_hT(b, p):
        v.wait_ge(s["hT_in_psum"], 3 * b + 2)
        need(v, s["down_done"], b - 1)
        v.tensor_copy(t.HT[p][:, 4 * T:8 * T], m.PJ[1][:, :]).then_inc(s["hT_dve"], 1)

    def take_output(b):
        v.wait_ge(s["down_done"], b + 1)
        x = m.X[:, bass.ds(b * D, D)]
        v.tensor_tensor(x, x, m.OV[:, 0:D], ALU.add).then_inc(s["res_done"], 1)

    def slots(b, p):
        for i in range(3):
            width = 512 if i < 2 else 128
            v.wait_ge(s["up_done"], 3 * b + i + 1)
            v.wait_ge(s["silu_done"], 3 * b + i + 1)
            if i == 0:
                need(v, s["hT_in_psum"], 3 * (b - 1))
            cols = slice(512 * i, 512 * i + width)
            v.tensor_tensor(t.Hn[p][:, cols], t.G[p][:, cols], up_banks[i][:, 0:width], ALU.mult)\
                .then_inc(s["mul_done"], 1)
        if not known_first(b):
            take_hT(b - 1, 1 - p)
        if not (isinstance(b, int) and b < 2):
            take_output(b - 2)

    for_batches(v, slots)
    take_hT(B - 1, 1)
    take_output(B - 2)
    take_output(B - 1)


def experts1_pool(po, m):
    t, s = r1_tiles(m), m.e1
    po.wait_ge(m.r1["combine_ready"], 1)

    def gate(b, p):
        po.wait_ge(s["mul_done"], 3 * (b + 1))
        h = t.Hn[p][:, 0:E1 * F1].rearrange("p (e f) -> p e f", e=E1)
        w = t.combine[:, bass.ds(b * E1, E1)].unsqueeze(2).to_broadcast([128, E1, F1])
        po.tensor_tensor(h, h, w, ALU.mult).then_inc(s["gated"], 1)

    for_batches(po, gate)


def program(nc, a, out, scratch, layers=6):
    with ExitStack() as ctx:
        place = {}

        def sb(name, shape, dt=F32):
            tile = ctx.enter_context(nc.sbuf_tensor(name, shape, dt))
            place[name] = nc.sbuf_base - shape[1] * mybir.dt.size(dt)
            return tile

        def parts(name, over, column, columns):
            return nc.alloc_sbuf_tensor_at(name, [128, columns], F32R, offset=place[over] + 4 * column)

        def ps(name):
            return ctx.enter_context(nc.psum_tensor(name, [128, 512], F32))

        def sem(name):
            return ctx.enter_context(nc.semaphore(name))

        def sems(prefix, names):
            return {n: sem(f"{prefix}_{n}") for n in names}

        m = Namespace()
        m.w = {name: sb(name, shape) for name, shape in WEIGHTS.items()}
        m.X = sb("X", [128, N])
        m.stats = sb("stats", [128, B * 6])
        m.mean, m.rstd, m.st1, m.st2 = (sb(n, [128, B]) for n in ("mean", "rstd", "st1", "st2"))
        m.xn = sb("xn", [128, 512])
        m.XTs = sb("XTs", [128, 512])
        m.small = sb("small", [128, 96])
        m.arena = sb("arena", [128, 20480])
        m.consts = sb("consts", [128, 3 * 128 + 2 * 16 + 256])
        m.ident, m.same_expert, m.earlier_rows = (m.consts[:, 128 * i:128 * i + 128] for i in range(3))
        m.headmask, m.minus_half = m.consts[:, 384:400], m.consts[:, 400:416]
        m.earlier_group = m.consts[:, 416:672]
        m.identb = sb("identb", [128, 128], BF16)
        m.ones = sb("ones", [1, 128])
        m.w1T, m.w3T, m.w2T = (m.w["W1"][:, FC * 128 * i:FC * 128 * (i + 1)] for i in range(3))
        m.XThi, m.XTlo = (parts(n, "arena", i, N) for n, i in (("XThi", 11264), ("XTlo", 13312)))
        m.wv = m.w["wqkv"][:, 2 * H * HD:]
        m.wv_hi, m.wv_lo = sb("wv_hi", [128, H * HD], F32R), parts("wv_lo", "wqkv", 2 * H * HD, H * HD)
        m.XTv = sb("XTv", [128, 512], F32R)
        m.XTparts = parts("XTparts", "XTs", 0, 512)
        m.W1hi, m.W1lo = parts("W1hi", "arena", 16384, E0 * F0), parts("W1lo", "W1", 0, E0 * F0)
        m.w13hi = parts("w13hi", "W2", 0, 2 * FC * 128)
        m.w1hi, m.w3hi = (m.w13hi[:, FC * 128 * i:FC * 128 * (i + 1)] for i in range(2))
        m.w1lo, m.w3lo = (m.W1lo[:, FC * 128 * i:FC * 128 * (i + 1)] for i in range(2))
        m.mask8 = sb("mask8", [128, B * KL], U8)
        m.maskb = sb("maskb", [128, B * KL], BF16)
        m.KT0hi, m.KT0lo = sb("KT0hi", [128, B * KL], F32R), parts("KT0lo", "arena", 12544, B * KL)
        m.Kblk_parts, m.q_parts = parts("Kblk_parts", "arena", 0, 4 * H * KL), parts("q_parts", "arena", 10752, 4 * T)
        m.KT1 = sb("KT1", [128, B * KL])
        m.V01 = sb("V01", [KL, B * 2 * D])

        m.S, m.TP, m.PJ = ([ps(f"{n}{i}") for i in range(2)] for n in ("S", "TP", "PJ"))
        m.OV, m.MX = ps("OV"), ps("MX")

        m.ld = {n: sem(f"ld_{n}") for n in LOADED}
        m.const_ready, m.stream_ready, m.var_ready, m.rstd_ready = (
            sem(n) for n in ("const_ready", "stream_ready", "var_ready", "rstd_ready"))
        m.moment_chain = sem("moment_chain")
        m.split_hi, m.split_lo = sem("split_hi"), sem("split_lo")
        m.att = [sems(f"att{i}", ATT_SEMS) for i in range(2)]
        m.att_w = [m.w["wqkv"][:, H * HD * i:H * HD * (i + 1)] for i in range(2)]
        m.att_k = [0, 3]
        m.v_save, m.v_load = ([sem(f"v_{n}{p}") for p in range(2)] for n in ("save", "load"))
        m.k0_high = sem("k0_high")
        m.k0_made, m.k0_taken, m.k1_made, m.k1_taken, m.v01_made, m.v01_taken, m.mask_ready, m.zeroed = (
            sem(n) for n in ("k0_made", "k0_taken", "k1_made", "k1_taken", "v01_made", "v01_taken", "mask_ready",
                             "zeroed"))
        m.cr = sems("cr", CR_SEMS)
        m.x1 = sems("x1", X1_SEMS)
        m.rt = sems("rt", RT_SEMS)
        m.r0 = sems("r0", ["chain", "bits", "shifted", "exp_done", "score_ready", "scoreT_in_psum", "counted", "summed",
                           "ties_counted", "ties_summed", "gateT_ready", "gate_in_psum", "gate_ready", "b2_ready"])
        m.e0 = sems("e0", ["up_done", "gelu_done", "down_done", "add_done", "bias_done", "y_saved"])
        m.r1 = sems("r1", ["chain", "score_ready", "combine_ready"])
        m.e1 = sems("e1", ["xT_ready", "gate_done", "up_done", "silu_done", "mul_done", "gated", "hT_in_psum",
                           "hT_act", "hT_dve", "down_done", "res_done"])
        m.b2sel_of = lambda t, b: t.b2sel[:, bass.ds(b * D, D)]
        out_saved = sem("out_saved")

        block = ctx.enter_context(nc.Block())

        @block.sync
        def _(sp):
            loads_sync(sp, m, a)
            att_sync(sp, m, scratch)
            if layers < 6:
                sp.wait_ge(m.stream_ready, layers + 1)
            for g in range(NG):
                if layers == 6:
                    sp.wait_ge(m.e1["res_done"], GRP * (g + 1))
                sp.dma_start(out[:, g * GT:(g + 1) * GT], m.X[:, g * GT:(g + 1) * GT]).then_inc(out_saved, 16)
            sp.wait_ge(out_saved, 16 * NG)

        @block.gpsimd
        def _(po):
            loads_pool(po, m, a)
            moments_pool(po, m, 0)
            att_pool(po, m, 0)
            if layers >= 2:
                attention1_loads_pool(po, m, a)
                moments_pool(po, m, 1)
                cross0_pool(po, m)
            if layers >= 3:
                moments_pool(po, m, 2)
                route0_pool(po, m)
                split_attention1_pool(po, m)
            if layers >= 4:
                clear_keys_pool(po, m, 0)
                moments_pool(po, m, 3)
                clear_keys_pool(po, m, 1)
                experts1_loads_pool(po, m, a)
                att_pool(po, m, 1)
            if layers >= 5:
                moments_pool(po, m, 4)
                split_experts1_pool(po, m)
            if layers >= 6:
                moments_pool(po, m, 5)
                experts1_pool(po, m)

        @block.scalar
        def _(act):
            att_scalar(act, m, 0)
            if layers >= 2:
                context_scalar(act, m)
                cross0_scalar(act, m)
            if layers >= 3:
                router_scalar(act, m, 0)
                route0_scalar(act, m)
                experts0_scalar(act, m)
            if layers >= 4:
                att_scalar(act, m, 1)
            if layers >= 5:
                cross1_scalar(act, m)
            if layers >= 6:
                router_scalar(act, m, 1)
                route1_scalar(act, m)
                experts1_scalar(act, m)

        @block.vector
        def _(v):
            setup_vector(v, m)
            moments_vector(v, m, 0)
            att_vector(v, m, 0)
            if layers >= 2:
                moments_vector(v, m, 1)
                context_vector(v, m)
                cross0_vector(v, m)
            if layers >= 3:
                moments_vector(v, m, 2)
                router_vector(v, m, 0)
                route0_vector(v, m)
                experts0_vector(v, m)
            if layers >= 4:
                moments_vector(v, m, 3)
                att_vector(v, m, 1)
            if layers >= 5:
                moments_vector(v, m, 4)
                cross1_vector(v, m)
            if layers >= 6:
                moments_vector(v, m, 5)
                router_vector(v, m, 1)
                route1_vector(v, m)
                experts1_vector(v, m)

        @block.tensor
        def _(pe):
            att_tensor(pe, m, 0)
            if layers >= 2:
                context_tensor(pe, m)
                cross0_tensor(pe, m)
            if layers >= 3:
                router_tensor(pe, m, 0)
                experts0_tensor(pe, m)
            if layers >= 4:
                att_tensor(pe, m, 1)
            if layers >= 5:
                cross1_tensor(pe, m)
            if layers >= 6:
                router_tensor(pe, m, 1)
                experts1_tensor(pe, m)


WEIGHTS = {
    "wqkv": [128, 3 * H * HD], "w_o": [128, H * HD],
    "ctxT": [128, B * KL], "x0Wk": [128, D], "x1WkT": [128, D], "WvBoth": [128, 2 * D], "x0bk": [128, 1],
    "bvBoth": [128, 2 * D], "x0Wq": [128, D], "x0Wo": [128, D], "x0bq": [128, 1], "x0bo": [1, D],
    "Wr": [128, E0], "W1": [128, E0 * F0], "W2": [128, E0 * F0], "b1T": [128, E0 * C0], "b2rep": [128, D],
    "x1WqT": [128, D], "x1WoT": [128, D], "x1bq": [128, 1], "x1bo": [1, D],
    "gateT": [128, E1],
}


def kernel(**inputs):
    import numpy as np
    import concourse.bacc as bacc
    from concourse.bass_utils import run_bass_kernel_spmd

    i = {k: np.asarray(x) for k, x in inputs.items()}

    def tall(w):
        return w.reshape(-1, 128, w.shape[-1]).transpose(1, 0, 2).reshape(128, -1)

    w1 = np.concatenate([i["L1_ffn_w1_e"].reshape(E1 * F1, D), i["L1_ffn_w1_s"]])
    w3 = np.concatenate([i["L1_ffn_w3_e"].reshape(E1 * F1, D), i["L1_ffn_w3_s"]])
    w2 = np.concatenate([i["L1_ffn_w2_e"].transpose(0, 2, 1).reshape(E1 * F1, D), i["L1_ffn_w2_s"].T])
    r, c = np.arange(128)[:, None], np.arange(128)[None, :]
    same = (r % E0 == c % E0).astype(np.float32)
    earlier = ((r % E0 == c % E0) & (r // E0 < c // E0)).astype(np.float32)
    heads = (r // XHD == np.arange(H)[None, :]).astype(np.float32)
    groups = np.tile((np.arange(G1)[:, None] > np.arange(G1)[None, :]).astype(np.float32).reshape(1, -1), (128, B))
    consts = np.concatenate([np.eye(128, dtype=np.float32), same, earlier, heads,
                             np.full((128, 16), -0.5, np.float32), groups], axis=1)
    a = {
        "x": i["x"].transpose(1, 0, 2).reshape(T, N), "consts": consts,
        "wqT": i["L0_attn_wq"].T, "wkT": i["L0_attn_wk"].T, "wvT": i["L0_attn_wv"].T, "woT": tall(i["L0_attn_wo"].T),
        "ctxT": i["ctx_1024"].transpose(2, 0, 1).reshape(D, B * KL),
        "mask": i["mask_Bx1xSxS2_bk1"][:, 0].transpose(1, 0, 2).reshape(T, B * KL),
        "x0Wk": i["L0_xattn_Wk"], "x1WkT": i["L1_xattn_Wk"].T,
        "WvBoth": np.concatenate([i["L0_xattn_Wv"], i["L1_xattn_Wv"].T], axis=1),
        "x0bk": i["L0_xattn_bk"][:, None],
        "bvBoth": np.tile(np.concatenate([i["L0_xattn_bv"], i["L1_xattn_bv"]])[None, :], (128, 1)),
        "x0Wq": i["L0_xattn_Wq"], "x0Wo": i["L0_xattn_Wo"], "x0bq": i["L0_xattn_bq"][:, None],
        "x0bo": i["L0_xattn_bo"][None, :],
        "Wr": i["L0_ffn_Wr"], "W1": i["L0_ffn_W1"].transpose(1, 0, 2).reshape(D, E0 * F0),
        "W2": tall(i["L0_ffn_W2"].reshape(E0 * F0, D)), "b1T": i["L0_ffn_b1"].reshape(E0 * C0, 128).T,
        "b2rep": np.tile(i["L0_ffn_b2"], (B, 1)),
        "wqkv": i["L1_attn_w_qkv"].transpose(2, 1, 0, 3).reshape(D, 3 * H * HD), "w_o": tall(i["L1_attn_w_o"]),
        "x1WqT": i["L1_xattn_Wq"].T, "x1WoT": i["L1_xattn_Wo"].T, "x1bq": i["L1_xattn_bq"][:, None],
        "x1bo": i["L1_xattn_bo"][None, :],
        "gateT": i["L1_ffn_w_gate"].T, "w1T": w1.T, "w3T": w3.T, "w2T": tall(w2),
    }
    nc = bacc.Bacc("TRN2", target_bir_lowering=False, num_devices=1)
    arrays, aps = {}, {}
    for name, x in a.items():
        x = np.ascontiguousarray(x)
        arrays[f"in_{name}"] = x
        aps[name] = nc.dram_tensor(f"in_{name}", x.shape, mybir.dt.from_np(x.dtype), kind="ExternalInput").ap()
    out = nc.dram_tensor("out", (T, N), F32, kind="ExternalOutput").ap()
    scratch = [nc.dram_tensor(f"v_scratch{p}", (T, H * HD), F32, kind="Internal").ap() for p in range(2)]
    program(nc, aps, out, scratch)
    result = run_bass_kernel_spmd(nc, [arrays], core_ids=[0]).results[0]["out"]
    return np.ascontiguousarray(result.reshape(T, B, D).transpose(1, 0, 2))
```

```python
from contextlib import ExitStack

import concourse.bass as bass
from concourse import mybir

F32 = mybir.dt.float32
F32R = mybir.dt.float32r
BF16 = mybir.dt.bfloat16
U8 = mybir.dt.uint8
U32 = mybir.dt.uint32
ALU = mybir.AluOpType
ACT = mybir.ActivationFunctionType
AX = mybir.AxisListType

B = 16
T = 128
D = 128
KL = 120
N = B * T
H = 16
HD = 64
U = 4
HU = H // U
XHD = D // H
E0, F0, CAP = 8, 512, 512
C0 = F0 // 128
E1, F1 = 16, 64
G1, TOPG, TOPK = 4, 2, 4
FC = E1 * F1 // 128 + 1
EPS = 1e-5
GRP = 4
NG = B // GRP
GT = GRP * T
MASKED = -1.0e15


def need(eng, sem, value):
    if isinstance(value, int) and value <= 0:
        return
    eng.wait_ge(sem, value)


class Chain:

    def __init__(self, eng, sem, base=0):
        self.eng, self.sem, self.base, self.n = eng, sem, base, 0

    def step(self, ins):
        ins.then_inc(self.sem, 1)
        self.n += 1
        self.eng.wait_ge(self.sem, self.base + self.n)


def for_batches(eng, body):
    body(0, 0)
    body(1, 1)
    with eng.Fori(0, (B - 4) // 2) as i:
        body(2 * i + 2, 0)
        body(2 * i + 3, 1)
    body(B - 2, 0)
    body(B - 1, 1)


def for_groups(eng, body):
    body(0)
    with eng.Fori(1, NG - 1) as g:
        body(g)
    body(NG - 1)


def split_product(pe, out, lhsT, rhs, start=True, stop=True):
    pe.matmul(out, lhsT[1], rhs[0], start=start, stop=False)
    pe.matmul(out, lhsT[0], rhs[1], start=False, stop=False)
    return pe.matmul(out, lhsT[0], rhs[0], start=False, stop=stop)


class Namespace:
    pass


def known_first(b):
    return isinstance(b, int) and b == 0


def known_last(b):
    return isinstance(b, int) and b == B - 1




def loads_sync(sp, m, a):
    sp.dma_start(m.X[:, :], a["x"]).then_inc(m.ld["x"], 16)
    sp.dma_start(m.consts[:, :], a["consts"]).then_inc(m.ld["consts"], 16)
    sp.dma_start(m.att_w[0], a["wqT"]).then_inc(m.ld["wqkT"], 16)
    sp.dma_start(m.att_w[1], a["wkT"]).then_inc(m.ld["wqkT"], 16)
    sp.dma_start(m.wv, a["wvT"]).then_inc(m.ld["wvT"], 16)
    sp.dma_start(m.w["w_o"][:, :], a["woT"]).then_inc(m.ld["woT"], 16)


def early_loads_sync(sp, m, a):
    for tile, name in ((m.w["ctxT"], "ctxT"), (m.mask8, "mask")):
        sp.dma_start(tile[:, :], a[name]).then_inc(m.ld["ctxT"], 16)
    for name in ("x0Wk", "x1WkT", "WvBoth", "x0bk", "bvBoth"):
        sp.dma_start(m.w[name][:, :], a[name]).then_inc(m.ld["xkv"], 16)
    for name in ("x0Wq", "x0Wo", "x0bq", "x0bo"):
        sp.dma_start(m.w[name][:, :], a[name]).then_inc(m.ld["x0"], 16)


def late_loads_sync(sp, m, a):
    for name in ("W1", "Wr", "W2", "b1T", "b2rep"):
        sp.dma_start(m.w[name][:, :], a[name]).then_inc(m.ld["ffn0"], 16)
    for name in ("x1WqT", "x1WoT", "x1bq", "x1bo"):
        sp.dma_start(m.w[name][:, :], a[name]).then_inc(m.ld["x1"], 16)


def attention1_loads_pool(po, m, a):
    po.wait_ge(m.stream_ready, 2)
    for tile, name in ((m.w["wqkv"], "wqkv"), (m.w["w_o"], "w_o")):
        po.dma_start(tile[:, :], a[name]).then_inc(m.ld["attn1"], 16)


def experts1_loads_pool(po, m, a):
    po.wait_ge(m.stream_ready, 4)
    for tile, name in ((m.w["gateT"][:, :], "gateT"), (m.w["W1"][:, 0:2 * FC * 128], "w13T"), (m.w2T, "w2T")):
        po.dma_start(tile, a[name]).then_inc(m.ld["ffn1"], 16)


ATT_PIECES, W1_PIECES, FFN1_PIECES = 2, B, 6
ATT_SPLIT = [0, ATT_PIECES + W1_PIECES]
W1_SPLIT, FFN1_SPLIT = ATT_PIECES, 2 * ATT_PIECES + W1_PIECES


def split_attention1_pool(po, m):
    loaded(po, m, "attn1")
    for i in range(ATT_PIECES):
        cols = slice(512 * i, 512 * i + 512)
        split_high(po, m, m.wv[:, cols], m.wv_hi[:, cols])
        po.wait_ge(m.split_hi, ATT_SPLIT[1] + i + 1)
        split_low(po, m, m.wv[:, cols], m.wv_hi[:, cols], m.wv_lo[:, cols])


def split_high(po, m, w, high):
    po.tensor_copy(high, w).then_inc(m.split_hi, 1)


def split_low(po, m, w, high, low):
    po.tensor_tensor(low, w, high, ALU.subtract).then_inc(m.split_lo, 1)


def split_experts1_pool(po, m):
    loaded(po, m, "ffn1")
    width = 2 * FC * 128 // FFN1_PIECES
    for i in range(FFN1_PIECES):
        cols = slice(width * i, width * (i + 1))
        split_high(po, m, m.w["W1"][:, cols], m.w13hi[:, cols])
        po.wait_ge(m.split_hi, FFN1_SPLIT + i + 1)
        split_low(po, m, m.w["W1"][:, cols], m.w13hi[:, cols], m.W1lo[:, cols])


LOADED = {"x": 16, "consts": 16, "wqkT": 32, "wvT": 16, "woT": 16, "ctxT": 32, "xkv": 80, "x0": 64,
          "ffn0": 80, "attn1": 32, "x1": 64, "ffn1": 48}


def loaded(eng, m, name):
    eng.wait_ge(m.ld[name], LOADED[name])


def setup_vector(v, m):
    loaded(v, m, "consts")
    v.tensor_copy(m.identb[:, :], m.ident).then_inc(m.const_ready, 1)
    v.memset(m.ones[:, :], 1.0).then_inc(m.const_ready, 1)
    loaded(v, m, "x")
    for b in range(B):
        ins = v.bn_stats(m.stats[:, 6 * b:6 * b + 6], m.X[:, b * D:(b + 1) * D])
        if b == EARLY - 1:
            ins.then_inc(m.const_ready, 1)
            v.wait_ge(m.const_ready, 3)
            moments_vector(v, m, 0, 0)
    ins.then_inc(m.stream_ready, 1)


EARLY = 12


def part_columns(part):
    return (slice(0, EARLY), slice(EARLY, B))[part]


def moments_vector(v, m, k, part):
    cols, base = part_columns(part), 12 * k + 6 * part
    mean, st1, st2 = m.mean[:, cols], m.st1[:, cols], m.st2[:, cols]
    if part == 1:
        v.wait_ge(m.stream_ready, k + 1)
    st = m.stats[:, :].rearrange("p (b s) -> p s b", s=6)[:, :, cols]
    v.tensor_tensor(mean, st[:, 1], st[:, 4], ALU.add).then_inc(m.moment_chain, 1)
    v.tensor_tensor(st1, st[:, 1], st[:, 4], ALU.subtract).then_inc(m.moment_chain, 1)
    v.tensor_tensor(st2, st[:, 2], st[:, 5], ALU.add).then_inc(m.moment_chain, 1)
    v.wait_ge(m.moment_chain, base + 3)
    v.tensor_tensor(st1, st1, st1, ALU.mult).then_inc(m.moment_chain, 1)
    v.tensor_scalar(st2, st2, 1.0 / D, EPS, ALU.mult, ALU.add).then_inc(m.moment_chain, 1)
    v.tensor_scalar(mean, mean, 0.5, None, ALU.mult).then_inc(m.moment_chain, 1)
    v.wait_ge(m.moment_chain, base + 6)
    v.scalar_tensor_tensor(st2, st1, 0.25, st2, ALU.mult, ALU.add).then_inc(m.var_ready, 1)


def moments_pool(po, m, k, part):
    po.wait_ge(m.var_ready, 2 * k + part + 1)
    if k == 0:
        loaded(po, m, "consts")
    cols = part_columns(part)
    po.tensor_tensor(m.rstd[:, cols], m.st2[:, cols], m.minus_half[:, cols], ALU.pow).then_inc(m.rstd_ready, 1)


def normalise(v, m, k, b, dst):
    if isinstance(b, int) and b in (0, 3):
        v.wait_ge(m.rstd_ready, 2 * k + 1 + b // 3)
    return v.tensor_scalar(dst, m.X[:, bass.ds(b * D, D)], m.mean[:, bass.ds(b, 1)], m.rstd[:, bass.ds(b, 1)],
                           ALU.subtract, ALU.mult)


def context_keys_tensor(pe, m, g):
    if g == 0:
        loaded(pe, m, "ctxT")
        loaded(pe, m, "xkv")
        pe.wait_ge(m.att[0]["v_evac"], 2 * B)
    cols = slice(GRP * KL * g, GRP * KL * (g + 1))
    for w, bank, made, taken in ((m.w["x0Wk"], m.PJ[0], m.k0_made, m.k0_taken),
                                 (m.w["x1WkT"], m.PJ[1], m.k1_made, m.k1_taken)):
        need(pe, taken, g)
        pe.matmul(bank[:, 0:GRP * KL], w[:, :], m.w["ctxT"][:, cols], start=True, stop=True).then_inc(made, 1)


def context_keys_scalar(act, m, g):
    act.wait_ge(m.k1_made, g + 1)
    act.activation(m.KT1[:, GRP * KL * g:GRP * KL * (g + 1)], m.PJ[1][:, 0:GRP * KL], ACT.Copy).then_inc(m.k1_taken, 1)


def context_keys_vector(v, m, g):
    if g == 0:
        loaded(v, m, "ctxT")
        loaded(v, m, "xkv")
        v.tensor_scalar(m.maskb[:, :], m.mask8[:, :], MASKED, None, ALU.mult).then_inc(m.mask_ready, 1)
    cols = slice(GRP * KL * g, GRP * KL * (g + 1))
    v.wait_ge(m.k0_made, g + 1)
    v.tensor_scalar(m.KT0hi[:, cols], m.PJ[0][:, 0:GRP * KL], m.w["x0bk"][:, 0:1], None, ALU.add).then_inc(m.k0_high, 1)
    v.wait_ge(m.k0_high, g + 1)
    v.scalar_tensor_tensor(m.KT0lo[:, cols], m.PJ[0][:, 0:GRP * KL], m.w["x0bk"][:, 0:1], m.KT0hi[:, cols],
                           ALU.add, ALU.subtract).then_inc(m.k0_taken, 1)


def context_values_tensor(pe, m, pairs):
    for i in pairs:
        if i < 2:
            pe.wait_ge((m.k0_taken, m.k1_taken)[i], NG)
        need(pe, m.v01_taken, i - 1)
        for b in (2 * i, 2 * i + 1):
            ins = pe.matmul(m.PJ[i % 2][0:KL, 256 * (b % 2):256 * (b % 2) + 256], m.w["ctxT"][:, KL * b:KL * (b + 1)],
                            m.w["WvBoth"][:, :], start=True, stop=True)
        ins.then_inc(m.v01_made, 1)


def context_values_vector(v, m, pairs):
    for i in pairs:
        v.wait_ge(m.v01_made, i + 1)
        bias = m.w["bvBoth"][0:KL, :].unsqueeze(1).to_broadcast([KL, 2, 2 * D])
        v.tensor_tensor(m.V01[:, 512 * i:512 * i + 512].rearrange("k (b d) -> k b d", b=2),
                        m.PJ[i % 2][0:KL, :].rearrange("k (b d) -> k b d", b=2), bias, ALU.add)\
            .then_inc(m.v01_taken, 1)


ATT_SEMS = ["xn_ready", "xT_in_psum", "xT_ready", "xTv_ready", "q_proj", "k_proj", "v_proj", "q_ready", "k_ready", "v_evac",
            "scores_ready", "negmax_ready", "exp_done", "inverse_ready", "probs_ready", "probsT_in_psum",
            "probsT_ready", "av_done", "av_evac", "out_done", "res_done"]


def att_tiles(m):
    t = Namespace()
    ar = m.arena
    t.Q = [ar[:, 0:2048], ar[:, 2048:4096]]
    t.K = [ar[:, 4096:6144], ar[:, 6144:8192]]
    t.V = [ar[:, 8192:9216], ar[:, 9216:10240]]
    t.Vst = [ar[:, 10240:11264], ar[:, 11264:12288]]
    t.P = [ar[:, 12288 + 512 * i:12800 + 512 * i] for i in range(U)]
    t.PT = [ar[:, 14336 + 512 * i:14848 + 512 * i] for i in range(2)]
    t.OT = [ar[:, 15360 + 1024 * i:16384 + 1024 * i] for i in range(2)]
    t.negmax = [m.small[:, 4 * u:4 * u + 4] for u in range(U)]
    t.total = [m.small[:, 16 + 4 * u:20 + 4 * u] for u in range(U)]
    t.inverse = [m.small[:, 32 + 4 * u:36 + 4 * u] for u in range(U)]
    t.xn = [m.xn[:, 0:D], m.xn[:, D:2 * D]]
    t.xT = [m.XTs[:, 0:T], m.XTs[:, T:2 * T]]
    t.xTv = [(m.XTv[:, i * T:(i + 1) * T], m.XTv[:, (2 + i) * T:(3 + i) * T]) for i in range(2)]
    return t


PIECES = {0: [("q", 0), ("q", 1)], 1: [("k", 0)], 2: [("k", 1), ("v", 0)], 3: [("v", 1)]}


def att_tensor(pe, m, layer):
    s, t = m.att[layer], att_tiles(m)
    wq, wk = m.att_w

    def transpose_tokens(b, p):
        pe.wait_ge(s["xn_ready"], b + 1)
        need(pe, s["res_done"], b - 3)
        need(pe, s["xTv_ready"], b)
        pe.transpose(m.MX[:, 0:T], t.xn[p], m.ident).then_inc(s["xT_in_psum"], 1)

    def project(b, p, kind, g):
        bank = m.PJ[g]
        if kind == "q":
            if g == 0:
                pe.wait_ge(s["xT_ready"], b + 1)
            need(pe, s["v_evac"], 2 * b - 1 + g)
        elif kind == "k":
            pe.wait_ge(s["q_ready"], 2 * b + 1 + g)
        else:
            pe.wait_ge(s["k_ready"], 2 * b + 1 + g)
        if kind == "v":
            if known_first(b):
                pe.wait_ge(m.split_lo, ATT_SPLIT[layer] + 1 + g)
            pe.wait_ge(s["xTv_ready"], b + 1)
            cols = slice(512 * g, 512 * g + 512)
            split_product(pe, bank[:, :], t.xTv[p], (m.wv_hi[:, cols], m.wv_lo[:, cols])).then_inc(s["v_proj"], 1)
            return
        w, done = (wq, s["q_proj"]) if kind == "q" else (wk, s["k_proj"])
        for c in range(4):
            chunk = 4 * g + c
            ins = pe.matmul(bank[:, c * T:(c + 1) * T], w[:, chunk * 128:(chunk + 1) * 128], t.xT[p],
                            start=True, stop=True)
        ins.then_inc(done, 1)

    def scores(b, p, u):
        n = U * b + u
        if u == 0:
            pe.wait_ge(s["q_ready"], 2 * (b + 1))
            pe.wait_ge(s["k_ready"], 2 * (b + 1))
        need(pe, s["exp_done"], n - 1)
        bank = m.S[u % 2]
        if layer == 0:
            for j in range(HU):
                h = HU * u + j
                ins = pe.matmul(bank[:, j * 128:(j + 1) * 128], t.Q[p][0:HD, h * 128:(h + 1) * 128],
                                t.K[p][0:HD, h * 128:(h + 1) * 128], start=True, stop=True)
        else:
            for j in range(2):
                pair = 2 * u + j
                ins = pe.matmul(bank[:, j * 256:(j + 1) * 256], t.Q[p][:, pair * 128:(pair + 1) * 128],
                                t.K[p][:, pair * 256:(pair + 1) * 256], start=True, stop=True)
        ins.then_inc(s["scores_ready"], 1)

    def transpose_probs(n, u):
        pe.wait_ge(s["probs_ready"], n + 1)
        need(pe, s["probsT_ready"], n - 1)
        for j in range(HU):
            ins = pe.transpose(m.TP[u % 2][:, j * 128:(j + 1) * 128], t.P[u][:, j * 128:(j + 1) * 128], m.ident)
        ins.then_inc(s["probsT_in_psum"], 1)

    def values(b, p, u):
        n = U * b + u
        pe.wait_ge(s["probsT_ready"], n + 1)
        need(pe, s["av_evac"], n)
        if u == 0:
            if layer == 0:
                pe.wait_ge(m.v_load[p], 8 * (b - p) + 16)
            else:
                pe.wait_ge(s["v_evac"], 2 * (b + 1))
        PT, V = t.PT[u % 2], t.V[p]
        for j in range(HU):
            h = HU * u + j
            if layer == 0:
                for par in range(2):
                    ins = pe.matmul(m.OV[par * 64:par * 64 + 64, j * 64:j * 64 + 64], V[:, h * HD:(h + 1) * HD],
                                    PT[:, j * 128 + par * 64:j * 128 + par * 64 + 64], start=True, stop=True)
            else:
                par = j % 2
                ins = pe.matmul(m.OV[par * 64:par * 64 + 64, (j // 2) * 128:(j // 2) * 128 + 128],
                                V[:, h * HD:(h + 1) * HD], PT[:, j * 128:(j + 1) * 128], start=True, stop=True)
        ins.then_inc(s["av_done"], 1)

    def output(b, p):
        pe.wait_ge(s["av_evac"], U * (b + 1))
        need(pe, s["xTv_ready"], min(b + 4, B) if isinstance(b, int) else b + 4)
        need(pe, s["res_done"], b)
        for c in range(8):
            ins = pe.matmul(m.MX[:, 0:D], t.OT[p][:, c * T:(c + 1) * T], m.w["w_o"][:, c * D:(c + 1) * D],
                            start=(c == 0), stop=(c == 7))
        ins.then_inc(s["out_done"], 1)

    loaded(pe, m, "consts")
    transpose_tokens(0, 0)
    for name in (("wqkT", "woT") if layer == 0 else ("attn1",)):
        loaded(pe, m, name)
    for u in range(U):
        for kind, g in PIECES[u]:
            project(0, 0, kind, g)
    transpose_tokens(1, 1)

    def slots(b, p):
        for u in range(U):
            scores(b, p, u)
            if not known_last(b):
                for kind, g in PIECES[u]:
                    project(b + 1, 1 - p, kind, g)
            n = U * b + u
            if not (known_first(b) and u < 1):
                transpose_probs(n - 1, (u - 1) % U)
            if not (known_first(b) and u < 2):
                values(b if u >= 2 else b - 1, p if u >= 2 else 1 - p, (u - 2) % U)
            if u == 1 and not (isinstance(b, int) and b + 2 >= B):
                transpose_tokens(b + 2, p)
            if u == 2 and not known_first(b):
                output(b - 1, 1 - p)
            if layer == 0 and known_last(b):
                context_keys_tensor(pe, m, u)

    for_batches(pe, slots)
    values(B - 1, 1, U - 2)
    if layer == 0:
        context_values_tensor(pe, m, range(0, 4))
    transpose_probs(U * B - 1, U - 1)
    if layer == 0:
        context_values_tensor(pe, m, range(4, 6))
    values(B - 1, 1, U - 1)
    if layer == 0:
        context_values_tensor(pe, m, range(6, B // 2))
    output(B - 1, 1)


def att_scalar(act, m, layer):
    s, t = m.att[layer], att_tiles(m)
    scale = HD ** -0.5

    def exps(b, p, u):
        n = U * b + u
        act.wait_ge(s["negmax_ready"], n + 1)
        need(act, s["probsT_in_psum"], n - 3)
        for j in range(HU):
            ins = act.activation(t.P[u][:, j * 128:(j + 1) * 128], m.S[u % 2][:, j * 128:(j + 1) * 128], ACT.Exp,
                                 bias=t.negmax[u][:, j:j + 1], accum_out=t.total[u][:, j:j + 1])
        ins.then_inc(s["exp_done"], 1)

    def take_q(b, p, g):
        act.wait_ge(s["q_proj"], 2 * b + g + 1)
        if layer == 0:
            for par in range(2):
                src = m.PJ[g][par * 64:par * 64 + 64, :].rearrange("d (c h t) -> d c h t", c=4, t=8)
                dst = t.Q[p][0:HD, :].rearrange("d (h r c t) -> d r c h t", h=H, r=2, c=8)[:, par, 4 * g:4 * g + 4]
                ins = act.activation(dst, src, ACT.Copy, scale=scale)
        else:
            ins = act.activation(t.Q[p][:, 512 * g:512 * g + 512], m.PJ[g][:, :], ACT.Copy, scale=scale)
        ins.then_inc(s["q_ready"], 1)

    def take_v(b, p, g):
        act.wait_ge(s["v_proj"], 2 * b + g + 1)
        if layer == 0:
            if not (isinstance(b, int) and b < 2):
                act.wait_ge(m.v_save[p], 8 * (b - p))
            dst = t.Vst[p]
        else:
            dst = t.V[p]
        act.activation(dst[:, 512 * g:512 * g + 512], m.PJ[g][:, :], ACT.Copy).then_inc(s["v_evac"], 1)

    def take_probsT(n, u):
        act.wait_ge(s["probsT_in_psum"], n + 1)
        need(act, s["av_done"], n - 1)
        act.activation(t.PT[u % 2], m.TP[u % 2][:, :], ACT.Copy).then_inc(s["probsT_ready"], 1)

    def take_xT(b, p):
        act.wait_ge(s["xT_in_psum"], b + 1)
        act.activation(t.xT[p], m.MX[:, 0:T], ACT.Copy)
        act.activation(t.xTv[p][0], m.MX[:, 0:T], ACT.Copy).then_inc(s["xT_ready"], 1)

    def piece(b, p, kind, g):
        if kind == "q":
            take_q(b, p, g)
        elif kind == "v":
            take_v(b, p, g)

    act.preload_act_table(ACT.Exp)
    take_xT(0, 0)
    if layer == 0:
        loaded(act, m, "wvT")
        for i in range(ATT_PIECES):
            cols = slice(512 * i, 512 * i + 512)
            act.activation(m.wv_hi[:, cols], m.wv[:, cols], ACT.Copy).then_inc(m.split_hi, 1)
    for u in range(U):
        for kind, g in PIECES[u]:
            piece(0, 0, kind, g)
    take_xT(1, 1)

    def slots(b, p):
        for u in range(U):
            exps(b, p, u)
            if not known_last(b):
                for kind, g in PIECES[u]:
                    piece(b + 1, 1 - p, kind, g)
            if not (known_first(b) and u < 1):
                take_probsT(U * b + u - 1, (u - 1) % U)
            if u == 1 and not (isinstance(b, int) and b + 2 >= B):
                take_xT(b + 2, p)
            if layer == 0 and known_last(b):
                context_keys_scalar(act, m, u)

    for_batches(act, slots)
    take_probsT(U * B - 1, U - 1)


def att_vector(v, m, layer):
    s, t = m.att[layer], att_tiles(m)

    def take_k(b, p, g):
        v.wait_ge(s["k_proj"], 2 * b + g + 1)
        if layer == 1 and isinstance(b, int) and b < 2:
            v.wait_ge(m.zeroed, 2 + b)
        for par in range(2):
            if layer == 0:
                src = m.PJ[g][par * 64:par * 64 + 64, :].rearrange("d (c h t) -> d c h t", c=4, t=8)
                dst = t.K[p][0:HD, :].rearrange("d (h t c r) -> d r c h t", h=H, t=8, r=2)[:, par, 4 * g:4 * g + 4]
            else:
                src = m.PJ[g][par * 64:par * 64 + 64, :].rearrange("d (c j) -> d c j", c=4)
                dst = t.K[p][par * 64:par * 64 + 64, :].rearrange("d (c r j) -> d r c j", r=2, j=128)[
                    :, par, 4 * g:4 * g + 4]
            ins = v.tensor_copy(dst, src)
        ins.then_inc(s["k_ready"], 1)

    def maxima(b, p, u):
        n = U * b + u
        v.wait_ge(s["scores_ready"], n + 1)
        v.tensor_reduce(t.negmax[u], m.S[u % 2][:, :].rearrange("p (j k) -> p j k", j=HU), AX.X, ALU.max,
                        negate=True).then_inc(s["negmax_ready"], 1)

    def inverse(b, p, u):
        n = U * b + u
        v.wait_ge(s["exp_done"], n + 1)
        v.reciprocal(t.inverse[u], t.total[u]).then_inc(s["inverse_ready"], 1)

    def take_av(b, p, u):
        n = U * b + u
        v.wait_ge(s["av_done"], n + 1)
        if layer == 0:
            src = m.OV[:, 0:256].rearrange("p (h c t) -> p h c t", h=HU, c=8)
            dst = t.OT[p].rearrange("p (c h t) -> p h c t", c=8, t=8)[:, HU * u:HU * u + HU]
        else:
            src, dst = m.OV[:, 0:256], t.OT[p][:, 256 * u:256 * u + 256]
        v.tensor_copy(dst, src).then_inc(s["av_evac"], 1)

    def take_output(b, p):
        v.wait_ge(s["out_done"], b + 1)
        x = m.X[:, bass.ds(b * D, D)]
        v.tensor_tensor(x, x, m.MX[:, 0:D], ALU.add).then_inc(s["res_done"], 1)
        v.wait_ge(s["res_done"], b + 1)
        return v.bn_stats(m.stats[:, bass.ds(6 * b, 6)], x)

    def tokens(b, p):
        need(v, s["xT_in_psum"], b - 1)
        normalise(v, m, m.att_k[layer], b, t.xn[p]).then_inc(s["xn_ready"], 1)

    def low_tokens(b, p):
        v.wait_ge(s["xT_ready"], b + 1)
        v.tensor_tensor(t.xTv[p][1], m.MX[:, 0:T], t.xTv[p][0], ALU.subtract).then_inc(s["xTv_ready"], 1)

    tokens(0, 0)
    tokens(1, 1)
    low_tokens(0, 0)
    if layer == 0:
        for i in range(ATT_PIECES):
            cols = slice(512 * i, 512 * i + 512)
            v.wait_ge(m.split_hi, i + 1)
            v.tensor_tensor(m.wv_lo[:, cols], m.wv[:, cols], m.wv_hi[:, cols], ALU.subtract).then_inc(m.split_lo, 1)
    take_k(0, 0, 0)
    take_k(0, 0, 1)
    low_tokens(1, 1)

    def slots(b, p):
        for u in range(U):
            if u == 2 and not (isinstance(b, int) and b + 2 >= B):
                low_tokens(b + 2, p)
            maxima(b, p, u)
            if not (known_first(b) and u < 3):
                take_av(b if u == 3 else b - 1, p if u == 3 else 1 - p, (u - 3) % U)
            if not known_last(b):
                for kind, g in PIECES[u]:
                    if kind == "k":
                        take_k(b + 1, 1 - p, g)
            if u == 3 and not known_first(b):
                take_output(b - 1, 1 - p)
            inverse(b, p, u)
            if u == 3 and isinstance(b, int) and b == B - 2:
                moments_vector(v, m, m.att_k[layer] + 1, 0)
            if u == 0 and not (isinstance(b, int) and b + 2 >= B):
                tokens(b + 2, p)
            if layer == 0 and known_last(b):
                context_keys_vector(v, m, u)

    moments_vector(v, m, m.att_k[layer], 1)
    for_batches(v, slots)
    take_av(B - 1, 1, 1)
    take_av(B - 1, 1, 2)
    if layer == 0:
        context_values_vector(v, m, range(0, 6))
    take_av(B - 1, 1, 3)
    if layer == 0:
        context_values_vector(v, m, range(6, B // 2))
    take_output(B - 1, 1).then_inc(m.stream_ready, 1)


def clear_keys_pool(po, m, p):
    po.wait_ge(m.stream_ready, 4)
    po.memset(att_tiles(m).K[p], 0.0).then_inc(m.zeroed, 1)


def att_pool(po, m, layer):
    s, t = m.att[layer], att_tiles(m)

    def divide(b, p, u):
        n = U * b + u
        po.wait_ge(s["inverse_ready"], n + 1)
        P = t.P[u].rearrange("p (j k) -> p j k", j=HU)
        po.tensor_tensor(P, P, t.inverse[u].unsqueeze(2).to_broadcast([128, HU, 128]), ALU.mult)\
            .then_inc(s["probs_ready"], 1)

    def slots(b, p):
        for u in range(U):
            divide(b, p, u)

    for_batches(po, slots)


def att_sync(sp, m, scratch):
    s, t = m.att[0], att_tiles(m)

    def move(b, p):
        sp.wait_ge(s["v_evac"], 2 * (b + 1))
        sp.dma_start(scratch[p], t.Vst[p]).then_inc(m.v_save[p], 16)
        sp.wait_ge(m.v_save[p], 8 * (b - p) + 16)
        sp.dma_start(t.V[p].rearrange("p (h d) -> p h d", h=H),
                     scratch[p].rearrange("(h t) (c d) -> (t c) h d", h=H, d=HD)).then_inc(m.v_load[p], 16)

    for_batches(sp, move)


def scale_bias(v, m, name, width):
    v.tensor_scalar(m.w[name][:, 0:1], m.w[name][:, 0:1], width ** -0.5, None, ALU.mult).then_inc(m.bias_scaled, 1)


CR_SEMS = ["xn_ready", "xT_in_psum", "xT_ready", "q_proj", "q_high", "q_ready", "kblk_ready", "vblk_ready",
           "scores_ready", "negmax_ready", "exp_done", "probsT_in_psum", "probsT_ready", "av_done",
           "inv_done", "inv_ready", "invT_in_psum", "invT_ready", "oT_ready", "out_done", "res_done"]


def cr_tiles(m):
    t = Namespace()
    ar = m.arena
    t.Kblk = [(m.Kblk_parts[:, H * KL * p:H * KL * (p + 1)], m.Kblk_parts[:, H * KL * (2 + p):H * KL * (3 + p)])
              for p in range(2)]
    t.P = [ar[:, 7680 + 512 * u:7680 + 512 * u + HU * KL] for u in range(U)]
    t.PT = [ar[:, 9728:10240], ar[:, 10240:10752]]
    t.qT = [(m.q_parts[:, i * T:(i + 1) * T], m.q_parts[:, (2 + i) * T:(3 + i) * T]) for i in range(2)]
    t.invT, t.oT = ar[:, 11264:11392], ar[:, 11392:11520]
    t.Vblk = [ar[0:KL, 11520 + 512 * p:12032 + 512 * p] for p in range(2)]
    t.total = [m.small[:, 0:16], m.small[:, 16:32]]
    t.inverse = m.small[:, 32:48]
    t.spread = ar[:, 14464:14592]
    t.negmax = [m.small[:, 48 + 4 * u:52 + 4 * u] for u in range(U)]
    t.q = [ar[:, 14592 + T * p:14592 + T * (p + 1)] for p in range(2)]
    t.xn = [m.xn[:, 0:D], m.xn[:, D:2 * D]]
    t.xT = m.XTs[:, 0:T]
    t.O = [m.OV, m.PJ[1]]
    return t


def cross0_tensor(pe, m):
    s, t = m.cr, cr_tiles(m)

    def transpose_tokens(b, p):
        pe.wait_ge(s["xn_ready"], b + 1)
        need(pe, s["q_ready"], b)
        pe.transpose(m.PJ[0][:, 0:T], t.xn[p], m.ident).then_inc(s["xT_in_psum"], 1)

    def project(b):
        pe.wait_ge(s["xT_ready"], b + 1)
        pe.matmul(m.PJ[0][:, 0:T], m.w["x0Wq"][:, :], t.xT, start=True, stop=True).then_inc(s["q_proj"], 1)

    def scores(b, p, u):
        n = U * b + u
        if u == 0:
            pe.wait_ge(s["q_ready"], b + 1)
            pe.wait_ge(s["kblk_ready"], b + 1)
        need(pe, s["exp_done"], n - 1)
        mask = m.maskb[:, bass.ds(b * KL, KL)].unsqueeze(1).to_broadcast([128, HU, KL])
        pe.matmul(m.S[u % 2][:, 0:HU * KL].rearrange("p (j k) -> p j k", j=HU), m.identb[:, :], mask,
                  start=True, stop=False)
        cols = slice(HU * KL * u, HU * KL * (u + 1))
        split_product(pe, m.S[u % 2][:, 0:HU * KL], t.qT[p], (t.Kblk[p][0][:, cols], t.Kblk[p][1][:, cols]),
                      start=False).then_inc(s["scores_ready"], 1)

    def transpose_probs(n, u):
        pe.wait_ge(s["exp_done"], n + 1)
        need(pe, s["probsT_ready"], n - 1)
        for j in range(HU):
            ins = pe.transpose(m.TP[u % 2][0:KL, j * 128:(j + 1) * 128], t.P[u][:, j * KL:(j + 1) * KL], m.ident)
        ins.then_inc(s["probsT_in_psum"], 1)

    def values(b, p, u):
        n = U * b + u
        pe.wait_ge(s["probsT_ready"], n + 1)
        if u == 0:
            pe.wait_ge(s["vblk_ready"], b + 1)
            need(pe, s["oT_ready"], b - 1)
        for j in range(HU):
            ins = pe.matmul(t.O[p][32 * u:32 * u + 32, 0:T], t.Vblk[p][:, 32 * (HU * u + j):32 * (HU * u + j) + 32],
                            t.PT[u % 2][0:KL, j * 128:(j + 1) * 128], start=(j == 0), stop=(j == HU - 1))
        ins.then_inc(s["av_done"], 1)

    def transpose_inverse(b):
        pe.wait_ge(s["inv_ready"], b + 1)
        need(pe, s["res_done"], b)
        pe.transpose(m.MX[:, 0:T], t.spread, m.ident)\
            .then_inc(s["invT_in_psum"], 1)

    def output(b):
        pe.wait_ge(s["oT_ready"], b + 1)
        pe.matmul(m.MX[:, 0:D], m.ones[0:1, :], m.w["x0bo"][0:1, :], start=True, stop=False)
        pe.matmul(m.MX[:, 0:D], t.oT, m.w["x0Wo"][:, :], start=False, stop=True).then_inc(s["out_done"], 1)

    loaded(pe, m, "x0")
    pe.wait_ge(m.mask_ready, 1)
    pe.wait_ge(m.const_ready, 2)
    pe.wait_ge(m.v01_taken, B // 2)
    pe.wait_ge(m.k0_taken, NG)
    pe.wait_ge(m.k1_taken, NG)
    transpose_tokens(0, 0)
    project(0)

    def slots(b, p):
        for u in range(U):
            n = U * b + u
            scores(b, p, u)
            if not (known_first(b) and u < 2):
                transpose_probs(n - 2, (u - 2) % U)
            if not (known_first(b) and u < 3):
                values(b if u == 3 else b - 1, p if u == 3 else 1 - p, (u - 3) % U)
            if u == 0 and not known_last(b):
                transpose_tokens(b + 1, 1 - p)
            if u == 2 and not known_first(b):
                transpose_inverse(b - 1)
            if u == 1 and not known_last(b):
                project(b + 1)
            if u == 0 and not (isinstance(b, int) and b < 2):
                output(b - 2)

    for_batches(pe, slots)
    transpose_probs(U * B - 2, U - 2)
    values(B - 1, 1, U - 3)
    output(B - 2)
    transpose_probs(U * B - 1, U - 1)
    values(B - 1, 1, U - 2)
    transpose_inverse(B - 1)
    values(B - 1, 1, U - 1)
    output(B - 1)


def w1_piece(b):
    return bass.ds(b * (E0 * F0 // B), E0 * F0 // B)


def cross0_scalar(act, m):
    s, t = m.cr, cr_tiles(m)

    def exps(b, p, u):
        n = U * b + u
        act.wait_ge(s["negmax_ready"], n + 1)
        need(act, s["probsT_in_psum"], n - 3)
        if u == 0:
            need(act, s["inv_done"], b - 1)
        for j in range(HU):
            ins = act.activation(t.P[u][:, j * KL:(j + 1) * KL], m.S[u % 2][:, j * KL:(j + 1) * KL], ACT.Exp,
                                 bias=t.negmax[u][:, j:j + 1],
                                 accum_out=t.total[p][:, HU * u + j:HU * u + j + 1])
        ins.then_inc(s["exp_done"], 1)

    def take_xT(b):
        act.wait_ge(s["xT_in_psum"], b + 1)
        act.activation(t.xT, m.PJ[0][:, 0:T], ACT.Copy).then_inc(s["xT_ready"], 1)

    def take_q(b, p):
        act.wait_ge(s["q_proj"], b + 1)
        bias, scale = m.w["x0bq"][:, 0:1], XHD ** -0.5
        act.activation(t.q[p], m.PJ[0][:, 0:T], ACT.Identity, bias=bias, scale=scale)
        act.activation(t.qT[p][0], m.PJ[0][:, 0:T], ACT.Identity, bias=bias, scale=scale).then_inc(s["q_high"], 1)

    def spread_inverse(b):
        act.wait_ge(s["inv_done"], b + 1)
        need(act, s["invT_in_psum"], b)
        act.activation(t.spread.rearrange("p (h d) -> p h d", h=H), t.inverse.unsqueeze(2).to_broadcast([128, H, XHD]),
                       ACT.Copy).then_inc(s["inv_ready"], 1)

    def take_inverse(b):
        act.wait_ge(s["invT_in_psum"], b + 1)
        need(act, s["oT_ready"], b)
        act.activation(t.invT, m.MX[:, 0:T], ACT.Copy).then_inc(s["invT_ready"], 1)

    def place_values(b, p):
        need(act, s["av_done"], U * (b - 1))
        for j in range(HU):
            own = t.Vblk[p].rearrange("k (u c) -> k u c", u=U)[:, :, (32 + XHD) * j:(32 + XHD) * j + XHD]
            head = m.V01[0:KL, bass.ds(b * 2 * D, D)].rearrange("k (u c) -> k u c", u=U)[:, :, XHD * j:XHD * (j + 1)]
            ins = act.activation(own, head, ACT.Copy)
        ins.then_inc(s["vblk_ready"], 1)

    loaded(act, m, "x0")
    act.preload_act_table(ACT.Exp)
    take_xT(0)
    act.wait_ge(m.bias_scaled, 1)
    take_q(0, 0)
    act.wait_ge(m.v01_taken, B // 2)
    act.wait_ge(m.zeroed, 1)
    place_values(0, 0)

    def slots(b, p):
        for u in range(U):
            exps(b, p, u)
            if u == 1 and not known_first(b):
                spread_inverse(b - 1)
            if u == 0 and not known_last(b):
                take_xT(b + 1)
            if u == 2 and not known_first(b):
                take_inverse(b - 1)
            if u == 1 and not known_last(b):
                take_q(b + 1, 1 - p)
            if u == 3 and not known_last(b):
                place_values(b + 1, 1 - p)
            if u == 2:
                if known_first(b):
                    loaded(act, m, "ffn0")
                act.activation(m.W1hi[:, w1_piece(b)], m.w["W1"][:, w1_piece(b)], ACT.Copy).then_inc(m.split_hi, 1)

    for_batches(act, slots)
    spread_inverse(B - 1)
    take_inverse(B - 1)


def cross0_vector(v, m):
    s, t = m.cr, cr_tiles(m)

    def maxima(b, u):
        n = U * b + u
        v.wait_ge(s["scores_ready"], n + 1)
        v.tensor_reduce(t.negmax[u], m.S[u % 2][:, 0:HU * KL].rearrange("p (j k) -> p j k", j=HU), AX.X, ALU.max,
                        negate=True).then_inc(s["negmax_ready"], 1)

    def take_probsT(n, u):
        v.wait_ge(s["probsT_in_psum"], n + 1)
        need(v, s["av_done"], n - 1)
        v.tensor_copy(t.PT[u % 2][0:KL, :], m.TP[u % 2][0:KL, :]).then_inc(s["probsT_ready"], 1)

    def tokens(b, p):
        need(v, s["xT_in_psum"], b - 1)
        normalise(v, m, 1, b, t.xn[p]).then_inc(s["xn_ready"], 1)

    def low_q(b, p):
        v.wait_ge(s["q_high"], b + 1)
        v.tensor_tensor(t.qT[p][1], t.q[p], t.qT[p][0], ALU.subtract).then_inc(s["q_ready"], 1)

    def inverses(b, p):
        v.wait_ge(s["exp_done"], U * (b + 1))
        need(v, s["inv_ready"], b)
        v.reciprocal(t.inverse, t.total[p]).then_inc(s["inv_done"], 1)

    def divide(b, p):
        v.wait_ge(s["av_done"], U * (b + 1))
        v.wait_ge(s["invT_ready"], b + 1)
        need(v, s["out_done"], b)
        v.tensor_tensor(t.oT, t.O[p][:, 0:T], t.invT, ALU.mult).then_inc(s["oT_ready"], 1)

    def take_output(b):
        v.wait_ge(s["out_done"], b + 1)
        x = m.X[:, bass.ds(b * D, D)]
        v.tensor_tensor(x, x, m.MX[:, 0:D], ALU.add).then_inc(s["res_done"], 1)
        v.wait_ge(s["res_done"], b + 1)
        return v.bn_stats(m.stats[:, bass.ds(6 * b, 6)], x)

    loaded(v, m, "x0")
    scale_bias(v, m, "x0bq", XHD)
    tokens(0, 0)
    tokens(1, 1)
    low_q(0, 0)

    def slots(b, p):
        for u in range(U):
            n = U * b + u
            maxima(b, u)
            if u == 3 and not known_first(b):
                divide(b - 1, 1 - p)
            if not (known_first(b) and u < 2):
                take_probsT(n - 2, (u - 2) % U)
            if u == 1 and not known_first(b):
                inverses(b - 1, 1 - p)
            if u == 1 and not (isinstance(b, int) and b + 2 >= B):
                tokens(b + 2, p)
            if u == 2 and not known_last(b):
                low_q(b + 1, 1 - p)
            if u == 1 and known_last(b):
                moments_vector(v, m, 2, 0)
            if u == 0 and not (isinstance(b, int) and b < 2):
                take_output(b - 2)

    moments_vector(v, m, 1, 1)
    for_batches(v, slots)
    take_probsT(U * B - 2, U - 2)
    take_output(B - 2)
    inverses(B - 1, 1)
    take_probsT(U * B - 1, U - 1)
    divide(B - 1, 1)
    take_output(B - 1).then_inc(m.stream_ready, 1)


def cross0_pool(po, m, a):
    s, t = m.cr, cr_tiles(m)

    def block(b, p):
        for part, keys in zip(t.Kblk[p], (m.KT0hi, m.KT0lo)):
            ins = po.tensor_tensor(part.rearrange("p (h k) -> p h k", h=H),
                                   keys[:, bass.ds(b * KL, KL)].unsqueeze(1).to_broadcast([128, H, KL]),
                                   m.headmask.unsqueeze(2).to_broadcast([128, H, KL]), ALU.mult)
        ins.then_inc(s["kblk_ready"], 1)

    def blocks(b, p):
        if not (isinstance(b, int) and b < 2):
            po.wait_ge(m.split_hi, W1_SPLIT + b - 1)
            po.wait_ge(s["scores_ready"], U * (b - 1))
            block(b, p)
            w1_low(b - 2)

    def w1_low(b):
        split_low(po, m, m.w["W1"][:, w1_piece(b)], m.W1hi[:, w1_piece(b)], m.W1lo[:, w1_piece(b)])

    moments_pool(po, m, 1, 0)
    po.wait_ge(m.att[0]["scores_ready"], U * B)
    po.wait_ge(m.k0_taken, NG)
    block(0, 0)
    block(1, 1)
    po.wait_ge(m.stream_ready, 2)
    po.memset(m.arena[:, 11520:12544], 0.0).then_inc(m.zeroed, 1)
    moments_pool(po, m, 1, 1)
    attention1_loads_pool(po, m, a)
    loaded(po, m, "ffn0")
    for_batches(po, blocks)
    po.wait_ge(m.split_hi, W1_SPLIT + B)
    w1_low(B - 2)
    w1_low(B - 1)
    moments_pool(po, m, 2, 0)


X1_SEMS = ["xn_ready", "xT_in_psum", "xT_ready", "q_proj", "q_ready", "scores_ready", "negmax_ready",
           "exp_done", "probsT_in_psum", "probsT_ready", "av_done", "inv_done", "o_ready", "oT_in_psum", "oT_ready",
           "out_done", "res_done"]
STAGES = 8


def x1_tiles(m):
    t = Namespace()
    ar = m.arena
    t.xn, t.xT, t.qT, t.P, t.PT, t.o, t.oT = ([ar[:, 256 * i + 128 * p:256 * i + 128 * p + 128] for p in range(2)]
                                              for i in range(7))
    t.negmax, t.total, t.inverse = ([m.small[:, 2 * i + p:2 * i + p + 1] for p in range(2)] for i in range(3))
    t.X, t.Q, t.S, t.PTp, t.AV, t.OTp, t.Y = (bank[:, 0:128] for bank in (m.MX, m.PJ[0], m.S[0], m.TP[0], m.OV,
                                                                          m.PJ[1], m.TP[1]))
    return t


def for_steps(eng, stages):
    def step(b, parity):
        for k in reversed(range(STAGES)):
            if stages[k] is not None and not (isinstance(b, int) and not 0 <= b + STAGES - 1 - k < B):
                stages[k](b + STAGES - 1 - k, (parity + STAGES - 1 - k) % 2)

    for b in range(1 - STAGES, 2):
        step(b, b % 2)
    with eng.Fori(0, (B - STAGES) // 2 - 1) as i:
        step(2 * i + 2, 0)
        step(2 * i + 3, 1)
    for b in range(B - STAGES, B):
        step(b, b % 2)


def cross1_tensor(pe, m):
    s, t = m.x1, x1_tiles(m)
    loaded(pe, m, "x1")

    def transpose_tokens(b, p):
        pe.wait_ge(s["xn_ready"], b + 1)
        need(pe, s["xT_ready"], b)
        pe.transpose(t.X, t.xn[p], m.ident).then_inc(s["xT_in_psum"], 1)

    def project(b, p):
        pe.wait_ge(s["xT_ready"], b + 1)
        need(pe, s["q_ready"], b)
        pe.matmul(t.Q, m.w["x1WqT"][:, :], t.xT[p], start=True, stop=True).then_inc(s["q_proj"], 1)

    def scores(b, p):
        pe.wait_ge(s["q_ready"], b + 1)
        need(pe, s["exp_done"], b)
        pe.matmul(t.S[:, 0:KL], t.qT[p], m.KT1[:, bass.ds(b * KL, KL)], start=True, stop=True)\
            .then_inc(s["scores_ready"], 1)

    def transpose_probs(b, p):
        pe.wait_ge(s["exp_done"], b + 1)
        need(pe, s["probsT_ready"], b)
        pe.transpose(t.PTp[0:KL, :], t.P[p][:, 0:KL], m.ident).then_inc(s["probsT_in_psum"], 1)

    def values(b, p):
        pe.wait_ge(s["probsT_ready"], b + 1)
        need(pe, s["o_ready"], b)
        pe.matmul(t.AV, t.PT[p][0:KL, :], m.V01[0:KL, bass.ds(b * 2 * D + D, D)], start=True, stop=True)\
            .then_inc(s["av_done"], 1)

    def transpose_o(b, p):
        pe.wait_ge(s["o_ready"], b + 1)
        need(pe, s["oT_ready"], b)
        pe.transpose(t.OTp, t.o[p], m.ident).then_inc(s["oT_in_psum"], 1)

    def output(b, p):
        pe.wait_ge(s["oT_ready"], b + 1)
        need(pe, s["res_done"], b)
        pe.matmul(t.Y, m.ones[0:1, :], m.w["x1bo"][0:1, :], start=True, stop=False)
        pe.matmul(t.Y, t.oT[p], m.w["x1WoT"][:, :], start=False, stop=True).then_inc(s["out_done"], 1)

    for_steps(pe, [None, transpose_tokens, project, scores, transpose_probs, values, transpose_o, output])


def cross1_scalar(act, m):
    s, t = m.x1, x1_tiles(m)
    loaded(act, m, "x1")

    def take_xT(b, p):
        act.wait_ge(s["xT_in_psum"], b + 1)
        need(act, s["q_proj"], b - 1)
        act.activation(t.xT[p], t.X, ACT.Copy).then_inc(s["xT_ready"], 1)

    def take_q(b, p):
        act.wait_ge(s["q_proj"], b + 1)
        need(act, s["scores_ready"], b - 1)
        act.activation(t.qT[p], t.Q, ACT.Identity, bias=m.w["x1bq"][:, 0:1], scale=D ** -0.5)\
            .then_inc(s["q_ready"], 1)

    def exps(b, p):
        act.wait_ge(s["negmax_ready"], b + 1)
        need(act, s["probsT_in_psum"], b - 1)
        act.activation(t.P[p][:, 0:KL], t.S[:, 0:KL], ACT.Exp, bias=t.negmax[p],
                       accum_out=t.total[p]).then_inc(s["exp_done"], 1)

    def take_probsT(b, p):
        act.wait_ge(s["probsT_in_psum"], b + 1)
        need(act, s["av_done"], b - 1)
        act.activation(t.PT[p][0:KL, :], t.PTp[0:KL, :], ACT.Copy).then_inc(s["probsT_ready"], 1)

    def take_oT(b, p):
        act.wait_ge(s["oT_in_psum"], b + 1)
        need(act, s["out_done"], b - 1)
        act.activation(t.oT[p], t.OTp, ACT.Copy).then_inc(s["oT_ready"], 1)

    act.wait_ge(m.bias_scaled, 2)
    for_steps(act, [None, take_xT, take_q, exps, take_probsT, None, take_oT, None])


def cross1_vector(v, m):
    s, t = m.x1, x1_tiles(m)

    def tokens(b, p):
        need(v, s["xT_in_psum"], b - 1)
        normalise(v, m, 4, b, t.xn[p]).then_inc(s["xn_ready"], 1)
        if isinstance(b, int) and b == 2:
            moments_vector(v, m, 4, 1)

    def maxima(b, p):
        v.wait_ge(s["scores_ready"], b + 1)
        v.tensor_reduce(t.negmax[p], t.S[:, 0:KL], AX.X, ALU.max, negate=True).then_inc(s["negmax_ready"], 1)

    def inverses(b, p):
        v.wait_ge(s["exp_done"], b + 1)
        v.reciprocal(t.inverse[p], t.total[p]).then_inc(s["inv_done"], 1)

    def take_values(b, p):
        v.wait_ge(s["av_done"], b + 1)
        v.wait_ge(s["inv_done"], b + 1)
        need(v, s["oT_in_psum"], b - 1)
        v.tensor_scalar(t.o[p], t.AV, t.inverse[p], None, ALU.mult).then_inc(s["o_ready"], 1)

    def take_output(b, p):
        v.wait_ge(s["out_done"], b + 1)
        x = m.X[:, bass.ds(b * D, D)]
        v.tensor_tensor(x, x, t.Y, ALU.add).then_inc(s["res_done"], 1)
        v.wait_ge(s["res_done"], b + 1)
        ins = v.bn_stats(m.stats[:, bass.ds(6 * b, 6)], x)
        if isinstance(b, int) and b == B - 3:
            moments_vector(v, m, 5, 0)
        if known_last(b):
            ins.then_inc(m.stream_ready, 1)

    loaded(v, m, "x1")
    scale_bias(v, m, "x1bq", D)
    for_steps(v, [tokens, None, None, maxima, inverses, take_values, None, take_output])


RT_SEMS = ["xn_ready", "xT_in_psum", "xT_ready", "xT_kept", "logits_done", "logits_ready"]


def rt_tiles(m):
    t = Namespace()
    t.xn = [m.xn[:, 0:D], m.xn[:, D:2 * D]]
    t.xT = [m.XTs[:, 0:T], m.XTs[:, T:2 * T]]
    t.X = [m.MX[:, 0:T], m.PJ[0][:, 0:T]]
    t.L = [m.OV, m.PJ[1]]
    return t


def router_tensor(pe, m, layer):
    s, t = m.rt, rt_tiles(m)
    w, E = ((m.w["Wr"], E0), (m.w["gateT"], E1))[layer]
    loaded(pe, m, ("ffn0", "ffn1")[layer])

    def transpose_tokens(b, p):
        k = b + B * layer
        pe.wait_ge(s["xn_ready"], k + 1)
        need(pe, s["xT_kept"], k - 1)
        pe.transpose(t.X[p], t.xn[p], m.ident).then_inc(s["xT_in_psum"], 1)

    def slots(b, p):
        k = b + B * layer
        if not known_last(b):
            transpose_tokens(b + 1, 1 - p)
        pe.wait_ge(s["xT_ready"], k + 1)
        need(pe, s["logits_ready"], k - 1)
        pe.matmul(t.L[p][:, 0:E], t.xT[p], w[:, :], start=True, stop=True).then_inc(s["logits_done"], 1)

    transpose_tokens(0, 0)
    for_batches(pe, slots)


def router_scalar(act, m, layer):
    s, t = m.rt, rt_tiles(m)

    def slots(b, p):
        k = b + B * layer
        act.wait_ge(s["xT_in_psum"], k + 1)
        need(act, s["logits_done"], k - 1)
        act.activation(m.XThi[:, bass.ds(b * T, T)], t.X[p], ACT.Copy)
        act.activation(t.xT[p], t.X[p], ACT.Copy).then_inc(s["xT_ready"], 1)

    for_batches(act, slots)


def router_vector(v, m, layer):
    s, t = m.rt, rt_tiles(m)
    E = (E0, E1)[layer]
    LG = m.arena[:, 6400:6400 + B * E]

    def tokens(b, p):
        k = b + B * layer
        need(v, s["xT_in_psum"], k - 1)
        normalise(v, m, (2, 5)[layer], b, t.xn[p]).then_inc(s["xn_ready"], 1)

    def slots(b, p):
        k = b + B * layer
        v.wait_ge(s["xT_ready"], k + 1)
        cols = bass.ds(b * T, T)
        v.tensor_tensor(m.XTlo[:, cols], t.X[p], m.XThi[:, cols], ALU.subtract).then_inc(s["xT_kept"], 1)
        if not (isinstance(b, int) and b + 2 >= B):
            tokens(b + 2, p)
        if known_first(b):
            moments_vector(v, m, (2, 5)[layer], 1)
        else:
            take_logits(b - 1, 1 - p)

    def take_logits(b, p):
        v.wait_ge(s["logits_done"], b + B * layer + 1)
        v.tensor_copy(LG[:, bass.ds(b * E, E)], t.L[p][:, 0:E]).then_inc(s["logits_ready"], 1)

    tokens(0, 0)
    tokens(1, 1)
    for_batches(v, slots)
    take_logits(B - 1, 1)


def r0_tiles(m):
    t = Namespace()
    ar = m.arena
    t.H = [ar[:, 0:2048], ar[:, 2048:4096]]
    t.Y = [ar[:, i:i + 512] for i in (8192, 8704, 9216, 9728, 10240, 10752, 15360, 15872)]
    t.gateT = ar[:, 4096:4224]
    t.gate = ar[:, 4224:4352]
    t.b2sel = ar[:, 4352:6400]
    t.score = ar[:, 6400:6528]
    t.scoreT = ar[:, 7168:7296]
    t.junk, t.above, t.equal, t.rank = (ar[:, 7296 + 128 * i:7424 + 128 * i] for i in range(4))
    t.threshold, t.candidate, t.bit, t.count, t.kept, t.room = (m.small[:, i:i + 1] for i in range(6))
    t.counts = m.small[:, 6:8]
    t.row = m.small[:, 16:32]
    return t


BITS = 30


def route0_vector(v, m):
    t, s = r0_tiles(m), m.r0
    score = t.score.rearrange("p (b e) -> p b e", e=E0)
    row = t.row.unsqueeze(2).to_broadcast([128, B, E0])
    c = Chain(v, s["chain"])
    v.wait_ge(m.rt["logits_ready"], B)
    c.step(v.tensor_reduce(t.row, score, AX.X, ALU.max))
    v.tensor_tensor(score, score, row, ALU.subtract).then_inc(s["shifted"], 1)
    v.wait_ge(s["exp_done"], 1)
    c.step(v.tensor_reduce(t.row, score, AX.X, ALU.add))
    c.step(v.reciprocal(t.row, t.row))
    v.tensor_tensor(score, score, row, ALU.mult).then_inc(s["score_ready"], 1)
    c.step(v.memset(t.threshold.bitcast(U32), 0))
    c.step(v.memset(t.bit.bitcast(U32), 1 << (BITS - 1)))
    v.wait_ge(s["scoreT_in_psum"], 1)
    c.step(v.tensor_copy(t.scoreT, m.MX[:, 0:128]))
    def keep_or_drop_bit(i):
        d = Chain(v, s["bits"], 4 * i)
        d.step(v.tensor_tensor(t.candidate.bitcast(U32), t.threshold.bitcast(U32), t.bit.bitcast(U32), ALU.bitwise_or))
        v.tensor_scalar(t.junk, t.scoreT, t.candidate, 0.0, ALU.is_ge, ALU.add, accum_out=t.count)\
            .then_inc(s["counted"], 1)
        d.step(v.tensor_scalar(t.bit.bitcast(U32), t.bit.bitcast(U32), 1, None, ALU.logical_shift_right))
        v.wait_ge(s["summed"], i + 1)
        d.step(v.tensor_scalar(t.kept, m.MX[:, 0:1], float(CAP), t.candidate, ALU.is_ge, ALU.mult))
        d.step(v.tensor_tensor(t.threshold, t.threshold, t.kept, ALU.max))

    with v.Fori(0, BITS // 2) as i:
        keep_or_drop_bit(2 * i)
        keep_or_drop_bit(2 * i + 1)
    c.step(v.tensor_scalar(t.above, t.scoreT, t.threshold, 0.0, ALU.is_gt, ALU.add, accum_out=t.counts[:, 0:1]))
    v.tensor_scalar(t.equal, t.scoreT, t.threshold, 0.0, ALU.is_equal, ALU.add, accum_out=t.counts[:, 1:2])\
        .then_inc(s["ties_counted"], 1)
    v.wait_ge(s["ties_summed"], 1)
    c.step(v.tensor_scalar(t.room, m.MX[:, 0:1], -1.0, float(CAP), ALU.mult, ALU.add))
    c.step(v.tensor_copy(t.count, m.MX[:, 1:2]))
    c.step(v.memset(t.junk, 1.0))
    c.step(v.tensor_tensor_scan(t.rank, t.junk, t.equal, t.count, ALU.mult, ALU.add))
    c.step(v.tensor_scalar(t.rank, t.rank, t.room, None, ALU.is_le))
    c.step(v.tensor_tensor(t.rank, t.rank, t.equal, ALU.mult))
    c.step(v.tensor_tensor(t.rank, t.rank, t.above, ALU.add))
    v.tensor_tensor(t.gateT, t.rank, t.scoreT, ALU.mult).then_inc(s["gateT_ready"], 1)
    v.wait_ge(s["gate_in_psum"], 1)
    v.tensor_copy(t.gate, m.MX[:, 0:128]).then_inc(s["gate_ready"], 1)


def route0_scalar(act, m):
    t, s = r0_tiles(m), m.r0
    act.wait_ge(s["shifted"], 1)
    act.activation(t.score, t.score, ACT.Exp).then_inc(s["exp_done"], 1)


def route0_pool(po, m):
    t = r0_tiles(m)
    po.wait_ge(m.stream_ready, 3)
    loaded(po, m, "ffn0")
    po.tensor_tensor(t.b2sel.rearrange("p (b d) -> p b d", b=B), m.w["b2rep"][:, :].unsqueeze(1).to_broadcast([128, B, D]),
                     m.headmask.unsqueeze(2).to_broadcast([128, B, D]), ALU.mult).then_inc(m.r0["b2_ready"], 1)


BIAS_AFTER = 4


def added(g, e):
    return (E0 + 1) * g + e + (1 if e <= BIAS_AFTER else 2)


def experts0_tensor(pe, m):
    t, s, r = r0_tiles(m), m.e0, m.r0
    hidden_banks = [m.S[0], m.S[1], m.TP[0], m.TP[1]]

    def up(g, e, c):
        n = E0 * g + e
        need(pe, s["gelu_done"], C0 * n - (C0 - 1) + c)
        w, x = slice((e * C0 + c) * 128, (e * C0 + c + 1) * 128), bass.ds(g * GT, GT)
        split_product(pe, hidden_banks[c][:, :], (m.W1hi[:, w], m.W1lo[:, w]), (m.XThi[:, x], m.XTlo[:, x]))\
            .then_inc(s["up_done"], 1)

    def down(g, e, i):
        n = E0 * g + e
        H = t.H[e % 2]
        if i == 0:
            pe.wait_ge(s["gelu_done"], C0 * (n + 1))
            if isinstance(g, int) and n < E0 + 2:
                need(pe, s["y_saved"], n - 1)
            else:
                pe.wait_ge(s["add_done"], added(g, e - 2) if e >= 2 else added(g - 1, e - 2 + E0))
        for c in range(C0):
            ins = pe.matmul(m.PJ[e % 2][:, i * D:(i + 1) * D], H[:, c * GT + i * T:c * GT + (i + 1) * T],
                            m.w["W2"][:, (e * C0 + c) * D:(e * C0 + c + 1) * D], start=(c == 0), stop=(c == C0 - 1))
        if i == GRP - 1:
            ins.then_inc(s["down_done"], 1)

    def biases(g):
        need(pe, s["add_done"], added(g - 1, BIAS_AFTER) + 1)
        for i in range(GRP):
            ins = pe.matmul(m.OV[:, i * D:(i + 1) * D], t.gateT, m.b2sel_of(t, GRP * g + i), start=True, stop=True)
        ins.then_inc(s["bias_done"], 1)

    def threshold_step(k):
        if k < BITS:
            pe.wait_ge(r["counted"], k + 1)
            pe.matmul(m.MX[:, 0:1], m.same_expert, t.count, start=True, stop=True).then_inc(r["summed"], 1)
        elif k == BITS:
            pe.wait_ge(r["ties_counted"], 1)
            pe.matmul(m.MX[:, 0:1], m.same_expert, t.counts[:, 0:1], start=True, stop=True)
            pe.matmul(m.MX[:, 1:2], m.earlier_rows, t.counts[:, 1:2], start=True, stop=True)\
                .then_inc(r["ties_summed"], 1)

    pe.wait_ge(m.rt["xT_kept"], B)
    pe.wait_ge(m.rt["logits_ready"], B)
    pe.wait_ge(m.split_lo, W1_SPLIT + W1_PIECES)
    for c in range(C0):
        if c == 2:
            pe.wait_ge(r["score_ready"], 1)
            pe.transpose(m.MX[:, 0:128], t.score, m.ident).then_inc(r["scoreT_in_psum"], 1)
        up(0, 0, c)
    for e in range(E0):
        for c in range(C0):
            threshold_step(C0 * e + c)
            up(0 if e < E0 - 1 else 1, (e + 1) % E0, c)
            down(0, e, c)
    pe.wait_ge(r["gateT_ready"], 1)
    pe.transpose(m.MX[:, 0:128], t.gateT, m.ident).then_inc(r["gate_in_psum"], 1)
    pe.wait_ge(r["b2_ready"], 1)
    biases(0)

    def group(g):
        for e in range(E0):
            if e < E0 - 1 or not (isinstance(g, int) and g == NG - 1):
                for c in range(C0):
                    up(g if e < E0 - 1 else g + 1, (e + 1) % E0, c)
            for i in range(GRP):
                down(g, e, i)
            if e == BIAS_AFTER:
                biases(g)

    group(1)
    with pe.Fori(2, NG - 1) as g:
        group(g)
    group(NG - 1)


def experts0_scalar(act, m):
    t, s = r0_tiles(m), m.e0
    hidden_banks = [m.S[0], m.S[1], m.TP[0], m.TP[1]]
    act.preload_act_table(ACT.Gelu)

    def gelus(g, e):
        n = E0 * g + e
        for c in range(C0):
            act.wait_ge(s["up_done"], C0 * n + c + 1)
            if c == 0:
                need(act, s["down_done"], n - 1)
            act.activation(t.H[e % 2][:, c * GT:(c + 1) * GT], hidden_banks[c][:, :], ACT.Gelu,
                           bias=m.w["b1T"][:, e * C0 + c:e * C0 + c + 1]).then_inc(s["gelu_done"], 1)

    gelus(0, 0)
    for e in range(E0):
        if e < E0 - 1:
            gelus(0, e + 1)
        act.wait_ge(s["down_done"], e + 1)
        act.activation(t.Y[e], m.PJ[e % 2][:, :], ACT.Copy).then_inc(s["y_saved"], 1)

    def group(g):
        for e in range(E0):
            gelus(g, e)

    with act.Fori(1, NG - 1) as g:
        group(g)
    group(NG - 1)


def experts0_vector(v, m):
    t, s = r0_tiles(m), m.e0

    def group(g):
        first = isinstance(g, int) and g == 0
        for e in range(E0):
            v.wait_ge(s["y_saved"] if first else s["down_done"], E0 * g + e + 1)
            need(v, s["add_done"], added(g, e) - 1)
            for i in range(GRP):
                x = m.X[:, bass.ds((GRP * g + i) * D, D)]
                y = (t.Y[e] if first else m.PJ[e % 2])[:, i * D:(i + 1) * D]
                ins = v.scalar_tensor_tensor(x, y, t.gate[:, bass.ds((GRP * g + i) * E0 + e, 1)], x, ALU.mult, ALU.add)
            ins.then_inc(s["add_done"], 1)
            if e == 2 and isinstance(g, int) and g == NG - 1:
                moments_vector(v, m, 3, 0)
            if e == BIAS_AFTER:
                v.wait_ge(s["bias_done"], g + 1)
                v.wait_ge(s["add_done"], added(g, e))
                x = m.X[:, bass.ds(g * GT, GT)]
                v.tensor_tensor(x, x, m.OV[:, :], ALU.add).then_inc(s["add_done"], 1)
        v.wait_ge(s["add_done"], (E0 + 1) * (g + 1))
        for i in range(GRP):
            ins = v.bn_stats(m.stats[:, bass.ds(6 * (GRP * g + i), 6)], m.X[:, bass.ds((GRP * g + i) * D, D)])
        return ins

    v.wait_ge(m.r0["gate_ready"], 1)
    group(0)
    with v.Fori(1, NG - 1) as g:
        group(g)
    group(NG - 1).then_inc(m.stream_ready, 1)


def r1_tiles(m):
    t = Namespace()
    ar = m.arena
    t.score = ar[:, 6400:6656]
    t.a, t.b, t.c, t.d = (ar[:, 6656 + 64 * i:6720 + 64 * i] for i in range(4))
    t.pair, t.tie = ar[:, 6912:7168], ar[:, 7168:7424]
    t.padded = ar[:, 7424:7808]
    t.marked = ar[:, 7808:8192]
    t.top = ar[:, 8192:8320]
    t.combine = ar[:, 8320:8576]
    t.row = m.small[:, 0:16]
    t.G = [ar[:, 0:1152], ar[:, 1152:2304]]
    t.Hn = [ar[:, 2304:3456], ar[:, 3456:4608]]
    t.HT = [ar[:, 8704:9856], ar[:, 9856:11008]]
    t.xT = [(m.XTparts[:, i * T:(i + 1) * T], m.XTparts[:, (2 + i) * T:(3 + i) * T]) for i in range(2)]
    return t


def route1_vector(v, m):
    t, s = r1_tiles(m), m.r1
    c = Chain(v, s["chain"])
    v.wait_ge(s["score_ready"], 1)
    ex = t.score.rearrange("p (g e) -> p e g", e=4)
    c.step(v.tensor_tensor(t.a, ex[:, 0], ex[:, 1], ALU.max))
    c.step(v.tensor_tensor(t.b, ex[:, 0], ex[:, 1], ALU.min))
    c.step(v.tensor_tensor(t.c, ex[:, 2], ex[:, 3], ALU.max))
    c.step(v.tensor_tensor(t.d, ex[:, 2], ex[:, 3], ALU.min))
    c.step(v.tensor_tensor(t.b, t.b, t.d, ALU.max))
    c.step(v.tensor_tensor(t.d, t.a, t.c, ALU.min))
    c.step(v.tensor_tensor(t.b, t.b, t.d, ALU.max))
    c.step(v.tensor_tensor(t.a, t.a, t.c, ALU.max))
    c.step(v.tensor_tensor(t.a, t.a, t.b, ALU.add))
    other = t.a.rearrange("p (b o) -> p b o", o=G1).unsqueeze(2).to_broadcast([128, B, G1, G1])
    own = t.a.rearrange("p (b o) -> p b o", o=G1).unsqueeze(3).to_broadcast([128, B, G1, G1])
    pair = t.pair.rearrange("p (b g o) -> p b g o", g=G1, o=G1)
    tie = t.tie.rearrange("p (b g o) -> p b g o", g=G1, o=G1)
    c.step(v.tensor_tensor(pair, other, own, ALU.is_gt))
    c.step(v.tensor_tensor(tie, other, own, ALU.is_equal))
    c.step(v.tensor_tensor(t.tie, t.tie, m.earlier_group, ALU.mult))
    c.step(v.tensor_tensor(t.pair, t.pair, t.tie, ALU.add))
    c.step(v.tensor_reduce(t.b, t.pair.rearrange("p (g o) -> p g o", o=G1), AX.X, ALU.add))
    c.step(v.tensor_scalar(t.b, t.b, float(TOPG), 4.0, ALU.is_lt, ALU.mult))
    c.step(v.tensor_scalar(t.b, t.b, -4.0, None, ALU.add))
    padded = t.padded.rearrange("p (b e) -> p b e", e=24)
    marked = t.marked.rearrange("p (b e) -> p b e", e=24)
    score = t.score.rearrange("p (b e) -> p b e", e=E1)
    c.step(v.memset(t.padded, -9.0))
    c.step(v.tensor_copy(marked[:, :, 0:E1].rearrange("p b (g e) -> p b g e", e=4),
                         t.b.rearrange("p (b g) -> p b g", g=G1).unsqueeze(3).to_broadcast([128, B, G1, 4])))
    c.step(v.tensor_tensor(padded[:, :, 0:E1], score, marked[:, :, 0:E1], ALU.add))
    for b in range(B):
        ins = v.max(t.top[:, 8 * b:8 * b + 8], t.padded[:, 24 * b:24 * b + 24])
    c.step(ins)
    c.step(v.memset(t.top.rearrange("p (b e) -> p b e", e=8)[:, :, TOPK:8], -9.0))
    for b in range(B):
        ins = v.match_replace(t.marked[:, 24 * b:24 * b + 24], t.top[:, 8 * b:8 * b + 8],
                              t.padded[:, 24 * b:24 * b + 24], -16.0)
    c.step(ins)
    combine = t.combine.rearrange("p (b e) -> p b e", e=E1)
    row = t.row.unsqueeze(2).to_broadcast([128, B, E1])
    c.step(v.tensor_scalar(combine, marked[:, :, 0:E1], -16.0, None, ALU.is_equal))
    c.step(v.tensor_tensor(t.combine, t.combine, t.score, ALU.mult))
    c.step(v.tensor_reduce(t.row, combine, AX.X, ALU.add))
    c.step(v.tensor_scalar(t.row, t.row, 1e-6, None, ALU.add))
    c.step(v.reciprocal(t.row, t.row))
    v.tensor_tensor(combine, combine, row, ALU.mult).then_inc(s["combine_ready"], 1)


def route1_scalar(act, m):
    t = r1_tiles(m)
    act.wait_ge(m.rt["logits_ready"], 2 * B)
    act.activation(t.score, t.score, ACT.Sigmoid).then_inc(m.r1["score_ready"], 1)


def experts1_tensor(pe, m):
    t, s = r1_tiles(m), m.e1
    gate_banks, up_banks = m.S, m.TP

    def up(b, p):
        pe.wait_ge(s["xT_ready"], b + 1)
        for i in range(2):
            for j, (bank, read, done) in enumerate(((gate_banks[i], s["silu_done"], s["gate_done"]),
                                                    (up_banks[i], s["mul_done"], s["up_done"]))):
                need(pe, read, 3 * (b - 1) + i + 1)
                cols = slice(1024 * j + 512 * i, 1024 * j + 512 * i + 512)
                split_product(pe, bank[:, :], t.xT[p], (m.w13hi[:, cols], m.w13lo[:, cols])).then_inc(done, 1)
        need(pe, s["mul_done"], 3 * b)
        cols = slice(2048, 2304)
        split_product(pe, m.MX[:, 0:256], t.xT[p], (m.w13hi[:, cols], m.w13lo[:, cols])).then_inc(s["gate_done"], 1)

    def transpose_hidden(b, p, part):
        pe.wait_ge(s["gated"], b + 1)
        bank = m.PJ[part % 2]
        if part == 0:
            need(pe, s["hT_act"], 2 * b)
        elif part == 1:
            need(pe, s["hT_dve"], b)
        else:
            pe.wait_ge(s["hT_act"], 2 * b + 1)
        chunks = range(4 * part, min(4 * part + 4, FC))
        for i, c in enumerate(chunks):
            ins = pe.transpose(bank[:, i * T:(i + 1) * T], t.Hn[p][:, c * 128:(c + 1) * 128], m.ident)
        ins.then_inc(s["hT_in_psum"], 1)

    def down(b, p):
        pe.wait_ge(s["hT_act"], 2 * (b + 1))
        pe.wait_ge(s["hT_dve"], b + 1)
        need(pe, s["res_done"], b)
        for c in range(FC):
            ins = pe.matmul(m.OV[:, 0:D], t.HT[p][:, c * T:(c + 1) * T], m.w2T[:, c * D:(c + 1) * D],
                            start=(c == 0), stop=(c == FC - 1))
        ins.then_inc(s["down_done"], 1)

    def slots(b, p):
        up(b, p)
        if not known_first(b):
            transpose_hidden(b - 1, 1 - p, 0)
            transpose_hidden(b - 1, 1 - p, 1)
        if not (isinstance(b, int) and b < 2):
            down(b - 2, p)
        if not known_first(b):
            transpose_hidden(b - 1, 1 - p, 2)

    pe.wait_ge(m.split_lo, FFN1_SPLIT + FFN1_PIECES)
    for_batches(pe, slots)
    transpose_hidden(B - 1, 1, 0)
    transpose_hidden(B - 1, 1, 1)
    down(B - 2, 0)
    transpose_hidden(B - 1, 1, 2)
    down(B - 1, 1)


def experts1_scalar(act, m):
    t, s = r1_tiles(m), m.e1
    gate_banks = [m.S[0], m.S[1], m.MX[:, 0:128]]
    act.preload_act_table(ACT.Silu)
    act.wait_ge(m.rt["xT_kept"], 2 * B)

    def take_x(b, p):
        need(act, s["gate_done"], 3 * (b - 1))
        act.activation(t.xT[p][0], m.XThi[:, bass.ds(b * T, T)], ACT.Copy)
        act.activation(t.xT[p][1], m.XTlo[:, bass.ds(b * T, T)], ACT.Copy).then_inc(s["xT_ready"], 1)

    def take_hT(b, p, part):
        act.wait_ge(s["hT_in_psum"], 3 * b + part + 1)
        need(act, s["down_done"], b - 1)
        n = 4 if part == 0 else 1
        act.activation(t.HT[p][:, 4 * part * T:(4 * part + n) * T], m.PJ[0][:, 0:n * T], ACT.Copy)\
            .then_inc(s["hT_act"], 1)

    take_x(0, 0)

    def slots(b, p):
        if not known_last(b):
            take_x(b + 1, 1 - p)
        for i in range(3):
            width = 512 if i < 2 else 128
            act.wait_ge(s["gate_done"], 3 * b + i + 1)
            if i == 0:
                need(act, s["mul_done"], 3 * (b - 1))
            act.activation(t.G[p][:, 512 * i:512 * i + width], gate_banks[i][:, 0:width], ACT.Silu)\
                .then_inc(s["silu_done"], 1)
        if not known_first(b):
            take_hT(b - 1, 1 - p, 0)
            take_hT(b - 1, 1 - p, 2)

    for_batches(act, slots)
    take_hT(B - 1, 1, 0)
    take_hT(B - 1, 1, 2)


def experts1_vector(v, m):
    t, s = r1_tiles(m), m.e1
    up_banks = [m.TP[0], m.TP[1], m.MX[:, 128:256]]

    def take_hT(b, p):
        v.wait_ge(s["hT_in_psum"], 3 * b + 2)
        need(v, s["down_done"], b - 1)
        v.tensor_copy(t.HT[p][:, 4 * T:8 * T], m.PJ[1][:, :]).then_inc(s["hT_dve"], 1)

    def take_output(b):
        v.wait_ge(s["down_done"], b + 1)
        x = m.X[:, bass.ds(b * D, D)]
        v.tensor_tensor(x, x, m.OV[:, 0:D], ALU.add).then_inc(s["res_done"], 1)

    def slots(b, p):
        for i in range(3):
            width = 512 if i < 2 else 128
            if i < 2:
                v.wait_ge(s["up_done"], 2 * b + i + 1)
            v.wait_ge(s["silu_done"], 3 * b + i + 1)
            if i == 0:
                need(v, s["hT_in_psum"], 3 * (b - 1))
            cols = slice(512 * i, 512 * i + width)
            v.tensor_tensor(t.Hn[p][:, cols], t.G[p][:, cols], up_banks[i][:, 0:width], ALU.mult)\
                .then_inc(s["mul_done"], 1)
        if not known_first(b):
            take_hT(b - 1, 1 - p)
        if not (isinstance(b, int) and b < 2):
            take_output(b - 2)

    for_batches(v, slots)
    take_hT(B - 1, 1)
    take_output(B - 2)
    take_output(B - 1)


def experts1_pool(po, m):
    t, s = r1_tiles(m), m.e1
    po.wait_ge(m.r1["combine_ready"], 1)

    def gate(b, p):
        po.wait_ge(s["mul_done"], 3 * (b + 1))
        h = t.Hn[p][:, 0:E1 * F1].rearrange("p (e f) -> p e f", e=E1)
        w = t.combine[:, bass.ds(b * E1, E1)].unsqueeze(2).to_broadcast([128, E1, F1])
        po.tensor_tensor(h, h, w, ALU.mult).then_inc(s["gated"], 1)

    for_batches(po, gate)


def program(nc, a, out, scratch, layers=6):
    with ExitStack() as ctx:
        place = {}

        def sb(name, shape, dt=F32):
            tile = ctx.enter_context(nc.sbuf_tensor(name, shape, dt))
            place[name] = nc.sbuf_base - shape[1] * mybir.dt.size(dt)
            return tile

        def parts(name, over, column, columns):
            return nc.alloc_sbuf_tensor_at(name, [128, columns], F32R, offset=place[over] + 4 * column)

        def ps(name):
            return ctx.enter_context(nc.psum_tensor(name, [128, 512], F32))

        def sem(name):
            return ctx.enter_context(nc.semaphore(name))

        def sems(prefix, names):
            return {n: sem(f"{prefix}_{n}") for n in names}

        m = Namespace()
        m.w = {name: sb(name, shape) for name, shape in WEIGHTS.items()}
        m.X = sb("X", [128, N])
        m.stats = sb("stats", [128, B * 6])
        m.mean, m.rstd, m.st1, m.st2 = (sb(n, [128, B]) for n in ("mean", "rstd", "st1", "st2"))
        m.xn = sb("xn", [128, 2 * D])
        m.XTs = sb("XTs", [128, 512])
        m.small = sb("small", [128, 96])
        m.arena = sb("arena", [128, 20480])
        m.consts = sb("consts", [128, 3 * 128 + 2 * 16 + 256])
        m.ident, m.same_expert, m.earlier_rows = (m.consts[:, 128 * i:128 * i + 128] for i in range(3))
        m.headmask, m.minus_half = m.consts[:, 384:400], m.consts[:, 400:416]
        m.earlier_group = m.consts[:, 416:672]
        m.identb = sb("identb", [128, 128], BF16)
        m.ones = sb("ones", [1, 128])
        m.w2T = m.w["W1"][:, 2 * FC * 128:3 * FC * 128]
        m.XThi, m.XTlo = (parts(n, "arena", i, N) for n, i in (("XThi", 11264), ("XTlo", 13312)))
        m.wv = m.w["wqkv"][:, 2 * H * HD:]
        m.wv_hi, m.wv_lo = sb("wv_hi", [128, H * HD], F32R), parts("wv_lo", "wqkv", 2 * H * HD, H * HD)
        m.XTv = sb("XTv", [128, 512], F32R)
        m.XTparts = parts("XTparts", "XTs", 0, 512)
        m.W1hi, m.W1lo = parts("W1hi", "arena", 16384, E0 * F0), parts("W1lo", "W1", 0, E0 * F0)
        m.w13hi, m.w13lo = parts("w13hi", "W2", 0, 2 * FC * 128), m.W1lo[:, 0:2 * FC * 128]
        m.mask8 = sb("mask8", [128, B * KL], U8)
        m.maskb = sb("maskb", [128, B * KL], BF16)
        m.KT0hi, m.KT0lo = (sb(n, [128, B * KL], F32R) for n in ("KT0hi", "KT0lo"))
        m.Kblk_parts, m.q_parts = parts("Kblk_parts", "arena", 0, 4 * H * KL), parts("q_parts", "arena", 10752, 4 * T)
        m.KT1 = sb("KT1", [128, B * KL])
        m.V01 = sb("V01", [KL, B * 2 * D])

        m.S, m.TP, m.PJ = ([ps(f"{n}{i}") for i in range(2)] for n in ("S", "TP", "PJ"))
        m.OV, m.MX = ps("OV"), ps("MX")

        m.ld = {n: sem(f"ld_{n}") for n in LOADED}
        m.const_ready, m.stream_ready, m.var_ready, m.rstd_ready = (
            sem(n) for n in ("const_ready", "stream_ready", "var_ready", "rstd_ready"))
        m.moment_chain = sem("moment_chain")
        m.split_hi, m.split_lo = sem("split_hi"), sem("split_lo")
        m.att = [sems(f"att{i}", ATT_SEMS) for i in range(2)]
        m.att_w = [m.w["wqkv"][:, H * HD * i:H * HD * (i + 1)] for i in range(2)]
        m.att_k = [0, 3]
        m.v_save, m.v_load = ([sem(f"v_{n}{p}") for p in range(2)] for n in ("save", "load"))
        m.k0_high, m.bias_scaled = sem("k0_high"), sem("bias_scaled")
        m.k0_made, m.k0_taken, m.k1_made, m.k1_taken, m.v01_made, m.v01_taken, m.mask_ready, m.zeroed = (
            sem(n) for n in ("k0_made", "k0_taken", "k1_made", "k1_taken", "v01_made", "v01_taken", "mask_ready",
                             "zeroed"))
        m.cr = sems("cr", CR_SEMS)
        m.x1 = sems("x1", X1_SEMS)
        m.rt = sems("rt", RT_SEMS)
        m.r0 = sems("r0", ["chain", "bits", "shifted", "exp_done", "score_ready", "scoreT_in_psum", "counted", "summed",
                           "ties_counted", "ties_summed", "gateT_ready", "gate_in_psum", "gate_ready", "b2_ready"])
        m.e0 = sems("e0", ["up_done", "gelu_done", "down_done", "add_done", "bias_done", "y_saved"])
        m.r1 = sems("r1", ["chain", "score_ready", "combine_ready"])
        m.e1 = sems("e1", ["xT_ready", "gate_done", "up_done", "silu_done", "mul_done", "gated", "hT_in_psum",
                           "hT_act", "hT_dve", "down_done", "res_done"])
        m.b2sel_of = lambda t, b: t.b2sel[:, bass.ds(b * D, D)]
        out_saved = sem("out_saved")

        block = ctx.enter_context(nc.Block())

        @block.sync
        def _(sp):
            loads_sync(sp, m, a)
            early_loads_sync(sp, m, a)
            att_sync(sp, m, scratch)
            late_loads_sync(sp, m, a)
            if layers < 6:
                sp.wait_ge(m.stream_ready, layers + 1)
            for g in range(NG):
                if layers == 6:
                    sp.wait_ge(m.e1["res_done"], GRP * (g + 1))
                sp.dma_start(out[:, g * GT:(g + 1) * GT], m.X[:, g * GT:(g + 1) * GT]).then_inc(out_saved, 16)
            sp.wait_ge(out_saved, 16 * NG)

        @block.gpsimd
        def _(po):
            moments_pool(po, m, 0, 0)
            moments_pool(po, m, 0, 1)
            att_pool(po, m, 0)
            if layers >= 2:
                cross0_pool(po, m, a)
            if layers >= 3:
                moments_pool(po, m, 2, 1)
                route0_pool(po, m)
                split_attention1_pool(po, m)
            if layers >= 4:
                moments_pool(po, m, 3, 0)
                clear_keys_pool(po, m, 0)
                moments_pool(po, m, 3, 1)
                clear_keys_pool(po, m, 1)
                att_pool(po, m, 1)
            if layers >= 5:
                moments_pool(po, m, 4, 0)
                experts1_loads_pool(po, m, a)
                moments_pool(po, m, 4, 1)
                split_experts1_pool(po, m)
            if layers >= 6:
                moments_pool(po, m, 5, 0)
                moments_pool(po, m, 5, 1)
                experts1_pool(po, m)

        @block.scalar
        def _(act):
            att_scalar(act, m, 0)
            if layers >= 2:
                cross0_scalar(act, m)
            if layers >= 3:
                router_scalar(act, m, 0)
                route0_scalar(act, m)
                experts0_scalar(act, m)
            if layers >= 4:
                att_scalar(act, m, 1)
            if layers >= 5:
                cross1_scalar(act, m)
            if layers >= 6:
                router_scalar(act, m, 1)
                route1_scalar(act, m)
                experts1_scalar(act, m)

        @block.vector
        def _(v):
            setup_vector(v, m)
            att_vector(v, m, 0)
            if layers >= 2:
                cross0_vector(v, m)
            if layers >= 3:
                router_vector(v, m, 0)
                route0_vector(v, m)
                experts0_vector(v, m)
            if layers >= 4:
                att_vector(v, m, 1)
            if layers >= 5:
                cross1_vector(v, m)
            if layers >= 6:
                router_vector(v, m, 1)
                route1_vector(v, m)
                experts1_vector(v, m)

        @block.tensor
        def _(pe):
            att_tensor(pe, m, 0)
            if layers >= 2:
                cross0_tensor(pe, m)
            if layers >= 3:
                router_tensor(pe, m, 0)
                experts0_tensor(pe, m)
            if layers >= 4:
                att_tensor(pe, m, 1)
            if layers >= 5:
                cross1_tensor(pe, m)
            if layers >= 6:
                router_tensor(pe, m, 1)
                experts1_tensor(pe, m)


WEIGHTS = {
    "wqkv": [128, 3 * H * HD], "w_o": [128, H * HD],
    "ctxT": [128, B * KL], "x0Wk": [128, D], "x1WkT": [128, D], "WvBoth": [128, 2 * D], "x0bk": [128, 1],
    "bvBoth": [128, 2 * D], "x0Wq": [128, D], "x0Wo": [128, D], "x0bq": [128, 1], "x0bo": [1, D],
    "Wr": [128, E0], "W1": [128, E0 * F0], "W2": [128, E0 * F0], "b1T": [128, E0 * C0], "b2rep": [128, D],
    "x1WqT": [128, D], "x1WoT": [128, D], "x1bq": [128, 1], "x1bo": [1, D],
    "gateT": [128, E1],
}


def kernel(**inputs):
    import numpy as np
    import concourse.bacc as bacc
    from concourse.bass_utils import run_bass_kernel_spmd

    i = {k: np.asarray(x) for k, x in inputs.items()}

    def tall(w):
        return w.reshape(-1, 128, w.shape[-1]).transpose(1, 0, 2).reshape(128, -1)

    w13 = np.concatenate([i["L1_ffn_w1_e"].reshape(E1 * F1, D), i["L1_ffn_w3_e"].reshape(E1 * F1, D),
                          i["L1_ffn_w1_s"], i["L1_ffn_w3_s"]])
    w2 = np.concatenate([i["L1_ffn_w2_e"].transpose(0, 2, 1).reshape(E1 * F1, D), i["L1_ffn_w2_s"].T])
    r, c = np.arange(128)[:, None], np.arange(128)[None, :]
    same = (r % E0 == c % E0).astype(np.float32)
    earlier = ((r % E0 == c % E0) & (r // E0 < c // E0)).astype(np.float32)
    heads = (r // XHD == np.arange(H)[None, :]).astype(np.float32)
    groups = np.tile((np.arange(G1)[:, None] > np.arange(G1)[None, :]).astype(np.float32).reshape(1, -1), (128, B))
    consts = np.concatenate([np.eye(128, dtype=np.float32), same, earlier, heads,
                             np.full((128, 16), -0.5, np.float32), groups], axis=1)
    a = {
        "x": i["x"].transpose(1, 0, 2).reshape(T, N), "consts": consts,
        "wqT": i["L0_attn_wq"].T, "wkT": i["L0_attn_wk"].T, "wvT": i["L0_attn_wv"].T, "woT": tall(i["L0_attn_wo"].T),
        "ctxT": i["ctx_1024"].transpose(2, 0, 1).reshape(D, B * KL),
        "mask": i["mask_Bx1xSxS2_bk1"][:, 0].transpose(1, 0, 2).reshape(T, B * KL),
        "x0Wk": i["L0_xattn_Wk"], "x1WkT": i["L1_xattn_Wk"].T,
        "WvBoth": np.concatenate([i["L0_xattn_Wv"], i["L1_xattn_Wv"].T], axis=1),
        "x0bk": i["L0_xattn_bk"][:, None],
        "bvBoth": np.tile(np.concatenate([i["L0_xattn_bv"], i["L1_xattn_bv"]])[None, :], (128, 1)),
        "x0Wq": i["L0_xattn_Wq"], "x0Wo": i["L0_xattn_Wo"], "x0bq": i["L0_xattn_bq"][:, None],
        "x0bo": i["L0_xattn_bo"][None, :],
        "Wr": i["L0_ffn_Wr"], "W1": i["L0_ffn_W1"].transpose(1, 0, 2).reshape(D, E0 * F0),
        "W2": tall(i["L0_ffn_W2"].reshape(E0 * F0, D)), "b1T": i["L0_ffn_b1"].reshape(E0 * C0, 128).T,
        "b2rep": np.tile(i["L0_ffn_b2"], (B, 1)),
        "wqkv": i["L1_attn_w_qkv"].transpose(2, 1, 0, 3).reshape(D, 3 * H * HD), "w_o": tall(i["L1_attn_w_o"]),
        "x1WqT": i["L1_xattn_Wq"].T, "x1WoT": i["L1_xattn_Wo"].T, "x1bq": i["L1_xattn_bq"][:, None],
        "x1bo": i["L1_xattn_bo"][None, :],
        "gateT": i["L1_ffn_w_gate"].T, "w13T": w13.T, "w2T": tall(w2),
    }
    nc = bacc.Bacc("TRN2", target_bir_lowering=False, num_devices=1)
    arrays, aps = {}, {}
    for name, x in a.items():
        x = np.ascontiguousarray(x)
        arrays[f"in_{name}"] = x
        aps[name] = nc.dram_tensor(f"in_{name}", x.shape, mybir.dt.from_np(x.dtype), kind="ExternalInput").ap()
    out = nc.dram_tensor("out", (T, N), F32, kind="ExternalOutput").ap()
    scratch = [nc.dram_tensor(f"v_scratch{p}", (T, H * HD), F32, kind="Internal").ap() for p in range(2)]
    program(nc, aps, out, scratch)
    result = run_bass_kernel_spmd(nc, [arrays], core_ids=[0]).results[0]["out"]
    return np.ascontiguousarray(result.reshape(T, B, D).transpose(1, 0, 2))
```
